# Optimizing a Trainium2 kernel written in Bass

```python
import numpy as np
import jax
import jax.numpy as jnp

def _softmax(x, axis=-1):
    return jax.nn.softmax(x, axis=axis)

def _gelu(x):
    return jax.nn.gelu(x, approximate=True)

def _silu(x):
    return jax.nn.silu(x)

def _sigmoid(x):
    return jax.nn.sigmoid(x)

def _layernorm(x, axis=-1, eps=1e-05):
    m = jnp.mean(x, axis=axis, keepdims=True)
    v = jnp.var(x, axis=axis, keepdims=True)
    return (x - m) / jnp.sqrt(v + eps)

def _scatter_add(tgt, idx, src, axis=0):
    return tgt.at[idx].add(src)

def _segment_sum(src, seg, n):
    return jax.ops.segment_sum(src, seg, n)
kernel_name = 'mk_decoder_preln_d2_seqx_r8_e67655'

def setup_inputs(seed: int=0):
    np.random.seed(seed)
    _w = jnp.asarray

    def _rec_inputs():
        import jax
        import jax.numpy as jnp
        _rk = jax.random.key(seed)
        x = 7.22e-05 + 1 * jax.random.normal(jax.random.fold_in(_rk, 1), (4, 512, 128), jnp.float32)
        _lenS = 512 - jax.random.randint(jax.random.fold_in(_rk, 7), (4,), 0, max(1, 512 // 4) + 1, jnp.int32)
        _lenS2 = 77 - jax.random.randint(jax.random.fold_in(_rk, 8), (4,), 0, max(1, 77 // 4) + 1, jnp.int32)
        _ctx_1024P = jax.random.normal(jax.random.fold_in(_rk, 11), (4, 16, 128), jnp.float32)
        _ctx_1024c = jax.random.dirichlet(jax.random.fold_in(_rk, 511), 0.3 * jnp.ones((16,), jnp.float32), (4, 77))
        _ctx_1024t = jnp.einsum('bsk,bkd->bsd', _ctx_1024c, _ctx_1024P)
        _ctx_1024t = _ctx_1024t * jax.lax.rsqrt(jnp.mean(jnp.square(_ctx_1024t)) + 1e-12) * 0.953939
        ctx_1024 = 4.13588e-05 + 0.999923 * (_ctx_1024t + 0.3 * jax.random.normal(jax.random.fold_in(_rk, 611), (4, 77, 128), jnp.float32))
        _validS = jnp.arange(512)[None, :] < _lenS[:, None]
        _validS2 = jnp.arange(77)[None, :] < _lenS2[:, None]
        _causal = jnp.tril(jnp.ones((512, 512), dtype=bool))
        mask_1xSxS2_ff0 = jnp.where(jnp.ones((1, 512, 77), dtype=bool), 0.0, -1000000000.0).astype(jnp.float32)
        return (x, ctx_1024, mask_1xSxS2_ff0)
    x, ctx_1024, mask_1xSxS2_ff0 = _rec_inputs()

    def _L0_attn_setup():
        import jax, jax.numpy as jnp
        import numpy as np
        import math
        DIM = 128
        N_HEADS = 16
        HEAD_DIM = DIM // N_HEADS

        def rope(x):
            S = x.shape[-2]
            D = x.shape[-1]
            pos = jnp.arange(S, dtype=x.dtype)[:, None]
            dim = jnp.arange(D // 2, dtype=x.dtype)[None, :]
            theta = pos / jnp.exp(2.0 * dim / D * math.log(10000.0))
            sin = jnp.sin(theta)[None, None]
            cos = jnp.cos(theta)[None, None]
            x1 = x[..., ::2]
            x2 = x[..., 1::2]
            out1 = x1 * cos - x2 * sin
            out2 = x1 * sin + x2 * cos
            return jnp.stack([out1, out2], axis=-1).reshape(x.shape)
        key = jax.random.key(seed)
        ks = jax.random.split(key, 9)
        B, S = (2, 256)
        s = 1.0 / math.sqrt(DIM)
        inp = {'x': jax.random.normal(ks[0], (B, S, DIM), dtype=jnp.float32), 'wq': jax.random.normal(ks[1], (DIM, DIM), dtype=jnp.float32) * s, 'bq': jnp.zeros((DIM,), dtype=jnp.float32), 'wk': jax.random.normal(ks[2], (DIM, DIM), dtype=jnp.float32) * s, 'bk': jnp.zeros((DIM,), dtype=jnp.float32), 'wv': jax.random.normal(ks[3], (DIM, DIM), dtype=jnp.float32) * s, 'bv': jnp.zeros((DIM,), dtype=jnp.float32), 'wo': jax.random.normal(ks[4], (DIM, DIM), dtype=jnp.float32) * s, 'bo': jnp.zeros((DIM,), dtype=jnp.float32)}
        return inp
    _L0_attn_all = _L0_attn_setup()
    _L0_attn_in = {k: v for k, v in _L0_attn_all.items() if k in ('wq', 'bq', 'wk', 'bk', 'wv', 'bv', 'wo', 'bo')}
    del _L0_attn_all

    def _L0_xattn_setup():
        import jax, jax.numpy as jnp
        import numpy as np
        B, S, D, H = (4, 256, 128, 16)
        HD = D // H

        def _split_heads(x):
            b, s, _ = x.shape
            return x.reshape(b, s, H, HD).transpose(0, 2, 1, 3)
        key = jax.random.key(seed)
        ks = jax.random.split(key, 11)
        s = 1.0 / np.sqrt(D)
        return {'Q': jax.random.normal(ks[0], (B, S, D), dtype=jnp.float32), 'K': jax.random.normal(ks[1], (B, S, D), dtype=jnp.float32), 'V': jax.random.normal(ks[2], (B, S, D), dtype=jnp.float32), 'Wq': jax.random.normal(ks[3], (D, D), dtype=jnp.float32) * s, 'bq': jnp.zeros((D,), dtype=jnp.float32), 'Wk': jax.random.normal(ks[4], (D, D), dtype=jnp.float32) * s, 'bk': jnp.zeros((D,), dtype=jnp.float32), 'Wv': jax.random.normal(ks[5], (D, D), dtype=jnp.float32) * s, 'bv': jnp.zeros((D,), dtype=jnp.float32), 'Wo': jax.random.normal(ks[6], (D, D), dtype=jnp.float32) * s, 'bo': jnp.zeros((D,), dtype=jnp.float32)}
    _L0_xattn_all = _L0_xattn_setup()
    _L0_xattn_in = {k: v for k, v in _L0_xattn_all.items() if k in ('Wq', 'bq', 'Wk', 'bk', 'Wv', 'bv', 'Wo', 'bo')}
    del _L0_xattn_all

    def _L0_ffn_setup():
        import jax, jax.numpy as jnp
        import numpy as np
        D_MODEL = 128
        NUM_EXPERTS = 8
        TOP_K = 2
        B, S = (1, 256)
        key = jax.random.key(seed)
        ks = jax.random.split(key, 8)
        sd = 1.0 / np.sqrt(D_MODEL)
        x = jax.random.normal(ks[0], (B, S, D_MODEL), dtype=jnp.float32)
        gate_w = jax.random.normal(ks[1], (D_MODEL, NUM_EXPERTS), dtype=jnp.float32) * sd
        gate_b = jnp.zeros((NUM_EXPERTS,), dtype=jnp.float32)
        w1 = jax.random.normal(ks[2], (NUM_EXPERTS, D_MODEL, 8 * D_MODEL), dtype=jnp.float32) * sd
        b1 = jnp.zeros((NUM_EXPERTS, 8 * D_MODEL), dtype=jnp.float32)
        w2 = jax.random.normal(ks[3], (NUM_EXPERTS, 4 * D_MODEL, D_MODEL), dtype=jnp.float32) * (1.0 / np.sqrt(4 * D_MODEL))
        b2 = jnp.zeros((NUM_EXPERTS, D_MODEL), dtype=jnp.float32)
        return {'x': x, 'gate_w': gate_w, 'gate_b': gate_b, 'w1': w1, 'b1': b1, 'w2': w2, 'b2': b2}
    _L0_ffn_all = _L0_ffn_setup()
    _L0_ffn_in = {k: v for k, v in _L0_ffn_all.items() if k in ('gate_w', 'gate_b', 'w1', 'b1', 'w2', 'b2')}
    del _L0_ffn_all

    def _L1_attn_setup():
        import jax, jax.numpy as jnp
        import numpy as np
        import math
        D_MODEL = 128
        NUM_HEADS = 16
        HEAD_DIM = D_MODEL // NUM_HEADS
        key = jax.random.key(seed)
        ks = jax.random.split(key, 9)
        B, S = (2, 256)
        scale = 1.0 / math.sqrt(D_MODEL)
        inp = {'hidden_states': jax.random.normal(ks[0], (B, S, D_MODEL), dtype=jnp.float32), 'wq': jax.random.normal(ks[1], (D_MODEL, D_MODEL), dtype=jnp.float32) * scale, 'bq': jnp.zeros((D_MODEL,), dtype=jnp.float32), 'wk': jax.random.normal(ks[2], (D_MODEL, D_MODEL), dtype=jnp.float32) * scale, 'bk': jnp.zeros((D_MODEL,), dtype=jnp.float32), 'wv': jax.random.normal(ks[3], (D_MODEL, D_MODEL), dtype=jnp.float32) * scale, 'bv': jnp.zeros((D_MODEL,), dtype=jnp.float32), 'wo': jax.random.normal(ks[4], (D_MODEL, D_MODEL), dtype=jnp.float32) * scale, 'bo': jnp.zeros((D_MODEL,), dtype=jnp.float32)}
        return inp
    _L1_attn_all = _L1_attn_setup()
    _L1_attn_in = {k: v for k, v in _L1_attn_all.items() if k in ('wq', 'bq', 'wk', 'bk', 'wv', 'bv', 'wo', 'bo')}
    del _L1_attn_all

    def _L1_xattn_setup():
        import jax, jax.numpy as jnp
        import numpy as np
        INP_SIZE = 128
        D_MODEL = 128
        B, S = (4, 256)
        key = jax.random.key(seed)
        ks = jax.random.split(key, 9)
        q = jax.random.normal(ks[0], (B, S, INP_SIZE), dtype=jnp.float32)
        k = jax.random.normal(ks[1], (B, S, INP_SIZE), dtype=jnp.float32)
        v = jax.random.normal(ks[2], (B, S, INP_SIZE), dtype=jnp.float32)
        mask = jnp.zeros((1, S, S), dtype=jnp.float32)
        kernel_q = jax.random.normal(ks[3], (INP_SIZE, D_MODEL), dtype=jnp.float32) * 0.05
        kernel_k = jax.random.normal(ks[4], (INP_SIZE, D_MODEL), dtype=jnp.float32) * 0.05
        kernel_v = jax.random.normal(ks[5], (INP_SIZE, D_MODEL), dtype=jnp.float32) * 0.05
        bias_q = jax.random.normal(ks[6], (D_MODEL,), dtype=jnp.float32) * 0.05
        bias_k = jax.random.normal(ks[7], (D_MODEL,), dtype=jnp.float32) * 0.05
        bias_v = jax.random.normal(ks[8], (D_MODEL,), dtype=jnp.float32) * 0.05
        return {'q': q, 'k': k, 'v': v, 'mask': mask, 'kernel_q': kernel_q, 'bias_q': bias_q, 'kernel_k': kernel_k, 'bias_k': bias_k, 'kernel_v': kernel_v, 'bias_v': bias_v}
    _L1_xattn_all = _L1_xattn_setup()
    _L1_xattn_in = {k: v for k, v in _L1_xattn_all.items() if k in ('kernel_q', 'bias_q', 'kernel_k', 'bias_k', 'kernel_v', 'bias_v')}
    del _L1_xattn_all

    def _L1_ffn_setup():
        import jax, jax.numpy as jnp
        import numpy as np
        B, S, D_MODEL, D_HIDDEN = (4, 256, 128, 512)

        def act_quant(x):
            scale = 127.0 / jnp.clip(jnp.max(jnp.abs(x), axis=-1, keepdims=True), 1e-05)
            return jnp.clip(jnp.round(x * scale), -128, 127) / scale

        def weight_quant(w):
            scale = 1.0 / jnp.clip(jnp.mean(jnp.abs(w)), 1e-05)
            return jnp.clip(jnp.round(w * scale), -1, 1) / scale

        def bit_linear(x, w):
            xq = x + jax.lax.stop_gradient(act_quant(x) - x)
            wq = w + jax.lax.stop_gradient(weight_quant(w) - w)
            return jnp.einsum('bsd,hd->bsh', xq, wq)

        def depthwise_conv1d(x_bcl, w, b):
            y = jax.lax.conv_general_dilated(x_bcl, w, window_strides=(1,), padding=[(1, 1)], dimension_numbers=('NCH', 'OIH', 'NCH'), feature_group_count=x_bcl.shape[1])
            return y + b[None, :, None]
        key = jax.random.key(seed)
        ks = jax.random.split(key, 5)
        lim1 = 1.0 / np.sqrt(D_MODEL)
        lim2 = 1.0 / np.sqrt(D_HIDDEN)
        limc = 1.0 / np.sqrt(3.0)
        return {'x': jax.random.normal(ks[0], (B, S, D_MODEL), dtype=jnp.float32), 'w1': jax.random.uniform(ks[1], (D_HIDDEN, D_MODEL), jnp.float32, -lim1, lim1), 'conv_w': jax.random.uniform(ks[2], (D_HIDDEN, 1, 3), jnp.float32, -limc, limc), 'conv_b': jax.random.uniform(ks[3], (D_HIDDEN,), jnp.float32, -limc, limc), 'w2': jax.random.uniform(ks[4], (D_MODEL, D_HIDDEN), jnp.float32, -lim2, lim2)}
    _L1_ffn_all = _L1_ffn_setup()
    _L1_ffn_in = {k: v for k, v in _L1_ffn_all.items() if k in ('w1', 'conv_w', 'conv_b', 'w2')}
    del _L1_ffn_all
    return {'x': x, 'ctx_1024': ctx_1024, 'mask_1xSxS2_ff0': mask_1xSxS2_ff0, 'L0_attn_wq': _L0_attn_in['wq'], 'L0_attn_bq': _L0_attn_in['bq'], 'L0_attn_wk': _L0_attn_in['wk'], 'L0_attn_bk': _L0_attn_in['bk'], 'L0_attn_wv': _L0_attn_in['wv'], 'L0_attn_bv': _L0_attn_in['bv'], 'L0_attn_wo': _L0_attn_in['wo'], 'L0_attn_bo': _L0_attn_in['bo'], 'L0_xattn_Wq': _L0_xattn_in['Wq'], 'L0_xattn_bq': _L0_xattn_in['bq'], 'L0_xattn_Wk': _L0_xattn_in['Wk'], 'L0_xattn_bk': _L0_xattn_in['bk'], 'L0_xattn_Wv': _L0_xattn_in['Wv'], 'L0_xattn_bv': _L0_xattn_in['bv'], 'L0_xattn_Wo': _L0_xattn_in['Wo'], 'L0_xattn_bo': _L0_xattn_in['bo'], 'L0_ffn_gate_w': _L0_ffn_in['gate_w'], 'L0_ffn_gate_b': _L0_ffn_in['gate_b'], 'L0_ffn_w1': _L0_ffn_in['w1'], 'L0_ffn_b1': _L0_ffn_in['b1'], 'L0_ffn_w2': _L0_ffn_in['w2'], 'L0_ffn_b2': _L0_ffn_in['b2'], 'L1_attn_wq': _L1_attn_in['wq'], 'L1_attn_bq': _L1_attn_in['bq'], 'L1_attn_wk': _L1_attn_in['wk'], 'L1_attn_bk': _L1_attn_in['bk'], 'L1_attn_wv': _L1_attn_in['wv'], 'L1_attn_bv': _L1_attn_in['bv'], 'L1_attn_wo': _L1_attn_in['wo'], 'L1_attn_bo': _L1_attn_in['bo'], 'L1_xattn_kernel_q': _L1_xattn_in['kernel_q'], 'L1_xattn_bias_q': _L1_xattn_in['bias_q'], 'L1_xattn_kernel_k': _L1_xattn_in['kernel_k'], 'L1_xattn_bias_k': _L1_xattn_in['bias_k'], 'L1_xattn_kernel_v': _L1_xattn_in['kernel_v'], 'L1_xattn_bias_v': _L1_xattn_in['bias_v'], 'L1_ffn_w1': _L1_ffn_in['w1'], 'L1_ffn_conv_w': _L1_ffn_in['conv_w'], 'L1_ffn_conv_b': _L1_ffn_in['conv_b'], 'L1_ffn_w2': _L1_ffn_in['w2']}

def reference(x, ctx_1024, mask_1xSxS2_ff0, L0_attn_wq, L0_attn_bq, L0_attn_wk, L0_attn_bk, L0_attn_wv, L0_attn_bv, L0_attn_wo, L0_attn_bo, L0_xattn_Wq, L0_xattn_bq, L0_xattn_Wk, L0_xattn_bk, L0_xattn_Wv, L0_xattn_bv, L0_xattn_Wo, L0_xattn_bo, L0_ffn_gate_w, L0_ffn_gate_b, L0_ffn_w1, L0_ffn_b1, L0_ffn_w2, L0_ffn_b2, L1_attn_wq, L1_attn_bq, L1_attn_wk, L1_attn_bk, L1_attn_wv, L1_attn_bv, L1_attn_wo, L1_attn_bo, L1_xattn_kernel_q, L1_xattn_bias_q, L1_xattn_kernel_k, L1_xattn_bias_k, L1_xattn_kernel_v, L1_xattn_bias_v, L1_ffn_w1, L1_ffn_conv_w, L1_ffn_conv_b, L1_ffn_w2):
    import jax
    import jax.numpy as jnp

    def _L0_attn_ref(x, wq, bq, wk, bk, wv, bv, wo, bo):
        import jax, jax.numpy as jnp
        import numpy as np
        import math
        DIM = 128
        N_HEADS = 16
        HEAD_DIM = DIM // N_HEADS

        def rope(x):
            S = x.shape[-2]
            D = x.shape[-1]
            pos = jnp.arange(S, dtype=x.dtype)[:, None]
            dim = jnp.arange(D // 2, dtype=x.dtype)[None, :]
            theta = pos / jnp.exp(2.0 * dim / D * math.log(10000.0))
            sin = jnp.sin(theta)[None, None]
            cos = jnp.cos(theta)[None, None]
            x1 = x[..., ::2]
            x2 = x[..., 1::2]
            out1 = x1 * cos - x2 * sin
            out2 = x1 * sin + x2 * cos
            return jnp.stack([out1, out2], axis=-1).reshape(x.shape)
        B, S, _ = x.shape

        def proj(w, b):
            y = jnp.einsum('bsd,ed->bse', x, w) + b
            return y.reshape(B, S, N_HEADS, HEAD_DIM).transpose(0, 2, 1, 3)
        q = rope(proj(wq, bq))
        k = rope(proj(wk, bk))
        v = proj(wv, bv)
        score = jnp.einsum('bhqd,bhkd->bhqk', q, k) / math.sqrt(HEAD_DIM)
        causal = jnp.tril(jnp.ones((S, S), dtype=bool))
        score = jnp.where(causal[None, None], score, -jnp.inf)
        attn = jax.nn.softmax(score, axis=-1)
        out = jnp.einsum('bhqk,bhkd->bhqd', attn, v)
        out = out.transpose(0, 2, 1, 3).reshape(B, S, DIM)
        return jnp.einsum('bsd,ed->bse', out, wo) + bo

    def _L0_xattn_ref(Q, K, V, Wq, bq, Wk, bk, Wv, bv, Wo, bo):
        import jax, jax.numpy as jnp
        import numpy as np
        B, S, D, H = (4, 256, 128, 16)
        HD = D // H

        def _split_heads(x):
            b, s, _ = x.shape
            return x.reshape(b, s, H, HD).transpose(0, 2, 1, 3)
        q = _split_heads(Q @ Wq + bq)
        k = _split_heads(K @ Wk + bk)
        v = _split_heads(V @ Wv + bv)
        scale = 1.0 / jnp.sqrt(jnp.float32(HD))
        scores = jnp.einsum('bhqd,bhkd->bhqk', q, k) * scale
        attn = jax.nn.softmax(scores, axis=-1)
        out = jnp.einsum('bhqk,bhkd->bhqd', attn, v)
        out = out.transpose(0, 2, 1, 3).reshape(Q.shape[0], -1, D)
        return out @ Wo + bo

    def _L0_ffn_ref(x, gate_w, gate_b, w1, b1, w2, b2):
        import jax, jax.numpy as jnp
        import numpy as np
        D_MODEL = 128
        NUM_EXPERTS = 8
        TOP_K = 2
        B, S = (1, 256)
        gate_logits = jnp.einsum('bsd,de->bse', x, gate_w) + gate_b
        weights, indices = jax.lax.top_k(gate_logits, TOP_K)
        weights = jax.nn.softmax(weights, axis=-1)
        h = jnp.einsum('bsd,edh->ebsh', x, w1) + b1[:, None, None, :]
        xh, gh = jnp.split(h, 2, axis=-1)
        act = jax.nn.silu(gh) * xh
        out_e = jnp.einsum('ebsf,efd->ebsd', act, w2) + b2[:, None, None, :]
        out_e = jnp.transpose(out_e, (1, 2, 0, 3))
        sel = jnp.take_along_axis(out_e, indices[..., None], axis=2)
        return jnp.sum(sel * weights[..., None], axis=2)

    def _L1_attn_ref(hidden_states, wq, bq, wk, bk, wv, bv, wo, bo):
        import jax, jax.numpy as jnp
        import numpy as np
        import math
        D_MODEL = 128
        NUM_HEADS = 16
        HEAD_DIM = D_MODEL // NUM_HEADS
        B, S, D = hidden_states.shape
        H, Hd = (NUM_HEADS, HEAD_DIM)

        def proj(w, b):
            y = jnp.einsum('bsd,ed->bse', hidden_states, w) + b
            return y.reshape(B, S, H, Hd).transpose(0, 2, 1, 3)
        q = proj(wq, bq)
        k = proj(wk, bk)
        v = proj(wv, bv)
        scores = jnp.einsum('bhqd,bhkd->bhqk', q, k) / math.sqrt(Hd)
        attn = jax.nn.softmax(scores, axis=-1)
        ctx = jnp.einsum('bhqk,bhkd->bhqd', attn, v)
        ctx = ctx.transpose(0, 2, 1, 3).reshape(B, S, D)
        out = jnp.einsum('bsd,ed->bse', ctx, wo) + bo
        return out

    def _L1_xattn_ref(q, k, v, mask, kernel_q, bias_q, kernel_k, bias_k, kernel_v, bias_v):
        import jax, jax.numpy as jnp
        import numpy as np
        INP_SIZE = 128
        D_MODEL = 128
        B, S = (4, 256)
        qp = jnp.einsum('bsi,id->bsd', q, kernel_q) + bias_q
        kp = jnp.einsum('bsi,id->bsd', k, kernel_k) + bias_k
        vp = jnp.einsum('bsi,id->bsd', v, kernel_v) + bias_v
        dk = jnp.asarray(kp.shape[-1], dtype=jnp.float32)
        logits = jnp.einsum('bqd,bkd->bqk', qp, kp) / jnp.sqrt(dk)
        logits = logits + mask
        attn = jax.nn.softmax(logits, axis=-1)
        out = jnp.einsum('bqk,bkd->bqd', attn, vp)
        return out

    def _L1_ffn_ref(x, w1, conv_w, conv_b, w2):
        import jax, jax.numpy as jnp
        import numpy as np
        B, S, D_MODEL, D_HIDDEN = (4, 256, 128, 512)

        def act_quant(x):
            scale = 127.0 / jnp.clip(jnp.max(jnp.abs(x), axis=-1, keepdims=True), 1e-05)
            return jnp.clip(jnp.round(x * scale), -128, 127) / scale

        def weight_quant(w):
            scale = 1.0 / jnp.clip(jnp.mean(jnp.abs(w)), 1e-05)
            return jnp.clip(jnp.round(w * scale), -1, 1) / scale

        def bit_linear(x, w):
            xq = x + jax.lax.stop_gradient(act_quant(x) - x)
            wq = w + jax.lax.stop_gradient(weight_quant(w) - w)
            return jnp.einsum('bsd,hd->bsh', xq, wq)

        def depthwise_conv1d(x_bcl, w, b):
            y = jax.lax.conv_general_dilated(x_bcl, w, window_strides=(1,), padding=[(1, 1)], dimension_numbers=('NCH', 'OIH', 'NCH'), feature_group_count=x_bcl.shape[1])
            return y + b[None, :, None]
        h = bit_linear(x, w1)
        h = depthwise_conv1d(h.transpose(0, 2, 1), conv_w, conv_b)
        h = h.transpose(0, 2, 1)
        h = jax.nn.silu(h)
        return bit_linear(h, w2)
    x = x + _L0_attn_ref(_layernorm(x, axis=-1), L0_attn_wq, L0_attn_bq, L0_attn_wk, L0_attn_bk, L0_attn_wv, L0_attn_bv, L0_attn_wo, L0_attn_bo)
    x = x + _L0_xattn_ref(_layernorm(x, axis=-1), ctx_1024, ctx_1024, L0_xattn_Wq, L0_xattn_bq, L0_xattn_Wk, L0_xattn_bk, L0_xattn_Wv, L0_xattn_bv, L0_xattn_Wo, L0_xattn_bo)
    x = x + _L0_ffn_ref(_layernorm(x, axis=-1), L0_ffn_gate_w, L0_ffn_gate_b, L0_ffn_w1, L0_ffn_b1, L0_ffn_w2, L0_ffn_b2)
    x = x + _L1_attn_ref(_layernorm(x, axis=-1), L1_attn_wq, L1_attn_bq, L1_attn_wk, L1_attn_bk, L1_attn_wv, L1_attn_bv, L1_attn_wo, L1_attn_bo)
    x = x + _L1_xattn_ref(_layernorm(x, axis=-1), ctx_1024, ctx_1024, mask_1xSxS2_ff0, L1_xattn_kernel_q, L1_xattn_bias_q, L1_xattn_kernel_k, L1_xattn_bias_k, L1_xattn_kernel_v, L1_xattn_bias_v)
    x = x + _L1_ffn_ref(_layernorm(x, axis=-1), L1_ffn_w1, L1_ffn_conv_w, L1_ffn_conv_b, L1_ffn_w2)
    return x

_drawn_inputs = setup_inputs


def setup_inputs(seed=0):
    import zlib

    import numpy as np

    out = dict(_drawn_inputs(seed))
    spreads = {'L0_attn_bq': (0.0, 0.288),
     'L0_attn_bk': (0.0, 0.272),
     'L0_attn_bv': (0.0, 0.1),
     'L0_attn_bo': (0.0, 0.1),
     'L0_xattn_bq': (0.0, 0.1),
     'L0_xattn_bk': (0.0, 0.8),
     'L0_xattn_bv': (0.0, 0.1),
     'L0_xattn_bo': (0.0, 0.1),
     'L0_ffn_gate_b': (0.0, 0.1),
     'L0_ffn_b1': (0.0, 0.1),
     'L0_ffn_b2': (0.0, 0.1),
     'L1_attn_bq': (0.0, 0.8),
     'L1_attn_bk': (0.0, 0.8),
     'L1_attn_bv': (0.0, 0.1),
     'L1_attn_bo': (0.0, 0.1)}
    factors = {'L1_xattn_bias_q': 8.0, 'L1_xattn_bias_k': 8.0}
    for name, (base, spread) in spreads.items():
        noise = np.random.default_rng([zlib.crc32(name.encode()), seed]).standard_normal(out[name].shape)
        drawn = base * np.exp(spread * noise) if base else spread * noise
        out[name] = jnp.asarray(drawn.astype(out[name].dtype))
    for name, factor in factors.items():
        out[name] = (out[name] * factor).astype(out[name].dtype)
    return out
```

```python
from contextlib import ExitStack
import math

import numpy as np

import concourse.bass as bass
from concourse import mybir
from concourse.alu_op_type import AluOpType as ALU

ACT = mybir.ActivationFunctionType
AX = mybir.AxisListType
F32 = mybir.dt.float32
BF16 = mybir.dt.bfloat16
I32 = mybir.dt.int32
U32 = mybir.dt.uint32

P = 128
NB, S, D = 4, 512, 128
QT = S // P
NT = NB * QT
NH, HD = 16, 8
SC = 77
HG = 4
UNITS = NH // HG
TERMS = 6
ROWS = TERMS * HD
SHIFT = 2
KR = ROWS + SHIFT
NE, FF = 8, 512
FC = FF // P
MT = 2 * NT + NE
ROUND = 1.5 * 2 ** 23
VW = 32
EPS = 1e-5
MASKED = -1e30
Q_PARTS = (0, 1, 2, 0, 1, 0)
K_PARTS = (0, 0, 0, 1, 1, 2)


def wait(e, sem, value):
    if isinstance(value, int) and value <= 0:
        return
    e.wait_ge(sem, value)


class Attention:

    def __init__(self, name, ln, keys, causal):
        self.name, self.ln, self.keys, self.causal = name, ln, keys, causal
        self.kt = -(-keys // P)
        self.kp = min(keys, P)
        self.items = []
        for qt in range(QT):
            n = (qt + 1) * P if causal else keys
            per = max(1, min(2, S // n))
            self.items += [(qt, h, per, n) for h in range(0, HG, per)]
        self.sem = {}
        self.rope = causal

    def totals(self):
        cross, units = self.name == "X0", UNITS * NB
        both = NB + 1 if cross else 2 * NB
        of = dict.fromkeys(ATT_SEMS, units)
        of |= dict.fromkeys(("part1", "rest", "part2", "part3"), both)
        of |= dict.fromkeys(("k_proj", "v_proj", "v_done"), 1 if cross else NB)
        of |= dict.fromkeys(("cos_sin", "roped"), 2 * NB if self.rope else 0)
        of |= dict.fromkeys(("merged", "merged_out", "proj", "x_new"), NB)
        of |= dict.fromkeys(("max_in", "max_out"), units * len(self.items))
        of |= dict.fromkeys(("scores", "probs"), 2 * self.kt * units)
        of |= {"q_proj": 2 * NB if self.rope else NB, "pv": self.kt * units, "shifted": 64 * NB,
               "slot": 16 * (4 if cross else 2) * NB, "stacked_q": 16 * TERMS * NB,
               "stacked_k": 16 * TERMS * (1 if cross else NB)}
        return of

    def first_query(self, kt):
        return kt * P if self.causal else 0

    def share(self, c):
        n = len(self.items)
        return range(n * c // self.kt, n * (c + 1) // self.kt)


ATT_SEMS = """q_proj k_proj v_proj part1 rest part2 part3 v_done stacked_q stacked_k values cos_sin roped
max_in max_out neg_hi neg_lo turned rows scores probs pv unit_scores pv_out out_turned
reciprocal normed merged merged_out proj x_new""".split()


def build(nc, d, out, layers=("A0", "X0", "M0", "A1", "X1", "F1")):
    ln_of = {n: i for i, n in enumerate(layers)}
    es = ExitStack()
    with es:
        def sb(name, shape, dt=F32):
            return es.enter_context(nc.sbuf_tensor(name, shape, dt))

        def ps(name, shape, dt=F32):
            return es.enter_context(nc.psum_tensor(name, shape, dt))

        def sem(name):
            return es.enter_context(nc.semaphore(name))

        a_self0 = Attention("A0", ln_of.get("A0"), S, True)
        a_cross = Attention("X0", ln_of.get("X0"), SC, False)
        a_self1 = Attention("A1", ln_of.get("A1"), S, False)
        atts = [a for a in (a_self0, a_cross, a_self1) if a.name in layers]
        att_sem = {n: sem(f"att_{n}") for n in ATT_SEMS}
        att_sem |= {n: [sem(f"att_{n}{i}") for i in range(UNITS)] for n in ("slot", "shifted")}
        since = dict.fromkeys(att_sem, 0)
        for a in atts:
            a.sem, a.since = att_sem, dict(since)
            since = {n: v + a.totals()[n] for n, v in since.items()}
        of_att = {a.name: (att_sem["x_new"], a.since["x_new"]) for a in atts}
        x_new = [of_att.get(n) or (sem(f"{n}_x"), 0) for n in layers]

        xs = sb("x_sb", [P, NT, D])
        stats = sb("stats", [P, QT, 6])
        mv = sb("mv", [P, QT, 2])
        var = sb("var", [P, QT])
        rstd = sb("rstd", [P, QT])
        mhalf = sb("mhalf", [P, QT])
        xn = sb("xn", [P, QT, D])
        xnT = sb("xnT", [P, S])
        ident = sb("ident", [P, P])
        identb = sb("identb", [P, P], BF16)
        ones_row = sb("ones_row", [1, P])
        mask_qk = sb("mask_qk", [P, P], BF16)
        mask_kq = sb("mask_kq", [P, P], BF16)
        parts = sb("parts", [P, 2, 3, S], BF16)
        rest = sb("rest", [P, 2, S])
        v9 = sb("v9", [P, NT, NH, HD + 1])
        stk = sb("stk", [P, UNITS, 2, 2, S], BF16)
        vsl = sb("vsl", [P, UNITS, QT, HG, VW])
        mx = sb("mx", [P, 2, QT, HG])
        neg = sb("neg", [P, 2, 2, 2, 2, QT], BF16)
        negT = sb("negT", [8 * QT, 2, P], BF16)
        probs = sb("probs", [P, 2, HG, S])
        oT = sb("oT", [P, S])
        rec = sb("rec", [P, QT, HG])
        otok = sb("otok", [P, QT, D])
        okT = sb("okT", [P, S])
        wts = {}
        for a in atts:
            wts[a.name] = {k: sb(f"{a.name}_{k}", [P, D]) for k in ("wq", "wk", "wv", "wo")}
            wts[a.name] |= {k: sb(f"{a.name}_{k}", [P, 1]) for k in ("bq", "bk")}
            wts[a.name] |= {k: sb(f"{a.name}_{k}", [1, D]) for k in ("bv", "bo")}
        wsw = [sb(f"A0_w{k}_swapped", [P, D]) for k in "qk"]
        bsw = [sb(f"A0_b{k}_swapped", [P, 1]) for k in "qk"]
        cos_sin = sb("cos_sin", [P, 2, S])
        ctxT = sb("ctxT", [P, NB * SC])
        gate_w, gate_b = sb("gate_w", [P, NE]), sb("gate_b", [1, NE])
        w1 = sb("w1", [P, NE, 2 * FF])
        w2 = sb("w2", [P, NE, FC, D])
        b1p, b2p = sb("b1p", [3, NE * 2 * FF], BF16), sb("b2p", [3, NE * D], BF16)
        ones3 = sb("ones3", [3, P], BF16)
        onesb = sb("onesb", [P, P], BF16)
        before = sb("before", [P, P], BF16)
        iota_e = sb("iota_e", [P, NE])
        iota_t = sb("iota_t", [P, MT])
        xn_all = sb("xn_all", [P, NT, D])
        lg = sb("lg", [P, QT, NE])
        top = sb("top", [P, QT, 8])
        top_at = sb("top_at", [P, QT, 8], U32)
        top_f = sb("top_f", [P, QT, 2])
        top_v = sb("top_v", [P, NT, 2])
        picked = sb("picked", [P, 2, NT, NE])
        routed = sb("routed", [P, NT, NE], BF16)
        small = {k: sb(f"moe_{k}", [P, NE]) for k in ("count", "tiles", "cum", "base")}
        routed_sum = sb("routed_sum", [P, NE], BF16)
        place = sb("place", [P, NT, NE])
        place_of = sb("place_of", [P, 2, NT, NE])
        place_f = sb("place_f", [P, 2, NT])
        place_u = sb("place_u", [P, 2, NT], U32)
        tile_le = sb("tile_le", [P, MT, NE])
        tile_f = sb("tile_f", [P, MT])
        tile_e = sb("tile_e", [P, MT], I32)
        gate = sb("gate", [P, 2, NT])
        gate_t = sb("gate_t", [P, 2, NT])
        zero = sb("zero", [P, D])
        dve_step = sb("dve_step", [1, 1])
        xw = {k: sb(f"X1_{k}", [P, D]) for k in ("wq", "wk", "wv")}
        xb_ = {k: sb(f"X1_{k}", [P, 1]) for k in ("bq", "bk")}
        x_bv = sb("X1_bv", [1, D])
        xmask = sb("xmask", [P, QT, SC])
        x_kT = sb("x_kT", [P, NB * SC])
        x_v = sb("x_v", [SC, NB, D])
        x_lg = sb("x_lg", [P, QT, SC])
        x_neg, x_sum, x_rec = sb("x_neg", [P, QT]), sb("x_sum", [P, QT]), sb("x_rec", [P, QT])
        f_w1, f_w2 = sb("f_w1", [P, FF]), sb("f_w2", [P, FC, D])
        f_w1c = sb("f_w1c", [P, 3, FF])
        f_w2q = sb("f_w2q", [P, FC, D], BF16)
        f_taps = sb("f_taps", [P, 3, FF])
        f_cb = sb("f_cb", [3, FF], BF16)
        f_abs, f_mean, f_inv = sb("f_abs", [P, 2]), sb("f_mean", [P, 2]), sb("f_inv", [P, 2])
        f_row = sb("f_row", [P, 2])
        onesf = sb("onesf", [P, P])
        f_amax, f_scale, f_back = sb("f_amax", [P, QT]), sb("f_scale", [P, QT]), sb("f_back", [P, QT])
        f_xT = sb("f_xT", [P, S + 2])
        f_h, f_hm = probs[:, 0, 0:2], probs[:, 0, 2:4]
        f_hq, f_hT = parts[:, 0, 0:2], parts[:, 1, 0:2]
        f_hmax, f_hscale, f_hback = sb("f_hmax", [P, 2]), sb("f_hscale", [P, 2]), sb("f_hback", [P, 2])

        bank_max = [ps(f"bank_max{i}", [P, S]) for i in range(2)]
        bank_st = [ps(f"bank_st{i}", [P, 2, S]) for i in range(2)]
        bank_pv = ps("bank_pv", [P, S])
        bank_misc = ps("bank_misc", [P, S])
        misc_bf = bank_misc[:].bitcast(BF16)

        scr_xn = nc.dram_tensor("routed_tokens", [MT * P, D], F32).ap()
        scr_y = nc.dram_tensor("expert_outputs", [MT * P, D], F32).ap()
        scr = {a.name: nc.dram_tensor(f"stack_{a.name}", [NB, ROWS, 2, NH, S], BF16).ap() for a in atts}
        scr_kx = nc.dram_tensor("stack_kx", [ROWS, NH, NB, SC], BF16).ap()

        s_x = sem("s_x")
        s_w = sem("s_w")
        s_const = sem("s_const")
        s_stat, s_aggr, s_var, s_rstd = sem("s_stat"), sem("s_aggr"), sem("s_var"), sem("s_rstd")
        s_xn, s_xnT, s_xnT_sb = sem("s_xn"), sem("s_xnT"), sem("s_xnT_sb")
        s_xnT_used = sem("s_xnT_used")
        s_out = sem("s_out")
        s_zero, s_pin, s_p, s_b1p, s_xq = sem("s_zero"), sem("s_pin"), sem("s_p"), sem("s_b1p"), sem("s_xq")

        block = es.enter_context(nc.Block())

        def x_tile(t, n=1):
            return xs[:, bass.ds(t, n), :]

        def take_wait(e):
            e.memset(dve_step[:], 0.0)

        def norm_dve(e, ln, b):
            g = 4 * ln + b
            if ln == 0:
                e.wait_ge(s_x, 16)
            else:
                e.wait_ge(x_new[ln - 1][0], x_new[ln - 1][1] + b + 1)
            for j in range(QT):
                e.bn_stats(stats[:, j, :], x_tile(4 * b + j).rearrange("p o d -> p (o d)")).then_inc(s_stat, 1)
            e.wait_ge(s_stat, QT * (g + 1))
            take_wait(e)
            for j in range(QT):
                e.bn_aggr(mv[:, j, :], stats[:, j, :]).then_inc(s_aggr, 1)
            e.wait_ge(s_aggr, QT * (g + 1))
            e.tensor_scalar(var[:], mv[:, :, 1], EPS, None, ALU.add).then_inc(s_var, 1)
            e.wait_ge(s_rstd, g + 1)
            e.wait_ge(s_xnT, g)
            for j in range(QT):
                i = e.tensor_scalar(xn[:, j, :], x_tile(4 * b + j).rearrange("p o d -> p (o d)"),
                                    mv[:, j, 0:1], rstd[:, j:j + 1], ALU.subtract, ALU.mult)
            i.then_inc(s_xn, 1)

        def norm_pool(e, ln, b):
            g = 4 * ln + b
            e.wait_ge(s_var, g + 1)
            e.tensor_tensor(rstd[:], var[:], mhalf[:], ALU.pow).then_inc(s_rstd, 1)

        def norm_pe(e, ln, b, bank):
            g = 4 * ln + b
            e.wait_ge(s_xn, g + 1)
            e.wait_ge(s_xnT_sb, g)
            for j in range(QT):
                i = e.transpose(bank[:, j * P:(j + 1) * P], xn[:, j, :], ident[:])
            i.then_inc(s_xnT, 1)

        def norm_act(e, ln, b, bank):
            g = 4 * ln + b
            e.wait_ge(s_xnT, g + 1)
            e.wait_ge(s_xnT_used, g)
            e.copy(xnT[:], bank[:]).then_inc(s_xnT_sb, 1)

        def stage_pe(e, a, b):
            s, w, g = a.sem, wts[a.name], 4 * a.ln + b
            norm_pe(e, a.ln, b, bank_misc)
            e.wait_ge(s_xnT_sb, g + 1)
            two = a is not a_cross
            e.wait_ge(s["rest"], a.since["rest"] + (2 * b if two else b + 1))
            e.matmul(bank_max[0][:], w["wq"][:], xnT[:], start=True, stop=True).then_inc(s["q_proj"], 1)
            if a.rope:
                e.wait_ge(s["cos_sin"], a.since["cos_sin"] + 2 * b)
                for z in range(2):
                    i = e.matmul(bank_st[z][:, 0], wsw[z][:], xnT[:], start=True, stop=True)
                i.then_inc(s["q_proj"], 1)
            if not two:
                e.drain().then_inc(s_xnT_used, 1)
                return
            e.matmul(bank_max[1][:], w["wk"][:], xnT[:], start=True, stop=True).then_inc(s["k_proj"], 1)
            e.wait_ge(s["v_done"], a.since["v_done"] + b)
            for j in range(QT):
                e.matmul(bank_pv[:, j * D:(j + 1) * D], xnT[:, j * P:(j + 1) * P], w["wv"][:], start=True, stop=False)
                i = e.matmul(bank_pv[:, j * D:(j + 1) * D], ones_row[:], w["bv"][:], start=False, stop=True)
            i.then_inc(s["v_proj"], 1)
            e.drain().then_inc(s_xnT_used, 1)

        def stack_sp(e, a, z, b, per, order):
            s = a.sem
            e.wait_ge(s["part3"], a.since["part3"] + per * b + order + 1)
            for t in range(TERMS):
                part = (Q_PARTS if z == 0 else K_PARTS)[t]
                e.dma_start(scr[a.name][bass.ds(b, 1), t * HD:(t + 1) * HD, z].rearrange("o d h n -> h (o d) n"),
                            parts[:, z, part, :]).then_inc(s["stacked_k" if z else "stacked_q"], 16)

        def heads(h):
            return 64 * (h // 2), h % 2

        def load_unit(e, a, u, slot, b, free=None):
            s = a.sem
            if free is not None:
                e.wait_ge(s["unit_scores"], a.since["unit_scores"] + free)
            for j in range(2):
                hh = slot * HG + 2 * j
                rows = slice(64 * j, 64 * j + ROWS)
                if a is a_cross:
                    e.dma_start(stk[rows, slot, 0], scr[a.name][bass.ds(b, 1), :, 0, hh:hh + 2, :]
                                .rearrange("o r h n -> (o r) h n")).then_inc(s["slot"][slot], 16)
                    e.dma_start(stk[rows, slot, 1, :, 0:SC], scr_kx[:, hh:hh + 2, bass.ds(b, 1), :]
                                .rearrange("r h o n -> r h (o n)")).then_inc(s["slot"][slot], 16)
                else:
                    e.dma_start(stk[rows, slot].rearrange("r z h n -> r z (h n)"),
                                scr[a.name][bass.ds(b, 1), :, :, hh:hh + 2, :]
                                .rearrange("o r z h n -> (o r) z (h n)")).then_inc(s["slot"][slot], 16)

        def slot_dmas(a):
            return 4 if a is a_cross else 2

        def values_pool(e, a, u, slot, b):
            s = a.sem
            wait(e, s["pv"], a.since["pv"] + a.kt * (u - UNITS + 1))
            if a is a_cross:
                i = e.tensor_copy(vsl[0:SC, slot, 0, :, 0:HD + 1],
                                  v9[0:SC, bass.ds(b, 1), slot * HG:(slot + 1) * HG, :].rearrange("p o h d -> p (o h) d"))
            else:
                i = e.tensor_copy(vsl[:, slot, :, :, 0:HD + 1], v9[:, bass.ds(4 * b, QT), slot * HG:(slot + 1) * HG, :])
            i.then_inc(s["values"], 1)

        def max_pe(e, a, u, slot, b, picks):
            s, n = a.sem, len(a.items)
            for m in picks:
                qt, h0, per, keys = a.items[m]
                if m == 0:
                    e.wait_ge(s["slot"][slot], a.since["slot"] + 16 * slot_dmas(a) * (b + 1))
                k = n * slot + m
                bank = bank_max[k % 2]
                wait(e, s["max_out"], a.since["max_out"] + n * u + m - 1)
                for i in range(per):
                    lo, pp = heads(h0 + i)
                    o = bank[:, i * keys:(i + 1) * keys]
                    mm = e.matmul(o, stk[lo:lo + ROWS, slot, 0, pp, qt * P:(qt + 1) * P],
                                  stk[lo:lo + ROWS, slot, 1, pp, 0:keys], start=True, stop=not a.causal)
                    if a.causal:
                        mm = e.matmul(o[:, qt * P:(qt + 1) * P], identb[:], mask_qk[:], start=False, stop=True)
                mm.then_inc(s["max_in"], 1)

        def max_dve(e, a, u, slot, picks):
            s, n = a.sem, len(a.items)
            for m in picks:
                qt, h0, per, keys = a.items[m]
                e.wait_ge(s["max_in"], a.since["max_in"] + n * u + m + 1)
                e.tensor_reduce(mx[:, slot % 2, qt, h0:h0 + per],
                                bank_max[(n * slot + m) % 2][:, 0:per * keys].rearrange("p (h k) -> p h k", h=per),
                                AX.X, ALU.max).then_inc(s["max_out"], 1)

        def negate_dve(e, a, u, slot):
            s, n = a.sem, len(a.items)
            e.wait_ge(s["max_out"], a.since["max_out"] + n * (u + 1))
            wait(e, s["turned"], a.since["turned"] + u - 1)
            src = mx[:, slot % 2].rearrange("p q (j h) -> p j h q", j=2)
            e.tensor_scalar(neg[:, slot % 2, :, 0], src, -1.0, None, ALU.mult).then_inc(s["neg_hi"], 1)
            e.wait_ge(s["neg_hi"], a.since["neg_hi"] + u + 1)
            for j in range(2):
                i = e.scalar_tensor_tensor(neg[:, slot % 2, j, 1], src[:, j], -1.0, neg[:, slot % 2, j, 0],
                                           ALU.mult, ALU.subtract)
            i.then_inc(s["neg_lo"], 1)

        def turn_pe(e, a, u, slot):
            s = a.sem
            e.wait_ge(s["neg_lo"], a.since["neg_lo"] + u + 1)
            e.transpose(misc_bf[0:8 * QT, 0:P], neg[:, slot % 2].rearrange("p j c h q -> p (j c h q)"),
                        identb[:]).then_inc(s["turned"], 1)

        def turn_dve(e, a, u, slot, b):
            s = a.sem
            e.wait_ge(s["turned"], a.since["turned"] + u + 1)
            wait(e, s["shifted"][(slot + 2) % UNITS], a.since["shifted"] + (64 * (b if slot < 2 else b + 1)))
            e.tensor_copy(negT[:, slot % 2, :], misc_bf[0:8 * QT, 0:P]).then_inc(s["rows"], 1)

        def shift_sp(e, a, u, slot):
            s = a.sem
            e.wait_ge(s["rows"], a.since["rows"] + u + 1)
            for j in range(2):
                for c in range(SHIFT):
                    r = (2 * j + c) * 2 * QT
                    e.dma_start(stk[64 * j + ROWS + c:64 * j + ROWS + c + 1, slot, 0].rearrange("o h n -> o (h n)"),
                                negT[r:r + 2 * QT, slot % 2, :]).then_inc(s["shifted"][slot], 16)

        def scores_pe(e, a, u, slot, b, kt):
            s = a.sem
            if kt == 0:
                e.wait_ge(s["shifted"][slot], a.since["shifted"] + 64 * (b + 1))
            q0 = a.first_query(kt)
            n = S - q0
            for j in range(2):
                wait(e, s["probs"], a.since["probs"] + 2 * a.kt * u + 2 * kt + j - 1)
                for pp in range(2):
                    lo = 64 * j
                    o = bank_st[j][0:a.kp, pp, 0:n]
                    mm = e.matmul(o, stk[lo:lo + KR, slot, 1, pp, kt * P:kt * P + a.kp],
                                  stk[lo:lo + KR, slot, 0, pp, q0:S], start=True, stop=not a.causal)
                    if a.causal:
                        mm = e.matmul(o[:, 0:P], identb[:], mask_kq[:], start=False, stop=True)
                mm.then_inc(s["scores"], 1)
            if kt == a.kt - 1:
                e.drain().then_inc(s["unit_scores"], 1)

        def exp_act(e, a, u, kt):
            s = a.sem
            n = S - a.first_query(kt)
            for j in range(2):
                e.wait_ge(s["scores"], a.since["scores"] + 2 * a.kt * u + 2 * kt + j + 1)
                if j == 0:
                    wait(e, s["pv"], a.since["pv"] + a.kt * u + kt - 1)
                half = probs[:, (kt if a.kt > 1 else 0) % 2] if a.kt > 1 else None
                dst = half[0:a.kp, 2 * j:2 * j + 2, 0:n]
                e.activation(dst, bank_st[j][0:a.kp, :, 0:n], ACT.Exp, scale=1 / math.sqrt(HD)).then_inc(s["probs"], 1)

        def exp_act_x(e, a, u, slot):
            s = a.sem
            for j in range(2):
                e.wait_ge(s["scores"], a.since["scores"] + 2 * u + j + 1)
                if j == 0:
                    wait(e, s["pv"], a.since["pv"] + u - 1)
                e.activation(probs[0:SC, slot % 2, 2 * j:2 * j + 2, :], bank_st[j][0:SC], ACT.Exp,
                             scale=1 / math.sqrt(HD)).then_inc(s["probs"], 1)

        def pv_pe(e, a, u, slot, kt):
            s = a.sem
            if kt == 0:
                e.wait_ge(s["values"], a.since["values"] + u + 1)
                e.wait_ge(s["pv_out"], a.since["pv_out"] + u) if not isinstance(u, int) or u > 0 else None
            e.wait_ge(s["probs"], a.since["probs"] + 2 * a.kt * u + 2 * kt + 2)
            q0 = a.first_query(kt)
            half = (kt if a.kt > 1 else slot) % 2
            for h in range(HG):
                mm = e.matmul(bank_pv[VW * h:VW * (h + 1), q0:S], vsl[0:a.kp, slot, kt, h, :],
                              probs[0:a.kp, half, h, 0:S - q0], start=(kt == 0), stop=(kt == a.kt - 1),
                              skip_group_check=True)
            mm.then_inc(s["pv"], 1)

        def pv_out_act(e, a, u):
            s = a.sem
            e.wait_ge(s["pv"], a.since["pv"] + a.kt * (u + 1))
            wait(e, s["out_turned"], a.since["out_turned"] + u)
            e.copy(oT[:], bank_pv[:]).then_inc(s["pv_out"], 1)

        def finish_pe(e, a, u):
            s = a.sem
            e.wait_ge(s["pv_out"], a.since["pv_out"] + u + 1)
            wait(e, s["normed"], a.since["normed"] + u)
            for j in range(QT):
                i = e.transpose(bank_misc[:, j * P:(j + 1) * P], oT[:, j * P:(j + 1) * P], ident[:])
            i.then_inc(s["out_turned"], 1)

        def finish_dve(e, a, u, hg, b):
            s = a.sem
            e.wait_ge(s["out_turned"], a.since["out_turned"] + u + 1)
            src = bank_misc[:].rearrange("p (q h c) -> p q h c", q=QT, h=HG)
            e.reciprocal(rec[:], src[:, :, :, HD]).then_inc(s["reciprocal"], 1)
            e.wait_ge(s["reciprocal"], a.since["reciprocal"] + u + 1)
            if hg == 0:
                wait(e, s["merged"], a.since["merged"] + b)
            e.tensor_tensor(otok[:, :, hg * HG * HD:(hg + 1) * HG * HD].rearrange("p q (h c) -> p q h c", h=HG),
                            src[:, :, :, 0:HD], rec[:].unsqueeze(3).to_broadcast([P, QT, HG, HD]),
                            ALU.mult).then_inc(s["normed"], 1)

        def merge_pe(e, a, b):
            s = a.sem
            e.wait_ge(s["normed"], a.since["normed"] + UNITS * (b + 1))
            for j in range(QT):
                i = e.transpose(bank_misc[:, j * P:(j + 1) * P], otok[:, j, :], ident[:])
            i.then_inc(s["merged"], 1)

        def merge_act(e, a, b):
            s = a.sem
            e.wait_ge(s["merged"], a.since["merged"] + b + 1)
            wait(e, s["proj"], a.since["proj"] + b)
            e.copy(okT[:], bank_misc[:]).then_inc(s["merged_out"], 1)

        def proj_pe(e, a, b):
            s, w = a.sem, wts[a.name]
            e.wait_ge(s["merged_out"], a.since["merged_out"] + b + 1)
            for j in range(QT):
                o = bank_misc[:, j * D:(j + 1) * D]
                e.matmul(o, okT[:, j * P:(j + 1) * P], w["wo"][:], start=True, stop=False)
                i = e.matmul(o, ones_row[:], w["bo"][:], start=False, stop=True)
            i.then_inc(s["proj"], 1)

        def proj_dve(e, a, b):
            s = a.sem
            e.wait_ge(s["proj"], a.since["proj"] + b + 1)
            xb = x_tile(4 * b, QT)
            e.tensor_tensor(xb, xb, bank_misc[:].rearrange("p (q d) -> p q d", q=QT), ALU.add).then_inc(s["x_new"], 1)

        def step_pe(e, a, u, hg, b, ahead, first=False):
            for c in range(a.kt):
                scores_pe(e, a, u, hg, b, c)
                if c == 0 and ahead > 0:
                    if a.sem is not None:
                        turn_pe(e, a, u + 1, (hg + 1) % UNITS)
                if c == min(1, a.kt - 1) and not first:
                    wait_misc_pe_turn(e, a, u + 1, ahead)
                    finish_pe(e, a, u - 1)
                if ahead > 1:
                    max_pe(e, a, u + 2, (hg + 2) % UNITS, b + (hg + 2) // UNITS, a.share(c))
                if c > 0:
                    pv_pe(e, a, u, hg, c - 1)
                if hg == 0 and not first:
                    if c == min(2, a.kt - 1):
                        wait_misc_pe_norm(e, a, u - 1)
                        merge_pe(e, a, b - 1)
                    if c == a.kt - 1:
                        proj_pe(e, a, b - 1)
            pv_pe(e, a, u, hg, a.kt - 1)

        def wait_misc_pe_turn(e, a, u, ahead):
            if ahead > 0:
                e.wait_ge(a.sem["rows"], a.since["rows"] + u + 1)

        def wait_misc_pe_norm(e, a, u):
            e.wait_ge(a.sem["normed"], a.since["normed"] + u + 1)

        def step_dve(e, a, u, hg, b, ahead, first=False):
            for c in range(a.kt):
                if c == 0 and ahead > 0:
                    turn_dve(e, a, u + 1, (hg + 1) % UNITS, b + (hg + 1) // UNITS)
                if c == min(1, a.kt - 1) and not first:
                    finish_dve(e, a, u - 1, (hg - 1) % UNITS, b - 1 if hg == 0 else b)
                if ahead > 1:
                    max_dve(e, a, u + 2, (hg + 2) % UNITS, a.share(c))
                if hg == 0 and not first and c == a.kt - 1:
                    proj_dve(e, a, b - 1)
            if ahead > 1:
                negate_dve(e, a, u + 2, (hg + 2) % UNITS)

        def step_act(e, a, u, hg, b, first=False):
            for c in range(a.kt):
                if a.kt > 1:
                    exp_act(e, a, u, c)
                else:
                    exp_act_x(e, a, u, hg)
                if c == 0 and not first:
                    pv_out_act(e, a, u - 1)
                if hg == 0 and not first and c == min(2, a.kt - 1):
                    merge_act(e, a, b - 1)

        def step_sp(e, a, u, hg, b, ahead):
            if not isinstance(u, int):
                pass
            if ahead > 0:
                shift_sp(e, a, u + 1, (hg + 1) % UNITS)

        def steps(e, a, one):
            one(e, a, 0, 0, 0, 2, True)
            with e.Fori(0, NB - 1) as b:
                for hg in (1, 2, 3, 4):
                    one(e, a, UNITS * b + hg, hg % UNITS, b + hg // UNITS, 2, False)
            for u in range(UNITS * (NB - 1) + 1, UNITS * NB):
                one(e, a, u, u % UNITS, NB - 1, min(2, UNITS * NB - 1 - u), False)

        def attention_pe(e, a):
            for u in range(2):
                max_pe(e, a, u, u, 0, range(len(a.items)))
            turn_pe(e, a, 0, 0)
            e.wait_ge(a.sem["rows"], a.since["rows"] + 1)
            steps(e, a, lambda e, a, u, hg, b, ahead, first: step_pe(e, a, u, hg, b, ahead, first))
            last = UNITS * NB - 1
            finish_pe(e, a, last)
            e.wait_ge(a.sem["normed"], a.since["normed"] + last + 1)
            merge_pe(e, a, NB - 1)
            proj_pe(e, a, NB - 1)

        def attention_dve(e, a):
            for u in range(2):
                max_dve(e, a, u, u, range(len(a.items)))
                negate_dve(e, a, u, u)
            turn_dve(e, a, 0, 0, 0)
            steps(e, a, lambda e, a, u, hg, b, ahead, first: step_dve(e, a, u, hg, b, ahead, first))
            finish_dve(e, a, UNITS * NB - 1, UNITS - 1, NB - 1)
            proj_dve(e, a, NB - 1)

        def attention_act(e, a):
            steps(e, a, lambda e, a, u, hg, b, ahead, first: step_act(e, a, u, hg, b, first))
            pv_out_act(e, a, UNITS * NB - 1)
            merge_act(e, a, NB - 1)

        def attention_pool(e, a):
            for u in range(UNITS):
                values_pool(e, a, u, u, 0)
            with e.Fori(1, NB) as b:
                for hg in range(UNITS):
                    values_pool(e, a, UNITS * b + hg, hg, b)

        def attention_sp(e, a):
            s = a.sem
            e.wait_ge(s["stacked_q"], a.since["stacked_q"] + 16 * TERMS * NB)
            e.wait_ge(s["stacked_k"], a.since["stacked_k"] + (16 * TERMS * (1 if a is a_cross else NB)))
            for u in range(UNITS):
                load_unit(e, a, u, u, 0)
            shift_sp(e, a, 0, 0)
            shift_sp(e, a, 1, 1)
            with e.Fori(1, NB) as b:
                for hg in range(UNITS):
                    u = UNITS * b + hg
                    load_unit(e, a, u, hg, b, free=u - 3)
                    shift_sp(e, a, u - 2, (hg + 2) % UNITS)
            for u in range(UNITS * NB - 2, UNITS * NB):
                shift_sp(e, a, u, u % UNITS)

        def roped(z):
            return probs[:, 1, z]

        def staging_pe(e, a):
            if a is a_cross:
                w = wts["X0"]
                s = a.sem
                e.matmul(bank_max[1][:, 0:NB * SC], w["wk"][:], ctxT[:], start=True, stop=True).then_inc(s["k_proj"], 1)
                for b in range(NB):
                    o = bank_pv[0:SC, b * D:(b + 1) * D]
                    e.matmul(o, ctxT[:, b * SC:(b + 1) * SC], w["wv"][:], start=True, stop=False)
                    i = e.matmul(o, ones_row[:, 0:SC], w["bv"][:], start=False, stop=True)
                i.then_inc(s["v_proj"], 1)
            with e.Fori(0, NB) as b:
                stage_pe(e, a, b)

        def staging_act(e, a):
            w, s = wts[a.name], a.sem
            if a is a_cross:
                e.wait_ge(s["k_proj"], a.since["k_proj"] + 1)
                e.activation(parts[:, 1, 0, 0:NB * SC], bank_max[1][:, 0:NB * SC], ACT.Identity, bias=w["bk"][:])\
                    .then_inc(s["part1"], 1)
                e.wait_ge(s["rest"], a.since["rest"] + 1)
                e.copy(parts[:, 1, 1, 0:NB * SC], rest[:, 1, 0:NB * SC]).then_inc(s["part2"], 1)
            with e.Fori(0, NB) as b:
                norm_act(e, a.ln, b, bank_misc)
                if a is a_cross:
                    e.wait_ge(s["q_proj"], a.since["q_proj"] + b + 1)
                    e.wait_ge(s["stacked_q"], a.since["stacked_q"] + 16 * TERMS * b)
                    e.activation(parts[:, 0, 0, :], bank_max[0][:], ACT.Identity, bias=w["bq"][:]).then_inc(s["part1"], 1)
                    e.wait_ge(s["rest"], a.since["rest"] + b + 2)
                    e.copy(parts[:, 0, 1, :], rest[:, 0, :]).then_inc(s["part2"], 1)
                else:
                    for z in range(2):
                        e.wait_ge(s["stacked_k" if z else "stacked_q"], a.since["stacked_k" if z else "stacked_q"] + 16 * TERMS * b)
                        if a.rope:
                            e.wait_ge(s["roped"], a.since["roped"] + 2 * b + z + 1)
                            e.copy(parts[:, z, 0, :], roped(z)).then_inc(s["part1"], 1)
                            continue
                        e.wait_ge(s["k_proj" if z else "q_proj"], a.since["k_proj" if z else "q_proj"] + b + 1)
                        e.activation(parts[:, z, 0, :], bank_max[z][:], ACT.Identity, bias=w["bk" if z else "bq"][:])\
                            .then_inc(s["part1"], 1)
                    for z in range(2):
                        e.wait_ge(s["rest"], a.since["rest"] + 2 * b + z + 1)
                        e.copy(parts[:, z, 1, :], rest[:, z, :]).then_inc(s["part2"], 1)

        def staging_dve(e, a):
            w, s = wts[a.name], a.sem
            if a is a_cross:
                e.wait_ge(s["part1"], a.since["part1"] + 1)
                e.scalar_tensor_tensor(rest[:, 1, 0:NB * SC], bank_max[1][:, 0:NB * SC], w["bk"][:],
                                       parts[:, 1, 0, 0:NB * SC], ALU.add, ALU.subtract).then_inc(s["rest"], 1)
                e.wait_ge(s["v_proj"], a.since["v_proj"] + 1)
                e.tensor_copy(v9[0:SC, 0:NB, :, 0:HD], bank_pv[0:SC].rearrange("p (b h d) -> p b h d", b=NB, h=NH))\
                    .then_inc(s["v_done"], 1)
            with e.Fori(0, NB) as b:
                norm_dve(e, a.ln, b)
                for z in range(2 if a.rope else 0):
                    e.wait_ge(s["k_proj" if z else "q_proj"], a.since["k_proj" if z else "q_proj"] + (b + 1 if z else 2 * b + 2))
                    e.wait_ge(s["roped"], a.since["roped"] + 2 * b)
                    e.scalar_tensor_tensor(probs[:, 0, z], bank_max[z][:], w["bk" if z else "bq"][:], cos_sin[:, 0],
                                           ALU.add, ALU.mult)
                    e.scalar_tensor_tensor(probs[:, 0, 2 + z], bank_st[z][:, 0], bsw[z][:], cos_sin[:, 1],
                                           ALU.add, ALU.mult).then_inc(s["cos_sin"], 1)
                for z in range(1 if a is a_cross else 2):
                    n0 = b + 1 if a is a_cross else 2 * b + z
                    e.wait_ge(s["part1"], a.since["part1"] + n0 + 1)
                    e.wait_ge(s["part3"], a.since["part3"] + (b + 1 if a is a_cross else 2 * b))
                    if a.rope:
                        e.tensor_tensor(rest[:, z, :], roped(z), parts[:, z, 0, :], ALU.subtract).then_inc(s["rest"], 1)
                        continue
                    e.scalar_tensor_tensor(rest[:, z, :], bank_max[z][:], w["bk" if z else "bq"][:], parts[:, z, 0, :],
                                           ALU.add, ALU.subtract).then_inc(s["rest"], 1)
                if a is not a_cross:
                    e.wait_ge(s["v_proj"], a.since["v_proj"] + b + 1)
                    e.tensor_copy(v9[:, bass.ds(4 * b, QT), :, 0:HD],
                                  bank_pv[:].rearrange("p (q h d) -> p q h d", q=QT, h=NH)).then_inc(s["v_done"], 1)

        def staging_pool(e, a):
            s = a.sem
            if a is a_cross:
                e.wait_ge(s["part2"], a.since["part2"] + 1)
                e.tensor_tensor(parts[:, 1, 2, 0:NB * SC], rest[:, 1, 0:NB * SC], parts[:, 1, 1, 0:NB * SC],
                                ALU.subtract).then_inc(s["part3"], 1)
            with e.Fori(0, NB) as b:
                norm_pool(e, a.ln, b)
                for z in range(2 if a.rope else 0):
                    e.wait_ge(s["cos_sin"], a.since["cos_sin"] + 2 * b + z + 1)
                    e.wait_ge(s["rest"], a.since["rest"] + 2 * b)
                    e.tensor_tensor(roped(z), probs[:, 0, z], probs[:, 0, 2 + z], ALU.add).then_inc(s["roped"], 1)
                for z in range(1 if a is a_cross else 2):
                    e.wait_ge(s["part2"], a.since["part2"] + (b + 1 if a is a_cross else 2 * b + z) + 1)
                    e.wait_ge(s["stacked_k" if z else "stacked_q"], a.since["stacked_k" if z else "stacked_q"] + 16 * TERMS * b)
                    e.tensor_tensor(parts[:, z, 2, :], rest[:, z, :], parts[:, z, 1, :], ALU.subtract)\
                        .then_inc(s["part3"], 1)
            e.wait_ge(s["v_done"], a.since["v_done"] + (1 if a is a_cross else NB))

        def staging_sp(e, a):
            s = a.sem
            if a is a_cross:
                e.wait_ge(s["part3"], a.since["part3"] + 1)
                for t in range(TERMS):
                    e.dma_start(scr_kx[t * HD:(t + 1) * HD].rearrange("d h b n -> h d (b n)"),
                                parts[:, 1, K_PARTS[t], 0:NB * SC]).then_inc(s["stacked_k"], 16)
            with e.Fori(0, NB) as b:
                if a is a_cross:
                    e.wait_ge(s["part3"], a.since["part3"] + b + 2)
                    for t in range(TERMS):
                        e.dma_start(scr[a.name][bass.ds(b, 1), t * HD:(t + 1) * HD, 0].rearrange("o d h n -> h (o d) n"),
                                    parts[:, 0, Q_PARTS[t], :]).then_inc(s["stacked_q"], 16)
                else:
                    for z in range(2):
                        stack_sp(e, a, z, b, 2, z)

        m = {n: sem(f"M0_{n}") for n in """gate_proj logits top top_at top_f picked routed kept sum_in
            rank count count2 floor cum base place place_of place_f place_u tile_le tile_f tile_e
            diff expo plus recip gates zeroed scattered xT xT_out hidden silu act actT actT_out y_in y_out
            weighed1 idx""".split()}
        m |= {n: [sem(f"M0_{n}{i}") for i in range(2)] for n in ("tile_in", "stored", "got1", "got2")}

        def moe_sp_early(e):
            e.wait_ge(m["zeroed"], 1)
            for t in range(MT):
                e.dma_start(scr_xn[t * P:(t + 1) * P, :], zero[:]).then_inc(s_zero, 16)

        def moe_dve(e, ln):
            with e.Fori(0, NB) as b:
                norm_dve(e, ln, b)
                e.wait_ge(m["gate_proj"], b + 1)
                e.tensor_copy(lg[:], bank_max[0][:, 0:QT * NE].rearrange("p (q n) -> p q n", q=QT))\
                    .then_inc(m["logits"], 1)
                e.wait_ge(m["logits"], b + 1)
                take_wait(e)
                for j in range(QT):
                    e.max(top[:, j, :], lg[:, j, :]).then_inc(m["top"], 1)
                e.wait_ge(m["top"], QT * (b + 1))
                take_wait(e)
                for j in range(QT):
                    e.max_index(top_at[:, j, :], top[:, j, :], lg[:, j, :]).then_inc(m["top_at"], 1)
                e.tensor_copy(top_v[:, bass.ds(4 * b, QT), :], top[:, :, 0:2])
                e.wait_ge(m["top_at"], QT * (b + 1))
                e.tensor_copy(top_f[:], top_at[:, :, 0:2]).then_inc(m["top_f"], 1)
                e.wait_ge(m["top_f"], b + 1)
                for k in range(2):
                    e.tensor_tensor(picked[:, k, bass.ds(4 * b, QT), :],
                                    iota_e[:].unsqueeze(1).to_broadcast([P, QT, NE]),
                                    top_f[:, :, k].unsqueeze(2).to_broadcast([P, QT, NE]),
                                    ALU.is_equal).then_inc(m["picked"], 1)
                e.wait_ge(m["picked"], 2 * (b + 1))
                e.tensor_tensor(routed[:, bass.ds(4 * b, QT), :], picked[:, 0, bass.ds(4 * b, QT), :],
                                picked[:, 1, bass.ds(4 * b, QT), :], ALU.add).then_inc(m["routed"], 1)
            e.wait_ge(m["routed"], NB)
            with nc.allow_low_precision("sums of up to 16 ones"):
                e.tensor_reduce(routed_sum[:], routed[:].rearrange("p t n -> p n t"), AX.X, ALU.add)\
                    .then_inc(m["sum_in"], 1)
            e.tensor_tensor(gate_t[:, 0], top_v[:, :, 1], top_v[:, :, 0], ALU.subtract).then_inc(m["diff"], 1)
            e.wait_ge(m["count"], 1)
            e.tensor_scalar(small["count"][:], bank_max[1][:, 0:NE], P - 1.0, 1.0 / P, ALU.add, ALU.mult)\
                .then_inc(m["count2"], 1)
            e.wait_ge(m["count2"], 1)
            e.tensor_scalar(small["tiles"][:], small["count"][:], -0.5 + 0.5 / P, ROUND, ALU.add, ALU.add)\
                .then_inc(m["floor"], 1)
            e.wait_ge(m["floor"], 1)
            e.tensor_scalar(small["count"][:], small["tiles"][:], -ROUND, None, ALU.add).then_inc(m["floor"], 1)
            e.wait_ge(m["floor"], 2)
            e.tensor_tensor_scan(small["cum"][:], onesf[:, 0:NE], small["count"][:], 0.0, ALU.mult, ALU.add)\
                .then_inc(m["cum"], 1)
            e.wait_ge(m["cum"], 1)
            e.tensor_tensor(small["base"][:], small["cum"][:], small["count"][:], ALU.subtract).then_inc(m["base"], 1)
            e.tensor_tensor(tile_le[:], small["cum"][:].unsqueeze(1).to_broadcast([P, MT, NE]),
                            iota_t[:].unsqueeze(2).to_broadcast([P, MT, NE]), ALU.is_le).then_inc(m["tile_le"], 1)
            e.wait_ge(m["rank"], 1)
            e.wait_ge(m["base"], 1)
            e.scalar_tensor_tensor(place[:].rearrange("p t n -> p t n"), small["base"][:].unsqueeze(1).to_broadcast([P, NT, NE]),
                                   float(P), bank_max[0][:, 0:NT * NE].rearrange("p (t n) -> p t n", n=NE),
                                   ALU.mult, ALU.add).then_inc(m["place"], 1)
            e.wait_ge(m["place"], 1)
            for k in range(2):
                e.tensor_tensor(place_of[:, k], picked[:, k], place[:], ALU.mult).then_inc(m["place_of"], 1)
            e.wait_ge(m["place_of"], 2)
            e.tensor_reduce(place_f[:], place_of[:], AX.X, ALU.add).then_inc(m["place_f"], 1)
            e.wait_ge(m["place_f"], 1)
            e.tensor_copy(place_u[:], place_f[:]).then_inc(m["place_u"], 1)
            e.wait_ge(m["tile_le"], 1)
            e.tensor_reduce(tile_f[:], tile_le[:], AX.X, ALU.add).then_inc(m["tile_f"], 1)
            e.wait_ge(m["tile_f"], 1)
            e.tensor_scalar(tile_e[:], tile_f[:], NE - 1.0, None, ALU.min).then_inc(m["tile_e"], 1)
            e.wait_ge(m["expo"], 1)
            e.tensor_scalar(gate[:, 1], gate_t[:, 1], 1.0, None, ALU.add).then_inc(m["plus"], 1)
            e.wait_ge(m["plus"], 1)
            e.reciprocal(gate[:, 0], gate[:, 1]).then_inc(m["recip"], 1)
            e.wait_ge(m["recip"], 1)
            e.tensor_tensor(gate[:, 1], gate[:, 0], gate_t[:, 1], ALU.mult).then_inc(m["gates"], 1)

            with e.Fori(0, MT // 2) as i:
                for k in range(2):
                    t = 2 * i + k
                    e.wait_ge(m["silu"], t + 1)
                    e.wait_ge(m["actT"], t)
                    e.tensor_tensor(act[:], hid[k][0], silu[:, k], ALU.mult).then_inc(m["act"], 1)
                    e.wait_ge(m["y_in"], t + 1)
                    e.wait_ge(m["stored"][k], 16 * i)
                    e.tensor_copy(y_sb[:, k], y_bank[:, 0:D]).then_inc(m["y_out"], 1)
            e.wait_ge(m["gates"], 1)
            for b in range(NB):
                for q in range(QT):
                    t = QT * b + q
                    for k in range(2):
                        e.wait_ge(m["got1" if k == 0 else "got2"][t % 2], 16 * (t // 2 + 1))
                        if k:
                            e.wait_ge(m["weighed1"], t + 1)
                        o = e.scalar_tensor_tensor(xs[:, t, :], got[:, t % 2, k], gate[:, k, t:t + 1], xs[:, t, :],
                                                   ALU.mult, ALU.add)
                        o.then_inc(m["weighed1"] if k == 0 else m["idx"], 1)
                e.wait_ge(m["idx"], QT * (b + 1))
                e.sem_inc(x_new[ln][0], 1)

        act = oT
        actT = okT
        silu = probs[:, 0, 0:2]
        y_sb = probs[:, 0, 2:4, 0:D]
        x_in = probs[:, 1, 0:2, 0:D]
        x_inT = probs[:, 1, 2:4, 0:P]
        got = probs[:].rearrange("p a h s -> p (a h s)")[:, 0:4 * D].rearrange("p (t k d) -> p t k d", t=2, k=2)
        hid = [(bank_max[0][:], bank_max[1][:]), (bank_st[1][:, 0], bank_st[1][:, 1])]
        y_bank = bank_st[0][:, 0]
        t_bank = bank_st[0][:, 1]

        def moe_pool(e, ln):
            with e.Fori(0, NB) as b:
                norm_pool(e, ln, b)
                e.wait_ge(s_xn, 4 * ln + b + 1)
                e.tensor_copy(xn_all[:, bass.ds(4 * b, QT), :], xn[:]).then_inc(m["kept"], 1)
            e.wait_ge(m["kept"], NB)
            e.wait_ge(m["place_u"], 1)
            e.wait_ge(s_zero, 16 * MT)
            for t in range(NT):
                for k in range(2):
                    e.indirect_dma_start(scr_xn, bass.IndirectOffsetOnAxis(ap=place_u[:, k, t:t + 1], axis=0),
                                         xn_all[:, t, :], None).then_inc(m["scattered"], 16)
            for k in range(2):
                e.wait_ge(m["stored"][k], 16 * (MT // 2))
            for t in range(NT):
                for k in range(2):
                    if t >= 2:
                        e.wait_ge(m["idx"], t - 1)
                    e.indirect_dma_start(got[:, t % 2, k], None, scr_y,
                                         bass.IndirectOffsetOnAxis(ap=place_u[:, k, t:t + 1], axis=0))\
                        .then_inc(m["got1" if k == 0 else "got2"][t % 2], 16)

        def moe_pe(e, ln):
            with e.Fori(0, NB) as b:
                norm_pe(e, ln, b, bank_misc)
                e.wait_ge(s_xnT_sb, 4 * ln + b + 1)
                e.wait_ge(m["logits"], b)
                for j in range(QT):
                    o = bank_max[0][:, j * NE:(j + 1) * NE]
                    e.matmul(o, xnT[:, j * P:(j + 1) * P], gate_w[:], start=True, stop=False)
                    i = e.matmul(o, ones_row[:], gate_b[:], start=False, stop=True)
                i.then_inc(m["gate_proj"], 1)
                e.drain().then_inc(s_xnT_used, 1)
            e.wait_ge(m["routed"], NB)
            r = routed[:].rearrange("p t n -> p (t n)")
            o = bank_max[0]
            e.matmul(o[:, 0:NT * NE], before[:], r, start=True, stop=False, skip_group_check=True)
            for k in range(1, NT):
                i = e.matmul(o[:, k * NE:NT * NE], onesb[:], r[:, 0:(NT - k) * NE], start=False, stop=(k == NT - 1),
                             skip_group_check=True)
            i.then_inc(m["rank"], 1)
            e.wait_ge(m["sum_in"], 1)
            e.matmul(bank_max[1][:, 0:NE], onesb[:], routed_sum[:], start=True, stop=True).then_inc(m["count"], 1)
            e.wait_ge(m["tile_e"], 1)
            e.wait_ge(m["place"], 1)
            with e.Fori(0, MT // 2) as i:
                for k in range(2):
                    t = 2 * i + k
                    ex = e.value_load(tile_e[0:1, bass.ds(t, 1)], min_val=0, max_val=NE - 1)
                    e.wait_ge(m["tile_in"][k], 16 * (i + 1))
                    e.wait_ge(m["xT_out"], t)
                    e.transpose(bank_misc[:, 0:P], x_in[:, k], ident[:]).then_inc(m["xT"], 1)
                    e.wait_ge(m["xT_out"], t + 1)
                    for z in range(2):
                        o = hid[k][z]
                        e.matmul(o, x_inT[:, k], w1[:, bass.ds(ex, 1), z * FF:(z + 1) * FF].rearrange("p o n -> p (o n)"),
                                 start=True, stop=False)
                        mm = e.matmul(o, ones3[:], b1p[:, bass.ds(ex * (2 * FF) + z * FF, FF)], start=False, stop=True)
                    mm.then_inc(m["hidden"], 1)
                    e.wait_ge(m["act"], t + 1)
                    e.wait_ge(m["actT_out"], t)
                    for c in range(FC):
                        mm = e.transpose(t_bank[:, c * P:(c + 1) * P], act[:, c * P:(c + 1) * P], ident[:])
                    mm.then_inc(m["actT"], 1)
                    e.wait_ge(m["actT_out"], t + 1)
                    e.wait_ge(m["y_out"], t)
                    for c in range(FC):
                        e.matmul(y_bank[:, 0:D], actT[:, c * P:(c + 1) * P],
                                 w2[:, bass.ds(ex, 1), c, :].rearrange("p o n -> p (o n)"), start=(c == 0), stop=False)
                    e.matmul(y_bank[:, 0:D], ones3[:], b2p[:, bass.ds(ex * D, D)], start=False, stop=True)\
                        .then_inc(m["y_in"], 1)

        def moe_act(e, ln):
            with e.Fori(0, NB) as b:
                norm_act(e, ln, b, bank_misc)
            e.wait_ge(m["diff"], 1)
            e.activation(gate_t[:, 1], gate_t[:, 0], ACT.Exp).then_inc(m["expo"], 1)
            with e.Fori(0, MT // 2) as i:
                for k in range(2):
                    t = 2 * i + k
                    e.wait_ge(m["xT"], t + 1)
                    e.wait_ge(m["hidden"], t)
                    e.copy(x_inT[:, k], bank_misc[:, 0:P]).then_inc(m["xT_out"], 1)
                    e.wait_ge(m["hidden"], t + 1)
                    e.wait_ge(m["act"], t)
                    e.activation(silu[:, k], hid[k][1], ACT.Silu).then_inc(m["silu"], 1)
                    e.wait_ge(m["actT"], t + 1)
                    e.wait_ge(m["y_in"], t)
                    e.copy(actT[:], t_bank).then_inc(m["actT_out"], 1)

        def moe_sp(e):
            e.wait_ge(m["scattered"], 16 * 2 * NT)
            for k in range(2):
                e.dma_start(x_in[:, k], scr_xn[k * P:(k + 1) * P, :]).then_inc(m["tile_in"][k], 16)
            with e.Fori(0, MT // 2 - 1) as i:
                for k in range(2):
                    e.wait_ge(m["xT"], 2 * i + k + 1)
                    e.dma_start(x_in[:, k], scr_xn[bass.ds((2 * i + k + 2) * P, P), :]).then_inc(m["tile_in"][k], 16)
                for k in range(2):
                    e.wait_ge(m["y_out"], 2 * i + k + 1)
                    e.dma_start(scr_y[bass.ds((2 * i + k) * P, P), :], y_sb[:, k]).then_inc(m["stored"][k], 16)
            for k in range(2):
                e.wait_ge(m["y_out"], MT - 1 + k)
                e.dma_start(scr_y[(MT - 2 + k) * P:(MT - 1 + k) * P, :], y_sb[:, k]).then_inc(m["stored"][k], 16)

        c = {n: sem(f"X1_{n}") for n in "k_proj k_out v_proj v_out q_proj q_out logits masked neg probs probsT probsT_out out recip".split()}
        x_qT = okT
        x_p = probs[:, 0, 0:QT, 0:SC]
        x_pT = oT

        def cross_pe(e, ln):
            e.matmul(bank_max[1][:, 0:NB * SC], xw["wk"][:], ctxT[:], start=True, stop=True).then_inc(c["k_proj"], 1)
            for b in range(NB):
                o = bank_pv[0:SC, b * D:(b + 1) * D]
                e.matmul(o, ctxT[:, b * SC:(b + 1) * SC], xw["wv"][:], start=True, stop=False)
                i = e.matmul(o, ones_row[:, 0:SC], x_bv[:], start=False, stop=True)
            i.then_inc(c["v_proj"], 1)
            e.wait_ge(c["k_out"], 1)
            e.wait_ge(c["v_out"], 1)
            with e.Fori(0, NB) as b:
                norm_pe(e, ln, b, bank_misc)
                e.wait_ge(s_xnT_sb, 4 * ln + b + 1)
                e.wait_ge(c["q_out"], b)
                e.matmul(bank_max[0][:], xw["wq"][:], xnT[:], start=True, stop=True).then_inc(c["q_proj"], 1)
                e.drain().then_inc(s_xnT_used, 1)
                e.wait_ge(c["q_out"], b + 1)
                e.wait_ge(c["masked"], b)
                for j in range(QT):
                    i = e.matmul(bank_max[1][:, j * SC:(j + 1) * SC], x_qT[:, j * P:(j + 1) * P],
                                 x_kT[:, bass.ds(b * SC, SC)], start=True, stop=True)
                i.then_inc(c["logits"], 1)
                e.wait_ge(c["probs"], QT * (b + 1))
                e.wait_ge(c["probsT_out"], b)
                for j in range(QT):
                    i = e.transpose(bank_st[0][0:SC, 0, j * P:(j + 1) * P], x_p[:, j], ident[:])
                i.then_inc(c["probsT"], 1)
                e.wait_ge(c["probsT_out"], b + 1)
                e.wait_ge(x_new[ln][0], b)
                for j in range(QT):
                    i = e.matmul(bank_st[1][:, 0, j * P:(j + 1) * P], x_pT[0:SC, j * P:(j + 1) * P],
                                 x_v[:, bass.ds(b, 1), :].rearrange("p o n -> p (o n)"), start=True, stop=True)
                i.then_inc(c["out"], 1)

        def cross_act(e, ln):
            e.wait_ge(c["k_proj"], 1)
            e.activation(x_kT[:], bank_max[1][:, 0:NB * SC], ACT.Identity, bias=xb_["bk"][:]).then_inc(c["k_out"], 1)
            with e.Fori(0, NB) as b:
                norm_act(e, ln, b, bank_misc)
                e.wait_ge(c["q_proj"], b + 1)
                e.wait_ge(c["logits"], b)
                e.activation(x_qT[:], bank_max[0][:], ACT.Identity, bias=xb_["bq"][:]).then_inc(c["q_out"], 1)
                e.wait_ge(c["neg"], b + 1)
                e.wait_ge(c["probsT"], b)
                e.wait_ge(c["recip"], b)
                for j in range(QT):
                    e.activation(x_p[:, j], x_lg[:, j], ACT.Exp, bias=x_neg[:, j:j + 1], accum_out=x_sum[:, j:j + 1])\
                        .then_inc(c["probs"], 1)
                e.wait_ge(c["probsT"], b + 1)
                e.wait_ge(c["out"], b)
                e.copy(x_pT[0:SC, :], bank_st[0][0:SC, 0]).then_inc(c["probsT_out"], 1)

        def cross_dve(e, ln):
            e.wait_ge(c["v_proj"], 1)
            e.tensor_copy(x_v[:], bank_pv[0:SC].rearrange("p (b d) -> p b d", b=NB)).then_inc(c["v_out"], 1)
            with e.Fori(0, NB) as b:
                norm_dve(e, ln, b)
                e.wait_ge(c["logits"], b + 1)
                e.wait_ge(c["probs"], QT * b)
                e.scalar_tensor_tensor(x_lg[:], bank_max[1][:, 0:QT * SC].rearrange("p (q k) -> p q k", q=QT),
                                       1 / math.sqrt(D), xmask[:], ALU.mult, ALU.add).then_inc(c["masked"], 1)
                e.wait_ge(c["masked"], b + 1)
                e.tensor_reduce(x_neg[:], x_lg[:], AX.X, ALU.max, negate=True).then_inc(c["neg"], 1)
                e.wait_ge(c["probs"], QT * (b + 1))
                e.reciprocal(x_rec[:], x_sum[:]).then_inc(c["recip"], 1)
                e.wait_ge(c["recip"], b + 1)
                e.wait_ge(c["out"], b + 1)
                for j in range(QT):
                    xj = x_tile(4 * b + j).rearrange("p o d -> p (o d)")
                    i = e.scalar_tensor_tensor(xj, bank_st[1][:, 0, j * P:(j + 1) * P], x_rec[:, j:j + 1], xj,
                                               ALU.mult, ALU.add)
                i.then_inc(x_new[ln][0], 1)

        f = {n: sem(f"F1_{n}") for n in """abs total mean inv q1 q2 q3 taps amax aclip arec scale back
            n1 n2 xT_out conv silu hmax hclip hrec hscale hback hm1 hm2 hq hT hT_out out added""".split()}

        def weights_dve(e):
            w = (f_w1[:], f_w2[:].rearrange("p c d -> p (c d)"))
            for k in range(2):
                e.tensor_reduce(f_abs[:, k:k + 1], w[k], AX.X, ALU.add, apply_absolute_value=True).then_inc(f["abs"], 1)
            e.wait_ge(f["total"], 1)
            e.tensor_scalar(f_mean[:], bank_misc[:, 0:2], 1.0 / (D * FF), 1e-5, ALU.mult, ALU.max).then_inc(f["mean"], 1)
            e.wait_ge(f["mean"], 1)
            e.reciprocal(f_inv[:], f_mean[:]).then_inc(f["inv"], 1)
            e.wait_ge(f["inv"], 1)
            for k in range(2):
                e.tensor_scalar(w[k], w[k], f_inv[:, k:k + 1], ROUND, ALU.mult, ALU.add).then_inc(f["q1"], 1)
            e.wait_ge(f["q1"], 2)
            for k in range(2):
                e.tensor_scalar(w[k], w[k], -ROUND, 1.0, ALU.add, ALU.min).then_inc(f["q2"], 1)
            e.wait_ge(f["q2"], 2)
            e.tensor_scalar(w[0], w[0], -1.0, f_mean[:, 0:1], ALU.max, ALU.mult).then_inc(f["q3"], 1)
            e.tensor_scalar(f_w2q[:].rearrange("p c d -> p (c d)"), w[1], -1.0, None, ALU.max).then_inc(f["q3"], 1)
            e.wait_ge(f["q3"], 2)
            for k in range(3):
                e.tensor_tensor(f_w1c[:, k], f_taps[:, k], w[0], ALU.mult).then_inc(f["taps"], 1)

        def ffn_dve(e, ln):
            with e.Fori(0, NB) as b:
                norm_dve(e, ln, b)
                e.wait_ge(s_xn, 4 * ln + b + 1)
                e.tensor_reduce(f_amax[:], xn[:], AX.X, ALU.max, apply_absolute_value=True).then_inc(f["amax"], 1)
                e.wait_ge(f["amax"], b + 1)
                e.tensor_scalar(f_amax[:], f_amax[:], 1e-5, None, ALU.max).then_inc(f["aclip"], 1)
                e.wait_ge(f["aclip"], b + 1)
                e.reciprocal(f_scale[:], f_amax[:]).then_inc(f["arec"], 1)
                e.tensor_scalar(f_back[:], f_amax[:], 1.0 / 127.0, None, ALU.mult).then_inc(f["back"], 1)
                e.wait_ge(f["arec"], b + 1)
                e.tensor_scalar(f_scale[:], f_scale[:], 127.0, None, ALU.mult).then_inc(f["scale"], 1)
                e.wait_ge(f["scale"], b + 1)
                for j in range(QT):
                    i = e.tensor_scalar(xn[:, j], xn[:, j], f_scale[:, j:j + 1], ROUND, ALU.mult, ALU.add)
                i.then_inc(f["n1"], 1)
                e.wait_ge(f["n1"], b + 1)
                e.tensor_scalar(xn[:], xn[:], -ROUND, 127.0, ALU.add, ALU.min).then_inc(f["n2"], 1)
                e.wait_ge(f["n2"], b + 1)
                for j in range(QT):
                    i = e.tensor_scalar(xn[:, j], xn[:, j], -128.0, f_back[:, j:j + 1], ALU.max, ALU.mult)
                i.then_inc(s_xq, 1)
                for j in range(QT):
                    t, k = QT * b + j, j % 2
                    e.wait_ge(f["silu"], t + 1)
                    e.tensor_reduce(f_hmax[:, k:k + 1], f_h[:, k], AX.X, ALU.max, apply_absolute_value=True)\
                        .then_inc(f["hmax"], 1)
                    e.wait_ge(f["hmax"], t + 1)
                    e.tensor_scalar(f_hmax[:, k:k + 1], f_hmax[:, k:k + 1], 1e-5, None, ALU.max).then_inc(f["hclip"], 1)
                    e.wait_ge(f["hclip"], t + 1)
                    e.reciprocal(f_hscale[:, k:k + 1], f_hmax[:, k:k + 1]).then_inc(f["hrec"], 1)
                    e.tensor_scalar(f_hback[:, k:k + 1], f_hmax[:, k:k + 1], 1.0 / 127.0, f_mean[:, 1:2],
                                    ALU.mult, ALU.mult).then_inc(f["hback"], 1)
                    e.wait_ge(f["hrec"], t + 1)
                    e.tensor_scalar(f_hscale[:, k:k + 1], f_hscale[:, k:k + 1], 127.0, None, ALU.mult)\
                        .then_inc(f["hscale"], 1)
                    e.wait_ge(f["hscale"], t + 1)
                    e.tensor_scalar(f_hm[:, k], f_h[:, k], f_hscale[:, k:k + 1], ROUND, ALU.mult, ALU.add)\
                        .then_inc(f["hm1"], 1)
                    e.wait_ge(f["hm1"], t + 1)
                    e.tensor_scalar(f_hm[:, k], f_hm[:, k], ROUND + 127.0, ROUND - 128.0, ALU.min, ALU.max)\
                        .then_inc(f["hm2"], 1)
                    e.wait_ge(f["out"], t + 1)
                    xj = x_tile(4 * b + j).rearrange("p o d -> p (o d)")
                    i = e.scalar_tensor_tensor(xj, bank_st[1][:, 0, 0:D], f_hback[:, k:k + 1], xj, ALU.mult, ALU.add)
                    i.then_inc(f["added"], 1)
                e.wait_ge(f["added"], QT * (b + 1))
                e.sem_inc(x_new[ln][0], 1)

        def ffn_pe(e, ln):
            e.wait_ge(f["taps"], 3)
            e.wait_ge(s_b1p, N_PARTS)
            with e.Fori(0, NB) as b:
                e.wait_ge(s_xq, b + 1)
                e.wait_ge(f["xT_out"], b)
                for j in range(QT):
                    i = e.transpose(bank_misc[:, j * P:(j + 1) * P], xn[:, j, :], ident[:])
                i.then_inc(s_xnT, 1)
                e.wait_ge(f["xT_out"], b + 1)
                for j in range(QT):
                    t, k = QT * b + j, j % 2
                    e.wait_ge(f["silu"], max(0, t - 1) if isinstance(t, int) else QT * b + j)
                    for tap in range(3):
                        e.matmul(bank_max[0][:], f_xT[:, j * P + tap:(j + 1) * P + tap], f_w1c[:, tap],
                                 start=(tap == 0), stop=False)
                    e.matmul(bank_max[0][:], ones3[:], f_cb[:], start=False, stop=True).then_inc(f["conv"], 1)
                    e.wait_ge(f["hq"], t + 1)
                    e.wait_ge(f["hT_out"], t)
                    for cc in range(FC):
                        i = e.transpose(f_tb[:, cc * P:(cc + 1) * P], f_hq[:, k, cc * P:(cc + 1) * P], identb[:])
                    i.then_inc(f["hT"], 1)
                    e.wait_ge(f["hT_out"], t + 1)
                    e.wait_ge(f["added"], t)
                    for cc in range(FC):
                        i = e.matmul(bank_st[1][:, 0, 0:D], f_hT[:, k, cc * P:(cc + 1) * P], f_w2q[:, cc, :],
                                     start=(cc == 0), stop=(cc == FC - 1))
                    i.then_inc(f["out"], 1)

        f_tb = bank_pv[:].bitcast(BF16)

        def ffn_act(e, ln):
            with e.Fori(0, NB) as b:
                e.wait_ge(s_xnT, 4 * ln + b + 1)
                e.wait_ge(f["conv"], QT * b)
                e.copy(f_xT[:, 1:S + 1], bank_misc[:]).then_inc(f["xT_out"], 1)
                for j in range(QT):
                    t, k = QT * b + j, j % 2
                    e.wait_ge(f["conv"], t + 1)
                    e.activation(f_h[:, k], bank_max[0][:], ACT.Silu).then_inc(f["silu"], 1)
                    e.wait_ge(f["hm2"], t + 1)
                    e.activation(f_hq[:, k], f_hm[:, k], ACT.Copy, bias=-ROUND).then_inc(f["hq"], 1)
                    e.wait_ge(f["hT"], t + 1)
                    e.copy(f_hT[:, k], f_tb[:, 0:FF]).then_inc(f["hT_out"], 1)

        def ffn_pool(e, ln):
            with e.Fori(0, NB) as b:
                norm_pool(e, ln, b)

        part_srcs = []
        if "M0" in layers:
            part_srcs += [(d["M0_b1"], b1p, NE * 2 * FF), (d["M0_b2"], b2p, NE * D)]
        if "F1" in layers:
            part_srcs += [(d["F1_cb"], f_cb, FF)]
        CH = 1024
        p_chunks = [(src, dst, o, min(CH, n - o)) for src, dst, n in part_srcs for o in range(0, n, CH)]
        N_PARTS = 16 * 3 * len(p_chunks)
        pr = probs[:].rearrange("p a h s -> p (a h s)")
        p_in, p_rest = pr[0:1, 0:CH], pr[0:1, CH:2 * CH]
        p_b = parts[:].rearrange("p a h s -> p (a h s)")
        p_part = [p_b[0:1, i * CH:(i + 1) * CH] for i in range(3)]

        def parts_pool(e):
            for n, (src, dst, o, w) in enumerate(p_chunks):
                e.wait_ge(s_pin, 16 * (n + 1))
                if n:
                    e.wait_ge(s_b1p, 48 * n)
                e.tensor_copy(p_part[0][:, 0:w], p_in[:, 0:w]).then_inc(s_p, 1)
                e.wait_ge(s_p, 5 * n + 1)
                e.tensor_tensor(p_rest[:, 0:w], p_in[:, 0:w], p_part[0][:, 0:w], ALU.subtract).then_inc(s_p, 1)
                e.wait_ge(s_p, 5 * n + 2)
                e.tensor_copy(p_part[1][:, 0:w], p_rest[:, 0:w]).then_inc(s_p, 1)
                e.wait_ge(s_p, 5 * n + 3)
                e.tensor_tensor(p_rest[:, 0:w], p_rest[:, 0:w], p_part[1][:, 0:w], ALU.subtract).then_inc(s_p, 1)
                e.wait_ge(s_p, 5 * n + 4)
                e.tensor_copy(p_part[2][:, 0:w], p_rest[:, 0:w]).then_inc(s_p, 1)

        def parts_sp(e):
            for n, (src, dst, o, w) in enumerate(p_chunks):
                if n:
                    e.wait_ge(s_p, 5 * n)
                e.dma_start(p_in[:, 0:w], src[:, o:o + w]).then_inc(s_pin, 16)
                e.wait_ge(s_p, 5 * (n + 1))
                for i in range(3):
                    e.dma_start(dst[i:i + 1, o:o + w], p_part[i][:, 0:w]).then_inc(s_b1p, 16)

        loads = []
        for a in atts:
            loads += [(wts[a.name][k][:], d[f"{a.name}_{k}"]) for k in wts[a.name]]
        if "A0" in layers:
            for i, k in enumerate("qk"):
                loads += [(wsw[i][:], d[f"A0_w{k}_swapped"]), (bsw[i][:], d[f"A0_b{k}_swapped"])]
            loads += [(cos_sin[:], d["cos_sin"])]
        if "X0" in layers or "X1" in layers:
            loads += [(ctxT[:], d["ctxT"])]
        if "M0" in layers:
            loads += [(gate_w[:], d["M0_gate_w"]), (gate_b[:], d["M0_gate_b"]),
                      (w1[:], d["M0_w1"].rearrange("e p n -> p e n")),
                      (w2[:].rearrange("p e c n -> p (e c) n"), d["M0_w2"].rearrange("e (c p) n -> p (e c) n", p=P))]
        if "X1" in layers:
            loads += [(xw[k][:], d[f"X1_{k}"]) for k in xw] + [(xb_[k][:], d[f"X1_{k}"]) for k in xb_]
            loads += [(x_bv[:], d["X1_bv"]), (xmask[:], d["xmask"].rearrange("(q p) k -> p q k", p=P))]
        if "F1" in layers:
            loads += [(f_w1[:], d["F1_w1"]), (f_w2[:], d["F1_w2"].rearrange("(c p) n -> p c n", p=P))]
            loads += [(f_taps[:, k], d["F1_taps"][k:k + 1, :].to_broadcast([P, FF])) for k in range(3)]

        def program(e, kind, table):
            for n in layers:
                for fn in table[n]:
                    fn(e, next((a for a in atts if a.name == n), ln_of[n]))

        @block.sync
        def _(e):
            e.dma_start(xs[:], d["x"].rearrange("(t p) d -> p t d", p=P)).then_inc(s_x, 16)
            for dst, src in loads:
                e.dma_start(dst, src).then_inc(s_w, 16)
            parts_sp(e)
            if "M0" in layers:
                moe_sp_early(e)
            program(e, "sp", {"A0": [staging_sp, attention_sp], "X0": [staging_sp, attention_sp],
                              "M0": [lambda e, ln: moe_sp(e)], "A1": [staging_sp, attention_sp], "X1": [], "F1": []})
            e.wait_ge(x_new[-1][0], x_new[-1][1] + NB)
            e.dma_start(out.rearrange("(t p) d -> p t d", p=P), xs[:]).then_inc(s_out, 16)
            e.wait_ge(s_out, 16)

        @block.gpsimd
        def _(e):
            e.memset(mhalf[:], -0.5)
            e.memset(ones_row[:], 1.0)
            e.memset(ones3[:], 1.0)
            e.memset(onesb[:], 1.0)
            e.memset(onesf[:], 1.0)
            e.memset(f_xT[:], 0.0)
            e.memset(zero[:], 0.0).then_inc(m["zeroed"], 1)
            e.memset(v9[:], 1.0)
            e.memset(vsl[:], 0.0)
            e.memset(stk[:], 1.0)
            e.iota(iota_e[:], pattern=[[1, NE]], base=0, channel_multiplier=0, allow_small_or_imprecise_dtypes=True)
            e.iota(iota_t[:], pattern=[[1, MT]], base=0, channel_multiplier=0, allow_small_or_imprecise_dtypes=True)
            e.memset(ident[:], 1.0).then_inc(s_const, 1)
            e.wait_ge(s_const, 1)
            e.affine_select(out=ident[:], in_=ident[:], compare_op=ALU.is_equal, fill=0.0, base=0,
                            pattern=[[-1, P]], channel_multiplier=1)
            e.affine_select(out=before[:], in_=onesb[:], compare_op=ALU.is_gt, fill=0.0, base=0,
                            pattern=[[1, P]], channel_multiplier=-1)
            e.memset(mask_qk[:], 0.0)
            e.memset(mask_kq[:], 0.0).then_inc(s_const, 1)
            e.wait_ge(s_const, 2)
            e.affine_select(out=mask_qk[:], in_=mask_qk[:], compare_op=ALU.is_ge, fill=MASKED, base=0,
                            pattern=[[-1, P]], channel_multiplier=1)
            e.affine_select(out=mask_kq[:], in_=mask_kq[:], compare_op=ALU.is_ge, fill=MASKED, base=0,
                            pattern=[[1, P]], channel_multiplier=-1)
            e.tensor_copy(identb[:], ident[:]).then_inc(s_const, 1)
            parts_pool(e)
            program(e, "pool", {"A0": [staging_pool, attention_pool], "X0": [staging_pool, attention_pool],
                                "M0": [moe_pool], "A1": [staging_pool, attention_pool],
                                "X1": [ffn_pool], "F1": [ffn_pool]})

        @block.tensor
        def _(e):
            e.wait_ge(s_w, 16 * len(loads))
            e.wait_ge(s_const, 3)
            if "F1" in layers:
                e.wait_ge(f["abs"], 2)
                e.matmul(bank_misc[:, 0:2], onesf[:], f_abs[:], start=True, stop=True).then_inc(f["total"], 1)
                e.wait_ge(f["mean"], 1)
            program(e, "pe", {"A0": [staging_pe, attention_pe], "X0": [staging_pe, attention_pe], "M0": [moe_pe],
                              "A1": [staging_pe, attention_pe], "X1": [cross_pe], "F1": [ffn_pe]})

        @block.vector
        def _(e):
            e.wait_ge(s_w, 16 * len(loads))
            e.wait_ge(s_const, 3)
            if "F1" in layers:
                weights_dve(e)
            e.wait_ge(s_b1p, N_PARTS)
            program(e, "dve", {"A0": [staging_dve, attention_dve], "X0": [staging_dve, attention_dve],
                               "M0": [moe_dve], "A1": [staging_dve, attention_dve], "X1": [cross_dve],
                               "F1": [ffn_dve]})

        @block.scalar
        def _(e):
            e.wait_ge(s_w, 16 * len(loads))
            e.wait_ge(s_b1p, N_PARTS)
            program(e, "act", {"A0": [staging_act, attention_act], "X0": [staging_act, attention_act],
                               "M0": [moe_act], "A1": [staging_act, attention_act], "X1": [cross_act],
                               "F1": [ffn_act]})


def lay_out(i):
    t = lambda v: np.ascontiguousarray(np.asarray(v).T)
    col = lambda v: np.asarray(v).reshape(P, 1)
    row = lambda v: np.asarray(v).reshape(1, -1)
    o = {"x": np.asarray(i["x"]).reshape(NT * P, D), "ctxT": t(np.asarray(i["ctx_1024"]).reshape(NB * SC, D)),
         "xmask": np.asarray(i["mask_1xSxS2_ff0"])[0]}
    for name, src in (("A0", "L0_attn_"), ("A1", "L1_attn_")):
        o |= {f"{name}_w{k}": t(i[f"{src}w{k}"]) for k in "qkvo"}
        o |= {f"{name}_b{k}": (col if k in "qk" else row)(i[f"{src}b{k}"]) for k in "qkvo"}
    o |= {f"X0_w{k}": np.asarray(i[f"L0_xattn_W{k}"]) for k in "qkvo"}
    o |= {f"X0_b{k}": (col if k in "qk" else row)(i[f"L0_xattn_b{k}"]) for k in "qkvo"}
    pair = np.arange(D) ^ 1
    for k in "qk":
        o[f"A0_w{k}_swapped"] = np.ascontiguousarray(o[f"A0_w{k}"][:, pair])
        o[f"A0_b{k}_swapped"] = np.ascontiguousarray(o[f"A0_b{k}"][pair])
    f32 = np.float32
    rate = np.exp((f32(2.0) * np.arange(HD // 2, dtype=f32) / f32(HD) * f32(math.log(10000.0))).astype(f32))
    theta = (np.arange(S, dtype=f32)[None, :] / rate[:, None]).astype(f32).astype(np.float64)
    which = (np.arange(D) % HD) // 2
    sign = np.where(np.arange(D) % 2 == 0, -1.0, 1.0)[:, None]
    o["cos_sin"] = np.stack([np.cos(theta)[which], sign * np.sin(theta)[which]], axis=1).astype(f32)
    o |= {"M0_gate_w": i["L0_ffn_gate_w"], "M0_gate_b": row(i["L0_ffn_gate_b"]), "M0_w1": i["L0_ffn_w1"],
          "M0_b1": row(i["L0_ffn_b1"]), "M0_w2": i["L0_ffn_w2"], "M0_b2": row(i["L0_ffn_b2"])}
    o |= {f"X1_w{k}": i[f"L1_xattn_kernel_{k}"] for k in "qkv"}
    o |= {f"X1_b{k}": (col if k in "qk" else row)(i[f"L1_xattn_bias_{k}"]) for k in "qkv"}
    o |= {"F1_w1": t(i["L1_ffn_w1"]), "F1_taps": np.ascontiguousarray(np.asarray(i["L1_ffn_conv_w"])[:, 0, :].T),
          "F1_cb": row(i["L1_ffn_conv_b"]), "F1_w2": t(i["L1_ffn_w2"])}
    return {k: np.ascontiguousarray(v) for k, v in o.items()}


def kernel(**inputs):
    import concourse.bacc as bacc
    from concourse.bass_utils import run_bass_kernel_spmd

    nc = bacc.Bacc("TRN2", target_bir_lowering=False, num_devices=1)
    arrays = {f"in_{k}": v for k, v in lay_out(inputs).items()}
    d = {k[3:]: nc.dram_tensor(k, v.shape, mybir.dt.from_np(v.dtype), kind="ExternalInput").ap() for k, v in arrays.items()}
    out = nc.dram_tensor("out", (NT * P, D), F32, kind="ExternalOutput").ap()
    build(nc, d, out)
    r = run_bass_kernel_spmd(nc, [arrays], core_ids=[0])
    return r.results[0]["out"].reshape(NB, S, D)
```

```python
from contextlib import ExitStack
import math

import numpy as np

import concourse.bass as bass
from concourse import mybir
from concourse.alu_op_type import AluOpType as ALU

ACT = mybir.ActivationFunctionType
AX = mybir.AxisListType
F32 = mybir.dt.float32
BF16 = mybir.dt.bfloat16
I32 = mybir.dt.int32
U32 = mybir.dt.uint32

P = 128
NB, S, D = 4, 512, 128
QT = S // P
NT = NB * QT
NH, HD = 16, 8
SC = 77
HG = 4
UNITS = NH // HG
TERMS = 6
ROWS = TERMS * HD
SHIFT = 2
KR = ROWS + SHIFT
NE, FF = 8, 512
FC = FF // P
MT = 2 * NT + NE
ROUND = 1.5 * 2 ** 23
VW = 32
EPS = 1e-5
FREE = 1
MASKED = -1e30
Q_PARTS = (0, 1, 2, 0, 1, 0)
K_PARTS = (0, 0, 0, 1, 1, 2)


def wait(e, sem, value):
    if isinstance(value, int) and value <= 0:
        return
    e.wait_ge(sem, value)


ATT_FREE = "out_turned normed merged proj rest cos_sin v_done stacked_k stacked_q roped part3".split()


class Attention:

    def __init__(self, name, ln, keys, causal):
        self.name, self.ln, self.keys, self.causal = name, ln, keys, causal
        self.kt = -(-keys // P)
        self.kp = min(keys, P)
        self.items = []
        for qt in range(QT):
            n = (qt + 1) * P if causal else keys
            per = max(1, min(2, S // n))
            self.items += [(qt, h, per, n) for h in range(0, HG, per)]
        self.sem = {}
        self.rope = causal

    def totals(self):
        cross, units = self.name == "X0", UNITS * NB
        both = NB + 1 if cross else 2 * NB
        of = dict.fromkeys(ATT_SEMS, units)
        of |= dict.fromkeys(("part1", "rest", "part2", "part3"), both)
        of |= dict.fromkeys(("k_proj", "v_proj", "v_done"), 1 if cross else NB)
        of |= dict.fromkeys(("cos_sin", "roped"), 2 * NB if self.rope else 0)
        of |= dict.fromkeys(("merged", "merged_out", "proj", "x_new"), NB)
        of |= dict.fromkeys(("max_in", "max_out"), units * len(self.items))
        of |= dict.fromkeys(("scores", "probs"), 2 * self.kt * units)
        of |= {"q_proj": 2 * NB if self.rope else NB, "pv": self.kt * units, "shifted": 64 * NB,
               "slot": 16 * (4 if cross else 2) * NB, "stacked_q": 16 * TERMS * NB,
               "stacked_k": 16 * TERMS * (1 if cross else NB)}
        return of

    def first_query(self, kt):
        return kt * P if self.causal else 0

    def share(self, c):
        n = len(self.items)
        return range(n * c // self.kt, n * (c + 1) // self.kt)


ATT_SEMS = """q_proj k_proj v_proj part1 rest part2 part3 v_done stacked_q stacked_k values cos_sin roped
max_in max_out neg_hi neg_lo turned rows scores probs pv unit_scores pv_out out_turned
reciprocal normed merged merged_out proj x_new""".split()


def build(nc, d, out, layers=("A0", "X0", "M0", "A1", "X1", "F1")):
    ln_of = {n: i for i, n in enumerate(layers)}
    es = ExitStack()
    with es:
        def sb(name, shape, dt=F32):
            return es.enter_context(nc.sbuf_tensor(name, shape, dt))

        def ps(name, shape, dt=F32):
            return es.enter_context(nc.psum_tensor(name, shape, dt))

        def sem(name):
            return es.enter_context(nc.semaphore(name))

        a_self0 = Attention("A0", ln_of.get("A0"), S, True)
        a_cross = Attention("X0", ln_of.get("X0"), SC, False)
        a_self1 = Attention("A1", ln_of.get("A1"), S, False)
        atts = [a for a in (a_self0, a_cross, a_self1) if a.name in layers]
        att_sem = {n: sem(f"att_{n}") for n in ATT_SEMS}
        att_sem |= {n: [sem(f"att_{n}{i}") for i in range(UNITS)] for n in ("slot", "shifted")}
        since = {n: FREE if n in ATT_FREE else 0 for n in att_sem}
        for a in atts:
            a.sem, a.since = att_sem, dict(since)
            since = {n: v + a.totals()[n] for n, v in since.items()}
        of_att = {a.name: (att_sem["x_new"], a.since["x_new"]) for a in atts}
        x_new = [of_att.get(n) or (sem(f"{n}_x"), FREE) for n in layers]

        xs = sb("x_sb", [P, NT, D])
        stats = sb("stats", [P, QT, 6])
        mv = sb("mv", [P, QT, 2])
        var = sb("var", [P, QT])
        rstd = sb("rstd", [P, QT])
        mhalf = sb("mhalf", [P, QT])
        xn = sb("xn", [P, QT, D])
        xnT = sb("xnT", [P, S])
        ident = sb("ident", [P, P])
        identb = sb("identb", [P, P], BF16)
        ones_row = sb("ones_row", [1, P])
        mask_qk = sb("mask_qk", [P, P], BF16)
        mask_kq = sb("mask_kq", [P, P], BF16)
        parts = sb("parts", [P, 2, 3, S], BF16)
        rest = sb("rest", [P, 2, S])
        v9 = sb("v9", [P, NT, NH, HD + 1])
        stk = sb("stk", [P, UNITS, 3, 2, S], BF16)
        fill = sb("fill", [P, 2, S], BF16)
        vsl = sb("vsl", [P, UNITS, QT, HG, VW])
        mx = sb("mx", [P, 2, QT, HG])
        neg = sb("neg", [P, 2, 2, 2, 2, QT], BF16)
        negT = sb("negT", [8 * QT, 2, P], BF16)
        probs = sb("probs", [P, 2, HG, S])
        oT = sb("oT", [P, S])
        rec = sb("rec", [P, QT, HG])
        otok = sb("otok", [P, QT, D])
        okT = sb("okT", [P, S])
        wts = {}
        for a in atts:
            wts[a.name] = {k: sb(f"{a.name}_{k}", [P, D]) for k in ("wq", "wk", "wv", "wo")}
            wts[a.name] |= {k: sb(f"{a.name}_{k}", [P, 1]) for k in ("bq", "bk")}
            wts[a.name] |= {k: sb(f"{a.name}_{k}", [1, D]) for k in ("bv", "bo")}
        wsw = [sb(f"A0_w{k}_swapped", [P, D]) for k in "qk"]
        bsw = [sb(f"A0_b{k}_swapped", [P, 1]) for k in "qk"]
        cos_sin = sb("cos_sin", [P, 2, S])
        ctxT = sb("ctxT", [P, NB * SC])
        gate_w, gate_b = sb("gate_w", [P, NE]), sb("gate_b", [1, NE])
        w1 = sb("w1", [P, NE, 2 * FF])
        w2 = sb("w2", [P, NE, FC, D])
        b1p, b2p = sb("b1p", [3, NE * 2 * FF], BF16), sb("b2p", [3, NE * D], BF16)
        ones3 = sb("ones3", [3, P], BF16)
        BIAS = (NE * 2 * FF + NE * D + FF) // P
        bias_in, bias_part = sb("bias_in", [P, BIAS]), sb("bias_part", [P, 3, BIAS], BF16)
        onesb = sb("onesb", [P, P], BF16)
        before = sb("before", [P, P], BF16)
        iota_e = sb("iota_e", [P, NE])
        iota_t = sb("iota_t", [P, MT])
        xn_all = v9[:].rearrange("p t h d -> p (t h d)")[:, 0:NT * D].rearrange("p (t d) -> p t d", t=NT)
        lg = sb("lg", [P, QT, NE])
        top = sb("top", [P, QT, 8])
        top_at = sb("top_at", [P, QT, 8], U32)
        top_f = sb("top_f", [P, QT, 2])
        top_v = sb("top_v", [P, NT, 2])
        picked = sb("picked", [P, 2, NT, NE])
        routed = sb("routed", [P, NT, NE], BF16)
        small = {k: sb(f"moe_{k}", [P, NE]) for k in ("count", "tiles", "cum", "base")}
        routed_sum = sb("routed_sum", [P, NE], BF16)
        place = sb("place", [P, NT, NE])
        place_of = sb("place_of", [P, 2, NT, NE])
        place_f = sb("place_f", [P, 2, NT])
        place_u = sb("place_u", [P, 2, NT], U32)
        tile_le = sb("tile_le", [P, MT, NE])
        tile_f = sb("tile_f", [P, MT])
        tile_e = sb("tile_e", [P, MT], I32)
        gate = sb("gate", [P, 2, NT])
        gate_t = sb("gate_t", [P, 2, NT])
        zero = sb("zero", [P, D])
        dve_step = sb("dve_step", [1, 1])
        xw = {k: sb(f"X1_{k}", [P, D]) for k in ("wq", "wk", "wv")}
        xb_ = {k: sb(f"X1_{k}", [P, 1]) for k in ("bq", "bk")}
        x_bv = sb("X1_bv", [1, D])
        xmask = sb("xmask", [P, QT, SC])
        x_kT = sb("x_kT", [P, NB * SC])
        x_v = sb("x_v", [SC, NB, D])
        x_lg = sb("x_lg", [P, QT, SC])
        x_neg, x_sum, x_rec = sb("x_neg", [P, QT]), sb("x_sum", [P, QT]), sb("x_rec", [P, QT])
        f_w1, f_w2 = sb("f_w1", [P, FF]), sb("f_w2", [P, FC, D])
        f_w1c = sb("f_w1c", [P, 3, FF])
        f_w2q = sb("f_w2q", [P, FC, D], BF16)
        f_taps = sb("f_taps", [P, 3, FF])
        f_cb = sb("f_cb", [3, FF], BF16)
        f_abs, f_mean, f_inv = sb("f_abs", [P, 2]), sb("f_mean", [P, 2]), sb("f_inv", [P, 2])
        f_row = sb("f_row", [P, 2])
        onesf = sb("onesf", [P, P])
        f_amax, f_scale, f_back = sb("f_amax", [P, QT]), sb("f_scale", [P, QT]), sb("f_back", [P, QT])
        f_xT = sb("f_xT", [P, S + 2])
        f_h, f_hm = probs[:, 0, 0:2], probs[:, 0, 2:4]
        f_hq, f_hT = parts[:, 0, 0:2], parts[:, 1, 0:2]
        f_hmax, f_hscale, f_hback = sb("f_hmax", [P, 2]), sb("f_hscale", [P, 2]), sb("f_hback", [P, 2])

        bank_max = [ps(f"bank_max{i}", [P, S]) for i in range(2)]
        bank_st = [ps(f"bank_st{i}", [P, 2, S]) for i in range(2)]
        bank_pv = ps("bank_pv", [P, S])
        bank_misc = ps("bank_misc", [P, S])
        misc_bf = bank_misc[:].bitcast(BF16)

        scr_xn = nc.dram_tensor("routed_tokens", [MT * P, D], F32).ap()
        scr_y = nc.dram_tensor("expert_outputs", [MT * P, D], F32).ap()
        scr = {a.name: nc.dram_tensor(f"stack_{a.name}", [NB, KR, 2, NH, S], BF16).ap() for a in atts}
        scr_kx = nc.dram_tensor("stack_kx", [KR, NH, NB, SC], BF16).ap()

        s_x = sem("s_x")
        s_w, s_later = sem("s_w"), sem("s_later")
        s_ones = sem("s_ones")
        s_fill, s_filled = sem("s_fill"), sem("s_filled")
        s_const = sem("s_const")
        s_stat, s_aggr, s_var, s_rstd = sem("s_stat"), sem("s_aggr"), sem("s_var"), sem("s_rstd")
        s_xn, s_xnT, s_xnT_sb = sem("s_xn"), sem("s_xnT"), sem("s_xnT_sb")
        s_xnT_used = sem("s_xnT_used")
        s_out = sem("s_out")
        s_zero, s_pin, s_p, s_b1p, s_xq = sem("s_zero"), sem("s_pin"), sem("s_p"), sem("s_b1p"), sem("s_xq")

        block = es.enter_context(nc.Block())

        def x_tile(t, n=1):
            return xs[:, bass.ds(t, n), :]

        def take_wait(e):
            e.memset(dve_step[:], 0.0)

        def norm_dve(e, ln, b):
            g = 4 * ln + b
            if ln == 0:
                e.wait_ge(s_x, 16)
            else:
                e.wait_ge(x_new[ln - 1][0], x_new[ln - 1][1] + b + 1)
            for j in range(QT):
                e.bn_stats(stats[:, j, :], x_tile(4 * b + j).rearrange("p o d -> p (o d)")).then_inc(s_stat, 1)
            e.wait_ge(s_stat, QT * (g + 1))
            take_wait(e)
            for j in range(QT):
                e.bn_aggr(mv[:, j, :], stats[:, j, :]).then_inc(s_aggr, 1)
            e.wait_ge(s_aggr, QT * (g + 1))
            e.tensor_scalar(var[:], mv[:, :, 1], EPS, None, ALU.add).then_inc(s_var, 1)
            e.wait_ge(s_rstd, g + 1)
            e.wait_ge(s_xnT, FREE + g)
            for j in range(QT):
                i = e.tensor_scalar(xn[:, j, :], x_tile(4 * b + j).rearrange("p o d -> p (o d)"),
                                    mv[:, j, 0:1], rstd[:, j:j + 1], ALU.subtract, ALU.mult)
            i.then_inc(s_xn, 1)

        def norm_pool(e, ln, b):
            g = 4 * ln + b
            e.wait_ge(s_var, g + 1)
            e.tensor_tensor(rstd[:], var[:], mhalf[:], ALU.pow).then_inc(s_rstd, 1)

        def norm_pe(e, ln, b, bank):
            g = 4 * ln + b
            e.wait_ge(s_xn, g + 1)
            e.wait_ge(s_xnT_sb, FREE + g)
            for j in range(QT):
                i = e.transpose(bank[:, j * P:(j + 1) * P], xn[:, j, :], ident[:])
            i.then_inc(s_xnT, 1)

        def norm_act(e, ln, b, bank):
            g = 4 * ln + b
            e.wait_ge(s_xnT, FREE + g + 1)
            e.wait_ge(s_xnT_used, FREE + g)
            e.copy(xnT[:], bank[:]).then_inc(s_xnT_sb, 1)

        def stage_pe(e, a, b):
            s, w, g = a.sem, wts[a.name], 4 * a.ln + b
            norm_pe(e, a.ln, b, bank_misc)
            e.wait_ge(s_xnT_sb, FREE + g + 1)
            two = a is not a_cross
            e.wait_ge(s["rest"], a.since["rest"] + (2 * b if two else b + 1))
            e.matmul(bank_max[0][:], w["wq"][:], xnT[:], start=True, stop=True).then_inc(s["q_proj"], 1)
            if a.rope:
                e.wait_ge(s["cos_sin"], a.since["cos_sin"] + 2 * b)
                for z in range(2):
                    i = e.matmul(bank_st[z][:, 0], wsw[z][:], xnT[:], start=True, stop=True)
                i.then_inc(s["q_proj"], 1)
            if not two:
                e.drain().then_inc(s_xnT_used, 1)
                return
            e.matmul(bank_max[1][:], w["wk"][:], xnT[:], start=True, stop=True).then_inc(s["k_proj"], 1)
            e.wait_ge(s["v_done"], a.since["v_done"] + b)
            for j in range(QT):
                e.matmul(bank_pv[:, j * D:(j + 1) * D], xnT[:, j * P:(j + 1) * P], w["wv"][:], start=True, stop=False)
                i = e.matmul(bank_pv[:, j * D:(j + 1) * D], ones_row[:], w["bv"][:], start=False, stop=True)
            i.then_inc(s["v_proj"], 1)
            e.drain().then_inc(s_xnT_used, 1)

        def stack_sp(e, a, z, b, per, order):
            s = a.sem
            e.wait_ge(s["part3"], a.since["part3"] + per * b + order + 1)
            for t in range(TERMS):
                part = (Q_PARTS if z == 0 else K_PARTS)[t]
                e.dma_start(scr[a.name][bass.ds(b, 1), t * HD:(t + 1) * HD, z].rearrange("o d h n -> h (o d) n"),
                            parts[:, z, part, :]).then_inc(s["stacked_k" if z else "stacked_q"], 16)

        def heads(h):
            return h // 2, h % 2

        def load_unit(e, a, u, slot, b, free=None):
            s = a.sem
            if free is not None:
                e.wait_ge(s["unit_scores"], a.since["unit_scores"] + free)
            for j in range(2):
                hh = slot * HG + 2 * j
                rows = slice(64 * j, 64 * j + KR)
                if a is a_cross:
                    e.dma_start(stk[rows, slot, 0], scr[a.name][bass.ds(b, 1), :, 0, hh:hh + 2, :]
                                .rearrange("o r h n -> (o r) h n")).then_inc(s["slot"][slot], 16)
                    e.dma_start(stk[rows, slot, 1 + j, :, 0:SC], scr_kx[:, hh:hh + 2, bass.ds(b, 1), :]
                                .rearrange("r h o n -> r h (o n)")).then_inc(s["slot"][slot], 16)
                else:
                    e.dma_start(stk[rows, slot, 0:j + 2:j + 1].rearrange("r z h n -> r z (h n)"),
                                scr[a.name][bass.ds(b, 1), :, :, hh:hh + 2, :]
                                .rearrange("o r z h n -> (o r) z (h n)")).then_inc(s["slot"][slot], 16)

        def slot_dmas(a):
            return 4 if a is a_cross else 2

        def values_pool(e, a, u, slot, b):
            s = a.sem
            wait(e, s["pv"], a.since["pv"] + a.kt * (u - UNITS + 1))
            if a is a_cross:
                i = e.tensor_copy(vsl[0:SC, slot, 0, :, 0:HD + 1],
                                  v9[0:SC, bass.ds(b, 1), slot * HG:(slot + 1) * HG, :].rearrange("p o h d -> p (o h) d"))
            else:
                i = e.tensor_copy(vsl[:, slot, :, :, 0:HD + 1], v9[:, bass.ds(4 * b, QT), slot * HG:(slot + 1) * HG, :])
            i.then_inc(s["values"], 1)

        def max_pe(e, a, u, slot, b, picks):
            s, n = a.sem, len(a.items)
            for m in picks:
                qt, h0, per, keys = a.items[m]
                if m == 0:
                    e.wait_ge(s["slot"][slot], a.since["slot"] + 16 * slot_dmas(a) * (b + 1))
                k = n * slot + m
                bank = bank_max[k % 2]
                wait(e, s["max_out"], a.since["max_out"] + n * u + m - 1)
                for i in range(per):
                    j, pp = heads(h0 + i)
                    o = bank[:, i * keys:(i + 1) * keys]
                    mm = e.matmul(o, stk[:, slot, 0, pp, qt * P:(qt + 1) * P], stk[:, slot, 1 + j, pp, 0:keys], start=True, stop=not a.causal)
                    if a.causal:
                        mm = e.matmul(o[:, qt * P:(qt + 1) * P], identb[:], mask_qk[:], start=False, stop=True)
                mm.then_inc(s["max_in"], 1)

        def max_dve(e, a, u, slot, picks):
            s, n = a.sem, len(a.items)
            for m in picks:
                qt, h0, per, keys = a.items[m]
                e.wait_ge(s["max_in"], a.since["max_in"] + n * u + m + 1)
                e.tensor_reduce(mx[:, slot % 2, qt, h0:h0 + per],
                                bank_max[(n * slot + m) % 2][:, 0:per * keys].rearrange("p (h k) -> p h k", h=per),
                                AX.X, ALU.max).then_inc(s["max_out"], 1)

        def negate_dve(e, a, u, slot):
            s, n = a.sem, len(a.items)
            e.wait_ge(s["max_out"], a.since["max_out"] + n * (u + 1))
            wait(e, s["turned"], a.since["turned"] + u - 1)
            src = mx[:, slot % 2].rearrange("p q (j h) -> p j h q", j=2)
            e.tensor_scalar(neg[:, slot % 2, :, 0], src, -1.0, None, ALU.mult).then_inc(s["neg_hi"], 1)
            e.wait_ge(s["neg_hi"], a.since["neg_hi"] + u + 1)
            for j in range(2):
                i = e.scalar_tensor_tensor(neg[:, slot % 2, j, 1], src[:, j], -1.0, neg[:, slot % 2, j, 0],
                                           ALU.mult, ALU.subtract)
            i.then_inc(s["neg_lo"], 1)

        def turn_pe(e, a, u, slot):
            s = a.sem
            e.wait_ge(s["neg_lo"], a.since["neg_lo"] + u + 1)
            e.transpose(misc_bf[0:8 * QT, 0:P], neg[:, slot % 2].rearrange("p j c h q -> p (j c h q)"),
                        identb[:]).then_inc(s["turned"], 1)

        def turn_dve(e, a, u, slot, b):
            s = a.sem
            e.wait_ge(s["turned"], a.since["turned"] + u + 1)
            wait(e, s["shifted"][(slot + 2) % UNITS], a.since["shifted"] + (64 * (b if slot < 2 else b + 1)))
            e.tensor_copy(negT[:, slot % 2, :], misc_bf[0:8 * QT, 0:P]).then_inc(s["rows"], 1)

        def shift_sp(e, a, u, slot):
            s = a.sem
            e.wait_ge(s["rows"], a.since["rows"] + u + 1)
            for j in range(2):
                for c in range(SHIFT):
                    r = (2 * j + c) * 2 * QT
                    e.dma_start(stk[64 * j + ROWS + c:64 * j + ROWS + c + 1, slot, 0].rearrange("o h n -> o (h n)"),
                                negT[r:r + 2 * QT, slot % 2, :]).then_inc(s["shifted"][slot], 16)

        def scores_pe(e, a, u, slot, b, kt):
            s = a.sem
            if kt == 0:
                e.wait_ge(s["shifted"][slot], a.since["shifted"] + 64 * (b + 1))
            q0 = a.first_query(kt)
            n = S - q0
            for j in range(2):
                wait(e, s["probs"], a.since["probs"] + 2 * a.kt * u + 2 * kt + j - 1)
                for pp in range(2):
                    o = bank_st[j][0:a.kp, pp, 0:n]
                    mm = e.matmul(o, stk[:, slot, 1 + j, pp, kt * P:kt * P + a.kp], stk[:, slot, 0, pp, q0:S], start=True, stop=not a.causal)
                    if a.causal:
                        mm = e.matmul(o[:, 0:P], identb[:], mask_kq[:], start=False, stop=True)
                mm.then_inc(s["scores"], 1)
            if kt == a.kt - 1:
                e.drain().then_inc(s["unit_scores"], 1)

        def exp_act(e, a, u, kt):
            s = a.sem
            n = S - a.first_query(kt)
            for j in range(2):
                e.wait_ge(s["scores"], a.since["scores"] + 2 * a.kt * u + 2 * kt + j + 1)
                if j == 0:
                    wait(e, s["pv"], a.since["pv"] + a.kt * u + kt - 1)
                half = probs[:, (kt if a.kt > 1 else 0) % 2] if a.kt > 1 else None
                dst = half[0:a.kp, 2 * j:2 * j + 2, 0:n]
                e.activation(dst, bank_st[j][0:a.kp, :, 0:n], ACT.Exp, scale=1 / math.sqrt(HD)).then_inc(s["probs"], 1)

        def exp_act_x(e, a, u, slot):
            s = a.sem
            for j in range(2):
                e.wait_ge(s["scores"], a.since["scores"] + 2 * u + j + 1)
                if j == 0:
                    wait(e, s["pv"], a.since["pv"] + u - 1)
                e.activation(probs[0:SC, slot % 2, 2 * j:2 * j + 2, :], bank_st[j][0:SC], ACT.Exp,
                             scale=1 / math.sqrt(HD)).then_inc(s["probs"], 1)

        def pv_pe(e, a, u, slot, kt):
            s = a.sem
            if kt == 0:
                e.wait_ge(s["values"], a.since["values"] + u + 1)
                e.wait_ge(s["pv_out"], a.since["pv_out"] + u) if not isinstance(u, int) or u > 0 else None
            e.wait_ge(s["probs"], a.since["probs"] + 2 * a.kt * u + 2 * kt + 2)
            q0 = a.first_query(kt)
            half = (kt if a.kt > 1 else slot) % 2
            for h in range(HG):
                mm = e.matmul(bank_pv[VW * h:VW * (h + 1), q0:S], vsl[0:a.kp, slot, kt, h, :],
                              probs[0:a.kp, half, h, 0:S - q0], start=(kt == 0), stop=(kt == a.kt - 1),
                              skip_group_check=True)
            mm.then_inc(s["pv"], 1)

        def pv_out_act(e, a, u):
            s = a.sem
            e.wait_ge(s["pv"], a.since["pv"] + a.kt * (u + 1))
            wait(e, s["out_turned"], a.since["out_turned"] + u)
            e.copy(oT[:], bank_pv[:]).then_inc(s["pv_out"], 1)

        def finish_pe(e, a, u):
            s = a.sem
            e.wait_ge(s["pv_out"], a.since["pv_out"] + u + 1)
            wait(e, s["normed"], a.since["normed"] + u)
            for j in range(QT):
                i = e.transpose(bank_misc[:, j * P:(j + 1) * P], oT[:, j * P:(j + 1) * P], ident[:])
            i.then_inc(s["out_turned"], 1)

        def finish_dve(e, a, u, hg, b):
            s = a.sem
            e.wait_ge(s["out_turned"], a.since["out_turned"] + u + 1)
            src = bank_misc[:].rearrange("p (q h c) -> p q h c", q=QT, h=HG)
            e.reciprocal(rec[:], src[:, :, :, HD]).then_inc(s["reciprocal"], 1)
            e.wait_ge(s["reciprocal"], a.since["reciprocal"] + u + 1)
            if hg == 0:
                wait(e, s["merged"], a.since["merged"] + b)
            e.tensor_tensor(otok[:, :, hg * HG * HD:(hg + 1) * HG * HD].rearrange("p q (h c) -> p q h c", h=HG),
                            src[:, :, :, 0:HD], rec[:].unsqueeze(3).to_broadcast([P, QT, HG, HD]),
                            ALU.mult).then_inc(s["normed"], 1)

        def merge_pe(e, a, b):
            s = a.sem
            e.wait_ge(s["normed"], a.since["normed"] + UNITS * (b + 1))
            for j in range(QT):
                i = e.transpose(bank_misc[:, j * P:(j + 1) * P], otok[:, j, :], ident[:])
            i.then_inc(s["merged"], 1)

        def merge_act(e, a, b):
            s = a.sem
            e.wait_ge(s["merged"], a.since["merged"] + b + 1)
            wait(e, s["proj"], a.since["proj"] + b)
            e.copy(okT[:], bank_misc[:]).then_inc(s["merged_out"], 1)

        def proj_pe(e, a, b):
            s, w = a.sem, wts[a.name]
            e.wait_ge(s["merged_out"], a.since["merged_out"] + b + 1)
            for j in range(QT):
                o = bank_misc[:, j * D:(j + 1) * D]
                e.matmul(o, okT[:, j * P:(j + 1) * P], w["wo"][:], start=True, stop=False)
                i = e.matmul(o, ones_row[:], w["bo"][:], start=False, stop=True)
            i.then_inc(s["proj"], 1)

        def proj_dve(e, a, b):
            s = a.sem
            e.wait_ge(s["proj"], a.since["proj"] + b + 1)
            xb = x_tile(4 * b, QT)
            e.tensor_tensor(xb, xb, bank_misc[:].rearrange("p (q d) -> p q d", q=QT), ALU.add).then_inc(s["x_new"], 1)

        def step_pe(e, a, u, hg, b, ahead, first=False):
            for c in range(a.kt):
                scores_pe(e, a, u, hg, b, c)
                if c == 0 and ahead > 0:
                    if a.sem is not None:
                        turn_pe(e, a, u + 1, (hg + 1) % UNITS)
                if c == min(1, a.kt - 1) and not first:
                    wait_misc_pe_turn(e, a, u + 1, ahead)
                    finish_pe(e, a, u - 1)
                if ahead > 1:
                    max_pe(e, a, u + 2, (hg + 2) % UNITS, b + (hg + 2) // UNITS, a.share(c))
                if c > 0:
                    pv_pe(e, a, u, hg, c - 1)
                if hg == 0 and not first:
                    if c == min(2, a.kt - 1):
                        wait_misc_pe_norm(e, a, u - 1)
                        merge_pe(e, a, b - 1)
                    if c == a.kt - 1:
                        proj_pe(e, a, b - 1)
            pv_pe(e, a, u, hg, a.kt - 1)

        def wait_misc_pe_turn(e, a, u, ahead):
            if ahead > 0:
                e.wait_ge(a.sem["rows"], a.since["rows"] + u + 1)

        def wait_misc_pe_norm(e, a, u):
            e.wait_ge(a.sem["normed"], a.since["normed"] + u + 1)

        def step_dve(e, a, u, hg, b, ahead, first=False):
            for c in range(a.kt):
                if c == 0 and ahead > 0:
                    turn_dve(e, a, u + 1, (hg + 1) % UNITS, b + (hg + 1) // UNITS)
                if c == min(1, a.kt - 1) and not first:
                    finish_dve(e, a, u - 1, (hg - 1) % UNITS, b - 1 if hg == 0 else b)
                if ahead > 1:
                    max_dve(e, a, u + 2, (hg + 2) % UNITS, a.share(c))
                if hg == 0 and not first and c == a.kt - 1:
                    proj_dve(e, a, b - 1)
            if ahead > 1:
                negate_dve(e, a, u + 2, (hg + 2) % UNITS)

        def step_act(e, a, u, hg, b, first=False):
            for c in range(a.kt):
                if a.kt > 1:
                    exp_act(e, a, u, c)
                else:
                    exp_act_x(e, a, u, hg)
                if c == 0 and not first:
                    pv_out_act(e, a, u - 1)
                if hg == 0 and not first and c == min(2, a.kt - 1):
                    merge_act(e, a, b - 1)

        def step_sp(e, a, u, hg, b, ahead):
            if not isinstance(u, int):
                pass
            if ahead > 0:
                shift_sp(e, a, u + 1, (hg + 1) % UNITS)

        def steps(e, a, one):
            one(e, a, 0, 0, 0, 2, True)
            with e.Fori(0, NB - 1) as b:
                for hg in (1, 2, 3, 4):
                    one(e, a, UNITS * b + hg, hg % UNITS, b + hg // UNITS, 2, False)
            for u in range(UNITS * (NB - 1) + 1, UNITS * NB):
                one(e, a, u, u % UNITS, NB - 1, min(2, UNITS * NB - 1 - u), False)

        def attention_pe(e, a):
            for u in range(2):
                max_pe(e, a, u, u, 0, range(len(a.items)))
            turn_pe(e, a, 0, 0)
            e.wait_ge(a.sem["rows"], a.since["rows"] + 1)
            steps(e, a, lambda e, a, u, hg, b, ahead, first: step_pe(e, a, u, hg, b, ahead, first))
            last = UNITS * NB - 1
            finish_pe(e, a, last)
            e.wait_ge(a.sem["normed"], a.since["normed"] + last + 1)
            merge_pe(e, a, NB - 1)
            proj_pe(e, a, NB - 1)

        def attention_dve(e, a):
            for u in range(2):
                max_dve(e, a, u, u, range(len(a.items)))
                negate_dve(e, a, u, u)
            turn_dve(e, a, 0, 0, 0)
            steps(e, a, lambda e, a, u, hg, b, ahead, first: step_dve(e, a, u, hg, b, ahead, first))
            finish_dve(e, a, UNITS * NB - 1, UNITS - 1, NB - 1)
            proj_dve(e, a, NB - 1)

        def attention_act(e, a):
            steps(e, a, lambda e, a, u, hg, b, ahead, first: step_act(e, a, u, hg, b, first))
            pv_out_act(e, a, UNITS * NB - 1)
            merge_act(e, a, NB - 1)

        def attention_pool(e, a):
            for u in range(UNITS):
                values_pool(e, a, u, u, 0)
            with e.Fori(1, NB) as b:
                for hg in range(UNITS):
                    values_pool(e, a, UNITS * b + hg, hg, b)

        def attention_sp(e, a):
            s = a.sem
            e.wait_ge(s_filled, 16 * sum(len(fills_of(o)) for o in ([a] if a is a_self0 else atts)))
            e.wait_ge(s["stacked_q"], a.since["stacked_q"] + 16 * TERMS * NB)
            e.wait_ge(s["stacked_k"], a.since["stacked_k"] + (16 * TERMS * (1 if a is a_cross else NB)))
            for u in range(UNITS):
                load_unit(e, a, u, u, 0)
            shift_sp(e, a, 0, 0)
            shift_sp(e, a, 1, 1)
            if a is a_self0:
                later_sp(e)
            with e.Fori(1, NB) as b:
                for hg in range(UNITS):
                    u = UNITS * b + hg
                    load_unit(e, a, u, hg, b, free=u - 3)
                    shift_sp(e, a, u - 2, (hg + 2) % UNITS)
            for u in range(UNITS * NB - 2, UNITS * NB):
                shift_sp(e, a, u, u % UNITS)

        def roped(z):
            return probs[:, 1, z]

        def staging_pe(e, a):
            if a is a_cross:
                w = wts["X0"]
                s = a.sem
                e.matmul(bank_max[1][:, 0:NB * SC], w["wk"][:], ctxT[:], start=True, stop=True).then_inc(s["k_proj"], 1)
                for b in range(NB):
                    o = bank_pv[0:SC, b * D:(b + 1) * D]
                    e.matmul(o, ctxT[:, b * SC:(b + 1) * SC], w["wv"][:], start=True, stop=False)
                    i = e.matmul(o, ones_row[:, 0:SC], w["bv"][:], start=False, stop=True)
                i.then_inc(s["v_proj"], 1)
            with e.Fori(0, NB) as b:
                stage_pe(e, a, b)

        def staging_act(e, a):
            w, s = wts[a.name], a.sem
            if a is a_cross:
                e.wait_ge(s["k_proj"], a.since["k_proj"] + 1)
                e.activation(parts[:, 1, 0, 0:NB * SC], bank_max[1][:, 0:NB * SC], ACT.Identity, bias=w["bk"][:])\
                    .then_inc(s["part1"], 1)
                e.wait_ge(s["rest"], a.since["rest"] + 1)
                e.copy(parts[:, 1, 1, 0:NB * SC], rest[:, 1, 0:NB * SC]).then_inc(s["part2"], 1)
            with e.Fori(0, NB) as b:
                norm_act(e, a.ln, b, bank_misc)
                if a is a_cross:
                    e.wait_ge(s["q_proj"], a.since["q_proj"] + b + 1)
                    e.wait_ge(s["stacked_q"], a.since["stacked_q"] + 16 * TERMS * b)
                    e.activation(parts[:, 0, 0, :], bank_max[0][:], ACT.Identity, bias=w["bq"][:]).then_inc(s["part1"], 1)
                    e.wait_ge(s["rest"], a.since["rest"] + b + 2)
                    e.copy(parts[:, 0, 1, :], rest[:, 0, :]).then_inc(s["part2"], 1)
                else:
                    for z in range(2):
                        e.wait_ge(s["stacked_k" if z else "stacked_q"], a.since["stacked_k" if z else "stacked_q"] + 16 * TERMS * b)
                        if a.rope:
                            e.wait_ge(s["roped"], a.since["roped"] + 2 * b + z + 1)
                            e.copy(parts[:, z, 0, :], roped(z)).then_inc(s["part1"], 1)
                            continue
                        e.wait_ge(s["k_proj" if z else "q_proj"], a.since["k_proj" if z else "q_proj"] + b + 1)
                        e.activation(parts[:, z, 0, :], bank_max[z][:], ACT.Identity, bias=w["bk" if z else "bq"][:])\
                            .then_inc(s["part1"], 1)
                    for z in range(2):
                        e.wait_ge(s["rest"], a.since["rest"] + 2 * b + z + 1)
                        e.copy(parts[:, z, 1, :], rest[:, z, :]).then_inc(s["part2"], 1)

        def staging_dve(e, a):
            w, s = wts[a.name], a.sem
            if a is a_cross:
                e.wait_ge(s["part1"], a.since["part1"] + 1)
                e.scalar_tensor_tensor(rest[:, 1, 0:NB * SC], bank_max[1][:, 0:NB * SC], w["bk"][:],
                                       parts[:, 1, 0, 0:NB * SC], ALU.add, ALU.subtract).then_inc(s["rest"], 1)
                e.wait_ge(s["v_proj"], a.since["v_proj"] + 1)
                e.tensor_copy(v9[0:SC, 0:NB, :, 0:HD], bank_pv[0:SC].rearrange("p (b h d) -> p b h d", b=NB, h=NH))\
                    .then_inc(s["v_done"], 1)
            with e.Fori(0, NB) as b:
                norm_dve(e, a.ln, b)
                for z in range(2 if a.rope else 0):
                    e.wait_ge(s["k_proj" if z else "q_proj"], a.since["k_proj" if z else "q_proj"] + (b + 1 if z else 2 * b + 2))
                    e.wait_ge(s["roped"], a.since["roped"] + 2 * b)
                    e.scalar_tensor_tensor(probs[:, 0, z], bank_max[z][:], w["bk" if z else "bq"][:], cos_sin[:, 0],
                                           ALU.add, ALU.mult)
                    e.scalar_tensor_tensor(probs[:, 0, 2 + z], bank_st[z][:, 0], bsw[z][:], cos_sin[:, 1],
                                           ALU.add, ALU.mult).then_inc(s["cos_sin"], 1)
                for z in range(1 if a is a_cross else 2):
                    n0 = b + 1 if a is a_cross else 2 * b + z
                    e.wait_ge(s["part1"], a.since["part1"] + n0 + 1)
                    e.wait_ge(s["part3"], a.since["part3"] + (b + 1 if a is a_cross else 2 * b))
                    if a.rope:
                        e.tensor_tensor(rest[:, z, :], roped(z), parts[:, z, 0, :], ALU.subtract).then_inc(s["rest"], 1)
                        continue
                    e.scalar_tensor_tensor(rest[:, z, :], bank_max[z][:], w["bk" if z else "bq"][:], parts[:, z, 0, :],
                                           ALU.add, ALU.subtract).then_inc(s["rest"], 1)
                if a is not a_cross:
                    e.wait_ge(s["v_proj"], a.since["v_proj"] + b + 1)
                    e.tensor_copy(v9[:, bass.ds(4 * b, QT), :, 0:HD],
                                  bank_pv[:].rearrange("p (q h d) -> p q h d", q=QT, h=NH)).then_inc(s["v_done"], 1)

        def staging_pool(e, a):
            s = a.sem
            if a is a_self1 and "M0" in layers:
                e.memset(v9[:, :, :, HD:HD + 1], 1.0).then_inc(s_ones, 1)
                e.wait_ge(s_ones, 1)
            if a is a_cross:
                e.wait_ge(s["part2"], a.since["part2"] + 1)
                e.tensor_tensor(parts[:, 1, 2, 0:NB * SC], rest[:, 1, 0:NB * SC], parts[:, 1, 1, 0:NB * SC],
                                ALU.subtract).then_inc(s["part3"], 1)
            with e.Fori(0, NB) as b:
                norm_pool(e, a.ln, b)
                for z in range(2 if a.rope else 0):
                    e.wait_ge(s["cos_sin"], a.since["cos_sin"] + 2 * b + z + 1)
                    e.wait_ge(s["rest"], a.since["rest"] + 2 * b)
                    e.tensor_tensor(roped(z), probs[:, 0, z], probs[:, 0, 2 + z], ALU.add).then_inc(s["roped"], 1)
                for z in range(1 if a is a_cross else 2):
                    e.wait_ge(s["part2"], a.since["part2"] + (b + 1 if a is a_cross else 2 * b + z) + 1)
                    e.wait_ge(s["stacked_k" if z else "stacked_q"], a.since["stacked_k" if z else "stacked_q"] + 16 * TERMS * b)
                    e.tensor_tensor(parts[:, z, 2, :], rest[:, z, :], parts[:, z, 1, :], ALU.subtract)\
                        .then_inc(s["part3"], 1)
            e.wait_ge(s["v_done"], a.since["v_done"] + (1 if a is a_cross else NB))

        def staging_sp(e, a):
            s = a.sem
            if a is a_cross:
                e.wait_ge(s["part3"], a.since["part3"] + 1)
                for t in range(TERMS):
                    e.dma_start(scr_kx[t * HD:(t + 1) * HD].rearrange("d h b n -> h d (b n)"),
                                parts[:, 1, K_PARTS[t], 0:NB * SC]).then_inc(s["stacked_k"], 16)
            with e.Fori(0, NB) as b:
                if a is a_cross:
                    e.wait_ge(s["part3"], a.since["part3"] + b + 2)
                    for t in range(TERMS):
                        e.dma_start(scr[a.name][bass.ds(b, 1), t * HD:(t + 1) * HD, 0].rearrange("o d h n -> h (o d) n"),
                                    parts[:, 0, Q_PARTS[t], :]).then_inc(s["stacked_q"], 16)
                else:
                    for z in range(2):
                        stack_sp(e, a, z, b, 2, z)

        m = {n: sem(f"M0_{n}") for n in """gate_proj logits top top_at top_f picked routed kept sum_in
            rank count count2 floor cum base place place_of place_f place_u tile_le tile_f tile_e
            diff expo plus recip gates zeroed scattered xT xT_out hidden silu act actT actT_out y_in y_out
            weighed""".split()}
        m |= {n: [sem(f"M0_{n}{i}") for i in range(2)] for n in ("tile_in", "stored")}
        m["got"] = [sem(f"M0_got{i}") for i in range(NB)]

        def moe_dve(e, ln):
            with e.Fori(0, NB) as b:
                norm_dve(e, ln, b)
                e.wait_ge(m["gate_proj"], b + 1)
                e.tensor_copy(lg[:], bank_max[0][:, 0:QT * NE].rearrange("p (q n) -> p q n", q=QT))\
                    .then_inc(m["logits"], 1)
                e.wait_ge(m["logits"], FREE + b + 1)
                take_wait(e)
                for j in range(QT):
                    e.max(top[:, j, :], lg[:, j, :]).then_inc(m["top"], 1)
                e.wait_ge(m["top"], QT * (b + 1))
                take_wait(e)
                for j in range(QT):
                    e.max_index(top_at[:, j, :], top[:, j, :], lg[:, j, :]).then_inc(m["top_at"], 1)
                e.tensor_copy(top_v[:, bass.ds(4 * b, QT), :], top[:, :, 0:2])
                e.wait_ge(m["top_at"], QT * (b + 1))
                e.tensor_copy(top_f[:], top_at[:, :, 0:2]).then_inc(m["top_f"], 1)
                e.wait_ge(m["top_f"], b + 1)
                for k in range(2):
                    e.tensor_tensor(picked[:, k, bass.ds(4 * b, QT), :],
                                    iota_e[:].unsqueeze(1).to_broadcast([P, QT, NE]),
                                    top_f[:, :, k].unsqueeze(2).to_broadcast([P, QT, NE]),
                                    ALU.is_equal).then_inc(m["picked"], 1)
                e.wait_ge(m["picked"], 2 * (b + 1))
                e.tensor_tensor(routed[:, bass.ds(4 * b, QT), :], picked[:, 0, bass.ds(4 * b, QT), :],
                                picked[:, 1, bass.ds(4 * b, QT), :], ALU.add).then_inc(m["routed"], 1)
            e.wait_ge(m["routed"], NB)
            with nc.allow_low_precision("sums of up to 16 ones"):
                e.tensor_reduce(routed_sum[:], routed[:].rearrange("p t n -> p n t"), AX.X, ALU.add)\
                    .then_inc(m["sum_in"], 1)
            e.tensor_tensor(gate_t[:, 0], top_v[:, :, 1], top_v[:, :, 0], ALU.subtract).then_inc(m["diff"], 1)
            e.wait_ge(m["count"], 1)
            e.tensor_scalar(small["count"][:], bank_max[1][:, 0:NE], P - 1.0, 1.0 / P, ALU.add, ALU.mult)\
                .then_inc(m["count2"], 1)
            e.wait_ge(m["count2"], 1)
            e.tensor_scalar(small["tiles"][:], small["count"][:], -0.5 + 0.5 / P, ROUND, ALU.add, ALU.add)\
                .then_inc(m["floor"], 1)
            e.wait_ge(m["floor"], 1)
            e.tensor_scalar(small["count"][:], small["tiles"][:], -ROUND, None, ALU.add).then_inc(m["floor"], 1)
            e.wait_ge(m["floor"], 2)
            e.tensor_tensor_scan(small["cum"][:], onesf[:, 0:NE], small["count"][:], 0.0, ALU.mult, ALU.add)\
                .then_inc(m["cum"], 1)
            e.wait_ge(m["cum"], 1)
            e.tensor_tensor(small["base"][:], small["cum"][:], small["count"][:], ALU.subtract).then_inc(m["base"], 1)
            e.tensor_tensor(tile_le[:], small["cum"][:].unsqueeze(1).to_broadcast([P, MT, NE]),
                            iota_t[:].unsqueeze(2).to_broadcast([P, MT, NE]), ALU.is_le).then_inc(m["tile_le"], 1)
            e.wait_ge(m["rank"], 1)
            e.wait_ge(m["base"], 1)
            e.scalar_tensor_tensor(place[:].rearrange("p t n -> p t n"), small["base"][:].unsqueeze(1).to_broadcast([P, NT, NE]),
                                   float(P), bank_max[0][:, 0:NT * NE].rearrange("p (t n) -> p t n", n=NE),
                                   ALU.mult, ALU.add).then_inc(m["place"], 1)
            e.wait_ge(m["place"], 1)
            for k in range(2):
                e.tensor_tensor(place_of[:, k], picked[:, k], place[:], ALU.mult).then_inc(m["place_of"], 1)
            e.wait_ge(m["place_of"], 2)
            e.tensor_reduce(place_f[:], place_of[:], AX.X, ALU.add).then_inc(m["place_f"], 1)
            e.wait_ge(m["place_f"], 1)
            e.tensor_copy(place_u[:], place_f[:]).then_inc(m["place_u"], 1)
            e.wait_ge(m["tile_le"], 1)
            e.tensor_reduce(tile_f[:], tile_le[:], AX.X, ALU.add).then_inc(m["tile_f"], 1)
            e.wait_ge(m["tile_f"], 1)
            e.tensor_scalar(tile_e[:], tile_f[:], NE - 1.0, None, ALU.min).then_inc(m["tile_e"], 1)
            e.wait_ge(m["expo"], 1)
            e.tensor_scalar(gate[:, 1], gate_t[:, 1], 1.0, None, ALU.add).then_inc(m["plus"], 1)
            e.wait_ge(m["plus"], 1)
            e.reciprocal(gate[:, 0], gate[:, 1]).then_inc(m["recip"], 1)
            e.wait_ge(m["recip"], 1)
            e.tensor_tensor(gate[:, 1], gate[:, 0], gate_t[:, 1], ALU.mult).then_inc(m["gates"], 1)

            if "F1" in layers:
                weights_dve(e)

            def turned(t, k):
                e.wait_ge(m["xT"], t + 1)
                e.tensor_copy(x_inT[:, k], bank_misc[:, 0:P]).then_inc(m["xT_out"], 1)

            def product(t, k):
                e.wait_ge(m["silu"], t + 1)
                e.tensor_tensor(act[:], hid[k][0], silu[:, k], ALU.mult).then_inc(m["act"], 1)
                e.wait_ge(m["actT"], t + 1)
                e.tensor_copy(actT[:], t_bank).then_inc(m["actT_out"], 1)

            for t in range(2):
                turned(t, t)
            with e.Fori(0, MT // 2 - 1) as i:
                for k in range(2):
                    product(2 * i + k, k)
                    turned(2 * i + k + 2, k)
            for k in range(2):
                product(MT - 2 + k, k)
            e.wait_ge(m["gates"], 1)
            for b in range(NB):
                e.wait_ge(m["got"][b], 16 * 2 * QT)
                for t in range(QT * b, QT * (b + 1)):
                    e.scalar_tensor_tensor(xs[:, t, :], got[:, t, 0], gate[:, 0, t:t + 1], xs[:, t, :],
                                           ALU.mult, ALU.add).then_inc(m["weighed"], 1)
                for t in range(QT * b, QT * (b + 1)):
                    e.wait_ge(m["weighed"], QT * b + t + 1)
                    o = e.scalar_tensor_tensor(xs[:, t, :], got[:, t, 1], gate[:, 1, t:t + 1], xs[:, t, :],
                                               ALU.mult, ALU.add)
                    o.then_inc(m["weighed"], 1)
                e.wait_ge(m["weighed"], 2 * QT * (b + 1))
                e.sem_inc(x_new[ln][0], 1)

        act = oT
        actT = okT
        silu = probs[:, 0, 0:2]
        y_sb = probs[:, 0, 2:4, 0:D]
        x_in = probs[:, 1, 0:2, 0:D]
        x_inT = probs[:, 1, 2:4, 0:P]
        got = probs[:].rearrange("p a h s -> p (a h s)").rearrange("p (t k d) -> p t k d", t=NT, k=2)
        hid = [(bank_max[0][:], bank_max[1][:]), (bank_st[1][:, 0], bank_st[1][:, 1])]
        y_bank = bank_st[0][:, 0]
        t_bank = bank_st[0][:, 1]

        def moe_pool(e, ln):
            with e.Fori(0, NB) as b:
                norm_pool(e, ln, b)
                e.wait_ge(s_xn, 4 * ln + b + 1)
                e.tensor_copy(xn_all[:, bass.ds(4 * b, QT), :], xn[:]).then_inc(m["kept"], 1)
            e.wait_ge(m["kept"], NB)
            e.wait_ge(m["place_u"], 1)
            e.wait_ge(s_zero, 16)
            for t in range(NT):
                for k in range(2):
                    e.indirect_dma_start(scr_xn, bass.IndirectOffsetOnAxis(ap=place_u[:, k, t:t + 1], axis=0),
                                         xn_all[:, t, :], None).then_inc(m["scattered"], 16)
            for k in range(2):
                e.wait_ge(m["stored"][k], FREE + 16 * (MT // 2))
            for t in range(NT):
                for k in range(2):
                    e.indirect_dma_start(got[:, t, k], None, scr_y,
                                         bass.IndirectOffsetOnAxis(ap=place_u[:, k, t:t + 1], axis=0))\
                        .then_inc(m["got"][t // QT], 16)

        def moe_pe(e, ln):
            with e.Fori(0, NB) as b:
                norm_pe(e, ln, b, bank_misc)
                e.wait_ge(s_xnT_sb, FREE + 4 * ln + b + 1)
                e.wait_ge(m["logits"], FREE + b)
                for j in range(QT):
                    o = bank_max[0][:, j * NE:(j + 1) * NE]
                    e.matmul(o, xnT[:, j * P:(j + 1) * P], gate_w[:], start=True, stop=False)
                    i = e.matmul(o, ones_row[:], gate_b[:], start=False, stop=True)
                i.then_inc(m["gate_proj"], 1)
                e.drain().then_inc(s_xnT_used, 1)
            e.wait_ge(m["routed"], NB)
            r = routed[:].rearrange("p t n -> p (t n)")
            o = bank_max[0]
            e.matmul(o[:, 0:NT * NE], before[:], r, start=True, stop=False, skip_group_check=True)
            for k in range(1, NT):
                i = e.matmul(o[:, k * NE:NT * NE], onesb[:], r[:, 0:(NT - k) * NE], start=False, stop=(k == NT - 1),
                             skip_group_check=True)
            i.then_inc(m["rank"], 1)
            e.wait_ge(m["sum_in"], 1)
            e.matmul(bank_max[1][:, 0:NE], onesb[:], routed_sum[:], start=True, stop=True).then_inc(m["count"], 1)
            e.wait_ge(m["tile_e"], 1)
            e.wait_ge(m["place"], 1)
            if "F1" in layers:
                weights_pe(e)
            e.wait_ge(s_b1p, 16 * 3 * len(part_srcs))

            def expert(t):
                return e.value_load(tile_e[0:1, bass.ds(t, 1)], min_val=0, max_val=NE - 1)

            def turn(k, loaded):
                e.wait_ge(m["tile_in"][k], loaded)
                e.transpose(bank_misc[:, 0:P], x_in[:, k], ident[:]).then_inc(m["xT"], 1)

            def hidden(t, k, ex, z):
                if z == 0:
                    e.wait_ge(m["xT_out"], t + 1)
                o = hid[k][z]
                e.matmul(o, x_inT[:, k], w1[:, bass.ds(ex, 1), z * FF:(z + 1) * FF].rearrange("p o n -> p (o n)"),
                         start=True, stop=False)
                mm = e.matmul(o, ones3[:], b1p[:, bass.ds(ex * (2 * FF) + z * FF, FF)], start=False, stop=True)
                if z == 1:
                    mm.then_inc(m["hidden"], 1)

            def turn_act(t):
                e.wait_ge(m["act"], t + 1)
                for c in range(FC):
                    mm = e.transpose(t_bank[:, c * P:(c + 1) * P], act[:, c * P:(c + 1) * P], ident[:])
                mm.then_inc(m["actT"], 1)

            def output(t, ex):
                e.wait_ge(m["actT_out"], t + 1)
                e.wait_ge(m["y_out"], FREE + t)
                for c in range(FC):
                    e.matmul(y_bank[:, 0:D], actT[:, c * P:(c + 1) * P],
                             w2[:, bass.ds(ex, 1), c, :].rearrange("p o n -> p (o n)"), start=(c == 0), stop=False)
                e.matmul(y_bank[:, 0:D], ones3[:], b2p[:, bass.ds(ex * D, D)], start=False, stop=True)\
                    .then_inc(m["y_in"], 1)

            turn(0, 16)
            e.wait_ge(m["xT_out"], 1)
            turn(1, 16)
            first = expert(0)
            for z in range(2):
                hidden(0, 0, first, z)
            with e.Fori(0, MT // 2 - 1) as i:
                ex = [expert(2 * i + k) for k in range(3)]
                for k in range(2):
                    t = 2 * i + k
                    hidden(t + 1, 1 - k, ex[k + 1], 0)
                    turn_act(t)
                    turn(k, 16 * (i + 2))
                    hidden(t + 1, 1 - k, ex[k + 1], 1)
                    output(t, ex[k])
            last = [expert(MT - 2 + k) for k in range(2)]
            hidden(MT - 1, 1, last[1], 0)
            turn_act(MT - 2)
            hidden(MT - 1, 1, last[1], 1)
            output(MT - 2, last[0])
            turn_act(MT - 1)
            output(MT - 1, last[1])

        def moe_act(e, ln):
            with e.Fori(0, NB) as b:
                norm_act(e, ln, b, bank_misc)
            e.wait_ge(m["diff"], 1)
            e.activation(gate_t[:, 1], gate_t[:, 0], ACT.Exp).then_inc(m["expo"], 1)

            def gate_part(t, k):
                e.wait_ge(m["hidden"], t + 1)
                e.activation(silu[:, k], hid[k][1], ACT.Silu).then_inc(m["silu"], 1)

            def keep(t, k, stored):
                e.wait_ge(m["y_in"], t + 1)
                e.wait_ge(m["stored"][k], FREE + stored)
                e.activation(y_sb[:, k], y_bank[:, 0:D], ACT.Copy).then_inc(m["y_out"], 1)

            gate_part(0, 0)
            with e.Fori(0, MT // 2 - 1) as i:
                for k in range(2):
                    gate_part(2 * i + k + 1, 1 - k)
                    keep(2 * i + k, k, 16 * i)
            gate_part(MT - 1, 1)
            for k in range(2):
                keep(MT - 2 + k, k, 16 * (MT // 2 - 1))

        def moe_sp(e):
            e.wait_ge(m["scattered"], 16 * 2 * NT)
            for k in range(2):
                e.dma_start(x_in[:, k], scr_xn[k * P:(k + 1) * P, :]).then_inc(m["tile_in"][k], 16)
            with e.Fori(0, MT // 2 - 1) as i:
                for k in range(2):
                    e.wait_ge(m["xT"], 2 * i + k + 1)
                    e.dma_start(x_in[:, k], scr_xn[bass.ds((2 * i + k + 2) * P, P), :]).then_inc(m["tile_in"][k], 16)
                for k in range(2):
                    e.wait_ge(m["y_out"], FREE + 2 * i + k + 1)
                    e.dma_start(scr_y[bass.ds((2 * i + k) * P, P), :], y_sb[:, k]).then_inc(m["stored"][k], 16)
            for k in range(2):
                e.wait_ge(m["y_out"], FREE + MT - 1 + k)
                e.dma_start(scr_y[(MT - 2 + k) * P:(MT - 1 + k) * P, :], y_sb[:, k]).then_inc(m["stored"][k], 16)

        c = {n: sem(f"X1_{n}") for n in "k_proj k_out v_proj v_out q_proj q_out logits masked neg probs probsT probsT_out out recip".split()}
        x_qT = okT
        x_p = probs[:, 0, 0:QT, 0:SC]
        x_pT = oT

        def cross_pe(e, ln):
            e.matmul(bank_max[1][:, 0:NB * SC], xw["wk"][:], ctxT[:], start=True, stop=True).then_inc(c["k_proj"], 1)
            for b in range(NB):
                o = bank_pv[0:SC, b * D:(b + 1) * D]
                e.matmul(o, ctxT[:, b * SC:(b + 1) * SC], xw["wv"][:], start=True, stop=False)
                i = e.matmul(o, ones_row[:, 0:SC], x_bv[:], start=False, stop=True)
            i.then_inc(c["v_proj"], 1)
            e.wait_ge(c["k_out"], 1)
            e.wait_ge(c["v_out"], 1)
            with e.Fori(0, NB) as b:
                norm_pe(e, ln, b, bank_misc)
                e.wait_ge(s_xnT_sb, FREE + 4 * ln + b + 1)
                e.wait_ge(c["q_out"], FREE + b)
                e.matmul(bank_max[0][:], xw["wq"][:], xnT[:], start=True, stop=True).then_inc(c["q_proj"], 1)
                e.drain().then_inc(s_xnT_used, 1)
                e.wait_ge(c["q_out"], FREE + b + 1)
                e.wait_ge(c["masked"], FREE + b)
                for j in range(QT):
                    i = e.matmul(bank_max[1][:, j * SC:(j + 1) * SC], x_qT[:, j * P:(j + 1) * P],
                                 x_kT[:, bass.ds(b * SC, SC)], start=True, stop=True)
                i.then_inc(c["logits"], 1)
                e.wait_ge(c["probs"], FREE + QT * (b + 1))
                e.wait_ge(c["probsT_out"], FREE + b)
                for j in range(QT):
                    i = e.transpose(bank_st[0][0:SC, 0, j * P:(j + 1) * P], x_p[:, j], ident[:])
                i.then_inc(c["probsT"], 1)
                e.wait_ge(c["probsT_out"], FREE + b + 1)
                e.wait_ge(x_new[ln][0], x_new[ln][1] + b)
                for j in range(QT):
                    i = e.matmul(bank_st[1][:, 0, j * P:(j + 1) * P], x_pT[0:SC, j * P:(j + 1) * P],
                                 x_v[:, bass.ds(b, 1), :].rearrange("p o n -> p (o n)"), start=True, stop=True)
                i.then_inc(c["out"], 1)

        def cross_act(e, ln):
            e.wait_ge(c["k_proj"], 1)
            e.activation(x_kT[:], bank_max[1][:, 0:NB * SC], ACT.Identity, bias=xb_["bk"][:]).then_inc(c["k_out"], 1)
            with e.Fori(0, NB) as b:
                norm_act(e, ln, b, bank_misc)
                e.wait_ge(c["q_proj"], b + 1)
                e.wait_ge(c["logits"], FREE + b)
                e.activation(x_qT[:], bank_max[0][:], ACT.Identity, bias=xb_["bq"][:]).then_inc(c["q_out"], 1)
                e.wait_ge(c["neg"], b + 1)
                e.wait_ge(c["probsT"], FREE + b)
                e.wait_ge(c["recip"], FREE + b)
                for j in range(QT):
                    e.activation(x_p[:, j], x_lg[:, j], ACT.Exp, bias=x_neg[:, j:j + 1], accum_out=x_sum[:, j:j + 1])\
                        .then_inc(c["probs"], 1)
                e.wait_ge(c["probsT"], FREE + b + 1)
                e.wait_ge(c["out"], FREE + b)
                e.copy(x_pT[0:SC, :], bank_st[0][0:SC, 0]).then_inc(c["probsT_out"], 1)

        def cross_dve(e, ln):
            e.wait_ge(c["v_proj"], 1)
            e.tensor_copy(x_v[:], bank_pv[0:SC].rearrange("p (b d) -> p b d", b=NB)).then_inc(c["v_out"], 1)
            with e.Fori(0, NB) as b:
                norm_dve(e, ln, b)
                e.wait_ge(c["logits"], FREE + b + 1)
                e.wait_ge(c["probs"], FREE + QT * b)
                e.scalar_tensor_tensor(x_lg[:], bank_max[1][:, 0:QT * SC].rearrange("p (q k) -> p q k", q=QT),
                                       1 / math.sqrt(D), xmask[:], ALU.mult, ALU.add).then_inc(c["masked"], 1)
                e.wait_ge(c["masked"], FREE + b + 1)
                e.tensor_reduce(x_neg[:], x_lg[:], AX.X, ALU.max, negate=True).then_inc(c["neg"], 1)
                e.wait_ge(c["probs"], FREE + QT * (b + 1))
                e.reciprocal(x_rec[:], x_sum[:]).then_inc(c["recip"], 1)
                e.wait_ge(c["recip"], FREE + b + 1)
                e.wait_ge(c["out"], FREE + b + 1)
                for j in range(QT):
                    xj = x_tile(4 * b + j).rearrange("p o d -> p (o d)")
                    i = e.scalar_tensor_tensor(xj, bank_st[1][:, 0, j * P:(j + 1) * P], x_rec[:, j:j + 1], xj,
                                               ALU.mult, ALU.add)
                i.then_inc(x_new[ln][0], 1)

        f = {n: sem(f"F1_{n}") for n in """abs total mean inv q1 q2 q3 taps amax aclip arec scale back
            n1 n2 xT_out conv silu hmax hclip hrec hscale hback hm1 hm2 hq hT hT_out out added""".split()}

        def weights_pe(e):
            e.wait_ge(f["abs"], 2)
            e.matmul(bank_misc[:, 0:2], onesf[:], f_abs[:], start=True, stop=True).then_inc(f["total"], 1)
            e.wait_ge(f["mean"], 1)

        def weights_dve(e):
            w = (f_w1[:], f_w2[:].rearrange("p c d -> p (c d)"))
            for k in range(2):
                e.tensor_reduce(f_abs[:, k:k + 1], w[k], AX.X, ALU.add, apply_absolute_value=True).then_inc(f["abs"], 1)
            e.wait_ge(f["total"], 1)
            e.tensor_scalar(f_mean[:], bank_misc[:, 0:2], 1.0 / (D * FF), 1e-5, ALU.mult, ALU.max).then_inc(f["mean"], 1)
            e.wait_ge(f["mean"], 1)
            e.reciprocal(f_inv[:], f_mean[:]).then_inc(f["inv"], 1)
            e.wait_ge(f["inv"], 1)
            for k in range(2):
                e.tensor_scalar(w[k], w[k], f_inv[:, k:k + 1], ROUND, ALU.mult, ALU.add).then_inc(f["q1"], 1)
            e.wait_ge(f["q1"], 2)
            for k in range(2):
                e.tensor_scalar(w[k], w[k], -ROUND, 1.0, ALU.add, ALU.min).then_inc(f["q2"], 1)
            e.wait_ge(f["q2"], 2)
            e.tensor_scalar(w[0], w[0], -1.0, f_mean[:, 0:1], ALU.max, ALU.mult).then_inc(f["q3"], 1)
            e.tensor_scalar(f_w2q[:].rearrange("p c d -> p (c d)"), w[1], -1.0, None, ALU.max).then_inc(f["q3"], 1)
            e.wait_ge(f["q3"], 2)
            for k in range(3):
                e.tensor_tensor(f_w1c[:, k], f_taps[:, k], w[0], ALU.mult).then_inc(f["taps"], 1)

        def ffn_dve(e, ln):
            if "M0" not in layers:
                weights_dve(e)
            with e.Fori(0, NB) as b:
                norm_dve(e, ln, b)
                e.wait_ge(s_xn, 4 * ln + b + 1)
                e.tensor_reduce(f_amax[:], xn[:], AX.X, ALU.max, apply_absolute_value=True).then_inc(f["amax"], 1)
                e.wait_ge(f["amax"], b + 1)
                e.tensor_scalar(f_amax[:], f_amax[:], 1e-5, None, ALU.max).then_inc(f["aclip"], 1)
                e.wait_ge(f["aclip"], b + 1)
                e.reciprocal(f_scale[:], f_amax[:]).then_inc(f["arec"], 1)
                e.tensor_scalar(f_back[:], f_amax[:], 1.0 / 127.0, None, ALU.mult).then_inc(f["back"], 1)
                e.wait_ge(f["arec"], b + 1)
                e.tensor_scalar(f_scale[:], f_scale[:], 127.0, None, ALU.mult).then_inc(f["scale"], 1)
                e.wait_ge(f["scale"], b + 1)
                for j in range(QT):
                    i = e.tensor_scalar(xn[:, j], xn[:, j], f_scale[:, j:j + 1], ROUND, ALU.mult, ALU.add)
                i.then_inc(f["n1"], 1)
                e.wait_ge(f["n1"], b + 1)
                e.tensor_scalar(xn[:], xn[:], -ROUND, 127.0, ALU.add, ALU.min).then_inc(f["n2"], 1)
                e.wait_ge(f["n2"], b + 1)
                for j in range(QT):
                    i = e.tensor_scalar(xn[:, j], xn[:, j], -128.0, f_back[:, j:j + 1], ALU.max, ALU.mult)
                i.then_inc(s_xq, 1)
                for j in range(QT):
                    t, k = QT * b + j, j % 2
                    e.wait_ge(f["silu"], FREE + t + 1)
                    e.tensor_reduce(f_hmax[:, k:k + 1], f_h[:, k], AX.X, ALU.max, apply_absolute_value=True)\
                        .then_inc(f["hmax"], 1)
                    e.wait_ge(f["hmax"], t + 1)
                    e.tensor_scalar(f_hmax[:, k:k + 1], f_hmax[:, k:k + 1], 1e-5, None, ALU.max).then_inc(f["hclip"], 1)
                    e.wait_ge(f["hclip"], t + 1)
                    e.reciprocal(f_hscale[:, k:k + 1], f_hmax[:, k:k + 1]).then_inc(f["hrec"], 1)
                    e.tensor_scalar(f_hback[:, k:k + 1], f_hmax[:, k:k + 1], 1.0 / 127.0, f_mean[:, 1:2],
                                    ALU.mult, ALU.mult).then_inc(f["hback"], 1)
                    e.wait_ge(f["hrec"], t + 1)
                    e.tensor_scalar(f_hscale[:, k:k + 1], f_hscale[:, k:k + 1], 127.0, None, ALU.mult)\
                        .then_inc(f["hscale"], 1)
                    e.wait_ge(f["hscale"], t + 1)
                    e.tensor_scalar(f_hm[:, k], f_h[:, k], f_hscale[:, k:k + 1], ROUND, ALU.mult, ALU.add)\
                        .then_inc(f["hm1"], 1)
                    e.wait_ge(f["hm1"], t + 1)
                    e.tensor_scalar(f_hm[:, k], f_hm[:, k], ROUND + 127.0, ROUND - 128.0, ALU.min, ALU.max)\
                        .then_inc(f["hm2"], 1)
                    e.wait_ge(f["out"], t + 1)
                    xj = x_tile(4 * b + j).rearrange("p o d -> p (o d)")
                    i = e.scalar_tensor_tensor(xj, bank_st[1][:, 0, 0:D], f_hback[:, k:k + 1], xj, ALU.mult, ALU.add)
                    i.then_inc(f["added"], 1)
                e.wait_ge(f["added"], FREE + QT * (b + 1))
                e.sem_inc(x_new[ln][0], 1)

        def ffn_pe(e, ln):
            if "M0" not in layers:
                weights_pe(e)
            e.wait_ge(f["taps"], 3)
            e.wait_ge(s_b1p, 16 * 3 * len(part_srcs))
            with e.Fori(0, NB) as b:
                e.wait_ge(s_xq, b + 1)
                e.wait_ge(f["xT_out"], FREE + b)
                for j in range(QT):
                    i = e.transpose(bank_misc[:, j * P:(j + 1) * P], xn[:, j, :], ident[:])
                i.then_inc(s_xnT, 1)
                e.wait_ge(f["xT_out"], FREE + b + 1)
                for j in range(QT):
                    t, k = QT * b + j, j % 2
                    e.wait_ge(f["silu"], FREE + t)
                    for tap in range(3):
                        e.matmul(bank_max[0][:], f_xT[:, j * P + tap:(j + 1) * P + tap], f_w1c[:, tap],
                                 start=(tap == 0), stop=False)
                    e.matmul(bank_max[0][:], ones3[:], f_cb[:], start=False, stop=True).then_inc(f["conv"], 1)
                    e.wait_ge(f["hq"], t + 1)
                    e.wait_ge(f["hT_out"], FREE + t)
                    for cc in range(FC):
                        i = e.transpose(f_tb[:, cc * P:(cc + 1) * P], f_hq[:, k, cc * P:(cc + 1) * P], identb[:])
                    i.then_inc(f["hT"], 1)
                    e.wait_ge(f["hT_out"], FREE + t + 1)
                    e.wait_ge(f["added"], FREE + t)
                    for cc in range(FC):
                        i = e.matmul(bank_st[1][:, 0, 0:D], f_hT[:, k, cc * P:(cc + 1) * P], f_w2q[:, cc, :],
                                     start=(cc == 0), stop=(cc == FC - 1))
                    i.then_inc(f["out"], 1)

        f_tb = bank_pv[:].bitcast(BF16)

        def ffn_act(e, ln):
            with e.Fori(0, NB) as b:
                e.wait_ge(s_xnT, FREE + 4 * ln + b + 1)
                e.wait_ge(f["conv"], FREE + QT * b)
                e.copy(f_xT[:, 1:S + 1], bank_misc[:]).then_inc(f["xT_out"], 1)
                for j in range(QT):
                    t, k = QT * b + j, j % 2
                    e.wait_ge(f["conv"], FREE + t + 1)
                    e.activation(f_h[:, k], bank_max[0][:], ACT.Silu).then_inc(f["silu"], 1)
                    e.wait_ge(f["hm2"], t + 1)
                    e.activation(f_hq[:, k], f_hm[:, k], ACT.Copy, bias=-ROUND).then_inc(f["hq"], 1)
                    e.wait_ge(f["hT"], t + 1)
                    e.copy(f_hT[:, k], f_tb[:, 0:FF]).then_inc(f["hT_out"], 1)

        def ffn_pool(e, ln):
            with e.Fori(0, NB) as b:
                norm_pool(e, ln, b)

        part_srcs = []
        if "M0" in layers:
            part_srcs += [(d["M0_b1"], b1p, NE * 2 * FF), (d["M0_b2"], b2p, NE * D)]
        if "F1" in layers:
            part_srcs += [(d["F1_cb"], f_cb, FF)]
        at = [0]
        for _, _, n in part_srcs:
            at.append(at[-1] + n // P)

        def parts_pool(e):
            if not part_srcs:
                return
            e.wait_ge(s_pin, 16 * len(part_srcs))
            e.tensor_copy(bias_part[:, 0, 0:at[-1]], bias_in[:, 0:at[-1]]).then_inc(s_p, 1)
            e.wait_ge(s_p, 1)
            e.tensor_tensor(bias_in[:, 0:at[-1]], bias_in[:, 0:at[-1]], bias_part[:, 0, 0:at[-1]], ALU.subtract).then_inc(s_p, 1)
            e.wait_ge(s_p, 2)
            e.tensor_copy(bias_part[:, 1, 0:at[-1]], bias_in[:, 0:at[-1]]).then_inc(s_p, 1)
            e.wait_ge(s_p, 3)
            e.tensor_tensor(bias_in[:, 0:at[-1]], bias_in[:, 0:at[-1]], bias_part[:, 1, 0:at[-1]], ALU.subtract).then_inc(s_p, 1)
            e.wait_ge(s_p, 4)
            e.tensor_copy(bias_part[:, 2, 0:at[-1]], bias_in[:, 0:at[-1]]).then_inc(s_p, 1)

        def parts_in_sp(e):
            for (src, _, n), o in zip(part_srcs, at):
                e.dma_start(bias_in[:, o:o + n // P], src.rearrange("o (p c) -> (o p) c", p=P)).then_inc(s_pin, 16)

        def parts_out_sp(e):
            if not part_srcs:
                return
            e.wait_ge(s_p, 5)
            for (_, dst, n), o in zip(part_srcs, at):
                for i in range(3):
                    e.dma_start(dst[i:i + 1, :], bias_part[:, i, o:o + n // P]).then_inc(s_b1p, 16)

        loads, later = [], []
        for a in atts:
            (loads if a is a_self0 else later).extend([(wts[a.name][k][:], d[f"{a.name}_{k}"]) for k in wts[a.name]])
        if "A0" in layers:
            for i, k in enumerate("qk"):
                loads += [(wsw[i][:], d[f"A0_w{k}_swapped"]), (bsw[i][:], d[f"A0_b{k}_swapped"])]
            loads += [(cos_sin[:], d["cos_sin"])]
        if "X0" in layers or "X1" in layers:
            later += [(ctxT[:], d["ctxT"])]
        if "M0" in layers:
            later += [(gate_w[:], d["M0_gate_w"]), (gate_b[:], d["M0_gate_b"]),
                      (w1[:], d["M0_w1"].rearrange("e p n -> p e n")),
                      (w2[:].rearrange("p e c n -> p (e c) n"), d["M0_w2"].rearrange("e (c p) n -> p (e c) n", p=P))]
        if "X1" in layers:
            later += [(xw[k][:], d[f"X1_{k}"]) for k in xw] + [(xb_[k][:], d[f"X1_{k}"]) for k in xb_]
            later += [(x_bv[:], d["X1_bv"]), (xmask[:], d["xmask"].rearrange("(q p) k -> p q k", p=P))]
        if "F1" in layers:
            later += [(f_w1[:], d["F1_w1"]), (f_w2[:], d["F1_w2"].rearrange("(c p) n -> p c n", p=P))]
            later += [(f_taps[:, k], d["F1_taps"][k:k + 1, :].to_broadcast([P, FF])) for k in range(3)]

        def program(e, kind, table):
            for n in layers:
                if n == "A0":
                    e.wait_ge(s_w, 16 * len(loads))
                elif n == layers[0] or layers[layers.index(n) - 1] == "A0":
                    e.wait_ge(s_later, 16 * len(later))
                for fn in table[n]:
                    fn(e, next((a for a in atts if a.name == n), ln_of[n]))

        def fills_of(a):
            l = [(scr[a.name][:, r, z].rearrange("b h n -> b (h n)"), fill[0:64, z])
                 for r in range(ROWS, KR) for z in range(1 if a is a_cross else 2)]
            if a is a_cross:
                l.append((scr_kx[ROWS:KR].rearrange("r h b n -> r (h b n)"), fill[0:SC, 1, 0:P]))
            return l

        def fill_sp(e, a):
            for dst, src in fills_of(a):
                e.dma_start(dst, src).then_inc(s_filled, 16)

        def later_sp(e):
            for a in atts:
                if a is not a_self0:
                    fill_sp(e, a)
            for dst, src in later:
                e.dma_start(dst, src).then_inc(s_later, 16)
            parts_in_sp(e)
            if "M0" in layers:
                e.wait_ge(m["zeroed"], 1)
                e.dma_start(scr_xn.rearrange("(t p) d -> p t d", p=P), zero[:].unsqueeze(1).to_broadcast([P, MT, D]))\
                    .then_inc(s_zero, 16)

        @block.sync
        def _(e):
            e.dma_start(xs[:], d["x"].rearrange("(t p) d -> p t d", p=P)).then_inc(s_x, 16)
            for dst, src in loads:
                e.dma_start(dst, src).then_inc(s_w, 16)
            e.wait_ge(s_fill, 1)
            if a_self0 in atts:
                fill_sp(e, a_self0)
            if layers[0] != "A0":
                later_sp(e)
                parts_out_sp(e)
                parts_out_sp(e)
            program(e, "sp", {"A0": [staging_sp, attention_sp, lambda e, a: parts_out_sp(e)], "X0": [staging_sp, attention_sp],
                              "M0": [lambda e, ln: moe_sp(e)], "A1": [staging_sp, attention_sp], "X1": [], "F1": []})
            e.wait_ge(x_new[-1][0], x_new[-1][1] + NB)
            e.dma_start(out.rearrange("(t p) d -> p t d", p=P), xs[:]).then_inc(s_out, 16)
            e.wait_ge(s_out, 16)

        @block.gpsimd
        def _(e):
            starts_at_one = [att_sem[n] for n in ATT_FREE] + [s_xnT, s_xnT_sb, s_xnT_used, m["logits"], m["y_out"]]
            starts_at_one += m["stored"] + [x for (x, _), n in zip(x_new, layers) if n not in of_att]
            starts_at_one += [c[n] for n in "q_out masked probsT_out logits probsT recip out probs".split()]
            starts_at_one += [f[n] for n in "xT_out silu hT_out added conv".split()]
            for free in starts_at_one:
                e.sem_inc(free, FREE)
            e.memset(mhalf[:], -0.5)
            e.memset(ones_row[:], 1.0)
            e.memset(ones3[:], 1.0)
            e.memset(onesb[:], 1.0)
            e.memset(onesf[:], 1.0)
            e.memset(f_xT[:], 0.0)
            for z in range(2):
                i = e.memset(fill[:, z], float(z))
            i.then_inc(s_fill, 1)
            e.memset(zero[:], 0.0).then_inc(m["zeroed"], 1)
            e.memset(v9[:], 1.0)
            e.memset(vsl[:], 0.0)
            e.memset(stk[:], 0.0)
            e.iota(iota_e[:], pattern=[[1, NE]], base=0, channel_multiplier=0, allow_small_or_imprecise_dtypes=True)
            e.iota(iota_t[:], pattern=[[1, MT]], base=0, channel_multiplier=0, allow_small_or_imprecise_dtypes=True)
            e.memset(ident[:], 1.0).then_inc(s_const, 1)
            e.wait_ge(s_const, 1)
            e.affine_select(out=ident[:], in_=ident[:], compare_op=ALU.is_equal, fill=0.0, base=0,
                            pattern=[[-1, P]], channel_multiplier=1)
            e.affine_select(out=before[:], in_=onesb[:], compare_op=ALU.is_gt, fill=0.0, base=0,
                            pattern=[[1, P]], channel_multiplier=-1)
            e.memset(mask_qk[:], 0.0)
            e.memset(mask_kq[:], 0.0).then_inc(s_const, 1)
            e.wait_ge(s_const, 2)
            e.affine_select(out=mask_qk[:], in_=mask_qk[:], compare_op=ALU.is_ge, fill=MASKED, base=0,
                            pattern=[[-1, P]], channel_multiplier=1)
            e.affine_select(out=mask_kq[:], in_=mask_kq[:], compare_op=ALU.is_ge, fill=MASKED, base=0,
                            pattern=[[1, P]], channel_multiplier=-1)
            e.tensor_copy(identb[:], ident[:]).then_inc(s_const, 1)
            if layers[0] != "A0":
                parts_pool(e)
            program(e, "pool", {"A0": [staging_pool, attention_pool, lambda e, a: parts_pool(e)], "X0": [staging_pool, attention_pool],
                                "M0": [moe_pool], "A1": [staging_pool, attention_pool],
                                "X1": [ffn_pool], "F1": [ffn_pool]})

        @block.tensor
        def _(e):
            e.wait_ge(s_const, 3)
            program(e, "pe", {"A0": [staging_pe, attention_pe], "X0": [staging_pe, attention_pe], "M0": [moe_pe],
                              "A1": [staging_pe, attention_pe], "X1": [cross_pe], "F1": [ffn_pe]})

        @block.vector
        def _(e):
            e.wait_ge(s_const, 3)
            program(e, "dve", {"A0": [staging_dve, attention_dve], "X0": [staging_dve, attention_dve],
                               "M0": [moe_dve], "A1": [staging_dve, attention_dve], "X1": [cross_dve],
                               "F1": [ffn_dve]})

        @block.scalar
        def _(e):
            program(e, "act", {"A0": [staging_act, attention_act], "X0": [staging_act, attention_act],
                               "M0": [moe_act], "A1": [staging_act, attention_act], "X1": [cross_act],
                               "F1": [ffn_act]})


def lay_out(i):
    t = lambda v: np.ascontiguousarray(np.asarray(v).T)
    col = lambda v: np.asarray(v).reshape(P, 1)
    row = lambda v: np.asarray(v).reshape(1, -1)
    o = {"x": np.asarray(i["x"]).reshape(NT * P, D), "ctxT": t(np.asarray(i["ctx_1024"]).reshape(NB * SC, D)),
         "xmask": np.asarray(i["mask_1xSxS2_ff0"])[0]}
    for name, src in (("A0", "L0_attn_"), ("A1", "L1_attn_")):
        o |= {f"{name}_w{k}": t(i[f"{src}w{k}"]) for k in "qkvo"}
        o |= {f"{name}_b{k}": (col if k in "qk" else row)(i[f"{src}b{k}"]) for k in "qkvo"}
    o |= {f"X0_w{k}": np.asarray(i[f"L0_xattn_W{k}"]) for k in "qkvo"}
    o |= {f"X0_b{k}": (col if k in "qk" else row)(i[f"L0_xattn_b{k}"]) for k in "qkvo"}
    pair = np.arange(D) ^ 1
    for k in "qk":
        o[f"A0_w{k}_swapped"] = np.ascontiguousarray(o[f"A0_w{k}"][:, pair])
        o[f"A0_b{k}_swapped"] = np.ascontiguousarray(o[f"A0_b{k}"][pair])
    f32 = np.float32
    rate = np.exp((f32(2.0) * np.arange(HD // 2, dtype=f32) / f32(HD) * f32(math.log(10000.0))).astype(f32))
    theta = (np.arange(S, dtype=f32)[None, :] / rate[:, None]).astype(f32).astype(np.float64)
    which = (np.arange(D) % HD) // 2
    sign = np.where(np.arange(D) % 2 == 0, -1.0, 1.0)[:, None]
    o["cos_sin"] = np.stack([np.cos(theta)[which], sign * np.sin(theta)[which]], axis=1).astype(f32)
    o |= {"M0_gate_w": i["L0_ffn_gate_w"], "M0_gate_b": row(i["L0_ffn_gate_b"]), "M0_w1": i["L0_ffn_w1"],
          "M0_b1": row(i["L0_ffn_b1"]), "M0_w2": i["L0_ffn_w2"], "M0_b2": row(i["L0_ffn_b2"])}
    o |= {f"X1_w{k}": i[f"L1_xattn_kernel_{k}"] for k in "qkv"}
    o |= {f"X1_b{k}": (col if k in "qk" else row)(i[f"L1_xattn_bias_{k}"]) for k in "qkv"}
    o |= {"F1_w1": t(i["L1_ffn_w1"]), "F1_taps": np.ascontiguousarray(np.asarray(i["L1_ffn_conv_w"])[:, 0, :].T),
          "F1_cb": row(i["L1_ffn_conv_b"]), "F1_w2": t(i["L1_ffn_w2"])}
    return {k: np.ascontiguousarray(v) for k, v in o.items()}


def kernel(**inputs):
    import concourse.bacc as bacc
    from concourse.bass_utils import run_bass_kernel_spmd

    nc = bacc.Bacc("TRN2", target_bir_lowering=False, num_devices=1)
    arrays = {f"in_{k}": v for k, v in lay_out(inputs).items()}
    d = {k[3:]: nc.dram_tensor(k, v.shape, mybir.dt.from_np(v.dtype), kind="ExternalInput").ap() for k, v in arrays.items()}
    out = nc.dram_tensor("out", (NT * P, D), F32, kind="ExternalOutput").ap()
    build(nc, d, out)
    r = run_bass_kernel_spmd(nc, [arrays], core_ids=[0])
    return r.results[0]["out"].reshape(NB, S, D)
```

```python
from contextlib import ExitStack
import math

import numpy as np

import concourse.bass as bass
from concourse import mybir
from concourse.alu_op_type import AluOpType as ALU

ACT = mybir.ActivationFunctionType
AX = mybir.AxisListType
F32 = mybir.dt.float32
BF16 = mybir.dt.bfloat16
I32 = mybir.dt.int32
U32 = mybir.dt.uint32

P = 128
NB, S, D = 4, 512, 128
QT = S // P
NT = NB * QT
NH, HD = 16, 8
SC = 77
HG = 4
UNITS = NH // HG
TERMS = 6
RUNS = 3
GR = 8
HR = HD * GR
SHIFT = 2
NE, FF = 8, 512
FC = FF // P
W_PIECES = NE + NE // 2
MT = 2 * NT + NE
CODED = 4
ROUND = 1.5 * 2 ** 23
VW = 32
EPS = 1e-5
FREE = 1
MASKED = -1e30
Q_RUNS = ((0, 3, 0, True), (3, 2, 1, True), (5, 1, 2, True))
K_RUNS = ((0, 3, 0, False), (3, 2, 0, False), (5, 1, 0, False))


def wait(e, sem, value):
    if isinstance(value, int) and value <= 0:
        return
    e.wait_ge(sem, value)


SLOT_DMAS = 3
ATT_FREE = "out_turned normed merged proj rest cos_sin v_done stacked_k stacked_q roped part3".split()


class Attention:

    def __init__(self, name, ln, keys, causal):
        self.name, self.ln, self.keys, self.causal = name, ln, keys, causal
        self.kt = -(-keys // P)
        self.kp = min(keys, P)
        self.items = []
        for qt in range(QT):
            n = (qt + 1) * P if causal else keys
            per = max(1, min(HG, 1 << int(math.log2(S // n))))
            self.items += [(qt, h, per, n) for h in range(0, HG, per)]
        self.sem = {}
        self.rope = causal

    def totals(self):
        cross, units = self.name == "X0", UNITS * NB
        both = NB + 1 if cross else 2 * NB
        of = dict.fromkeys(ATT_SEMS, units)
        of |= dict.fromkeys(("part1", "rest", "part2", "part3"), both)
        of |= dict.fromkeys(("k_proj", "v_proj", "v_done"), 1 if cross else NB)
        of |= dict.fromkeys(("cos_sin", "roped"), 2 * NB if self.rope else 0)
        of |= dict.fromkeys(("merged", "merged_out", "proj", "x_new"), NB)
        of |= dict.fromkeys(("max_in", "max_out"), units * len(self.items))
        of |= dict.fromkeys(("scores", "probs"), 2 * self.kt * units)
        of |= {"q_proj": 2 * NB if self.rope else NB, "pv": self.kt * units, "shifted": 16 * NB,
               "slot": 16 * SLOT_DMAS * NB, "stacked_q": 16 * RUNS * NB,
               "stacked_k": 16 * RUNS * (1 if cross else NB)}
        return of

    def first_query(self, kt):
        return kt * P if self.causal else 0

    def share(self, c):
        n = len(self.items)
        return range(n * c // self.kt, n * (c + 1) // self.kt)


ATT_SEMS = """q_proj k_proj v_proj part1 rest part2 part3 v_done stacked_q stacked_k values cos_sin roped
max_in max_out neg_hi neg_lo turned rows scores probs pv pv_out out_turned
reciprocal normed merged merged_out proj x_new""".split()


def build(nc, d, out, layers=("A0", "X0", "M0", "A1", "X1", "F1")):
    ln_of = {n: i for i, n in enumerate(layers)}
    es = ExitStack()
    with es:
        def sb(name, shape, dt=F32):
            return es.enter_context(nc.sbuf_tensor(name, shape, dt))

        def ps(name, shape, dt=F32):
            return es.enter_context(nc.psum_tensor(name, shape, dt))

        def sem(name):
            return es.enter_context(nc.semaphore(name))

        a_self0 = Attention("A0", ln_of.get("A0"), S, True)
        a_cross = Attention("X0", ln_of.get("X0"), SC, False)
        a_self1 = Attention("A1", ln_of.get("A1"), S, False)
        atts = [a for a in (a_self0, a_cross, a_self1) if a.name in layers]
        att_sem = {n: sem(f"att_{n}") for n in ATT_SEMS}
        att_sem |= {n: [sem(f"att_{n}{i}") for i in range(UNITS)] for n in ("slot", "shifted")}
        since = {n: FREE if n in ATT_FREE else 0 for n in att_sem}
        for a in atts:
            a.sem, a.since = att_sem, dict(since)
            since = {n: v + a.totals()[n] for n, v in since.items()}
        of_att = {a.name: (att_sem["x_new"], a.since["x_new"]) for a in atts}
        x_new = [of_att.get(n) or (sem(f"{n}_x"), FREE) for n in layers]

        xs = sb("x_sb", [P, NT, D])
        stats = sb("stats", [P, QT, 6])
        mv = sb("mv", [P, QT, 2])
        var = sb("var", [P, QT])
        rstd = sb("rstd", [P, QT])
        mhalf = sb("mhalf", [P, QT])
        xn = sb("xn", [P, QT, D])
        xnT = sb("xnT", [P, S])
        ident = sb("ident", [P, P])
        identb = sb("identb", [P, P], BF16)
        ones_row = sb("ones_row", [1, P])
        mask_qk = sb("mask_qk", [P, P], BF16)
        mask_kq = sb("mask_kq", [P, P], BF16)
        parts = sb("parts", [P, 2, 3, S], BF16)
        rest = sb("rest", [P, 2, S])
        v9 = sb("v9", [P, NT, NH, HD + 1])
        stk = sb("stk", [P, UNITS, 3, 2, S], BF16)
        fill = sb("fill", [P, 2, S], BF16)
        vsl = sb("vsl", [P, UNITS, QT, HG, VW])
        mx = sb("mx", [P, 2, QT, HG])
        neg = sb("neg", [P, 2, 2, 2, 2, QT], BF16)
        negT = sb("negT", [8 * QT, 2, P], BF16)
        probs = sb("probs", [P, 2, HG, S])
        oT = sb("oT", [P, S])
        rec = sb("rec", [P, QT, HG])
        otok = sb("otok", [P, QT, D])
        okT = sb("okT", [P, S])
        wts = {}
        for a in atts:
            wts[a.name] = {k: sb(f"{a.name}_{k}", [P, D]) for k in ("wq", "wk", "wv", "wo")}
            wts[a.name] |= {k: sb(f"{a.name}_{k}", [P, 1]) for k in ("bq", "bk")}
            wts[a.name] |= {"bv": sb(f"{a.name}_bv", [P, D]), "bo": sb(f"{a.name}_bo", [1, D])}
        wsw = [sb(f"A0_w{k}_swapped", [P, D]) for k in "qk"]
        bsw = [sb(f"A0_b{k}_swapped", [P, 1]) for k in "qk"]
        cos_sin = sb("cos_sin", [P, 2, S])
        ctxT = sb("ctxT", [P, NB * SC])
        gate_w, gate_b = sb("gate_w", [P, NE]), sb("gate_b", [1, NE])
        w12 = sb("w12", [P, W_PIECES, 2 * FF])
        w1 = w12[:, 0:NE]
        w2 = w12[:, NE:W_PIECES].rearrange("p a n -> p (a n)").rearrange("p (e c n) -> p e c n", e=NE, c=FC)
        b1p, b2p = sb("b1p", [P, NE * 2 * FF], BF16), sb("b2p", [P, NE * D], BF16)
        BIAS = (NE * 2 * FF + NE * D + FF) // P
        bias_in, bias_part = sb("bias_in", [P, BIAS]), sb("bias_part", [P, 3, BIAS], BF16)
        onesb = sb("onesb", [P, P], BF16)
        before = sb("before", [P, P], BF16)
        iota_e = sb("iota_e", [P, NE])
        iota_t = sb("iota_t", [P, MT])
        xn_all = v9[:].rearrange("p t h d -> p (t h d)")[:, 0:NT * D].rearrange("p (t d) -> p t d", t=NT)
        lg = sb("lg", [P, QT, NE])
        top = sb("top", [P, QT, 8])
        top_at = sb("top_at", [P, QT, 8], U32)
        top_f = sb("top_f", [P, QT, 2])
        top_v = sb("top_v", [P, NT, 2])
        picked = sb("picked", [P, 2, NT, NE])
        routed = sb("routed", [P, NT, NE], BF16)
        small = {k: sb(f"moe_{k}", [P, NE]) for k in ("count", "tiles", "cum", "base")}
        routed_sum = sb("routed_sum", [P, NE], BF16)
        place = sb("place", [P, NT, NE])
        place_of = sb("place_of", [P, 2, NT, NE])
        place_f = sb("place_f", [P, 2, NT])
        place_u = sb("place_u", [P, 2, NT], U32)
        tile_le = sb("tile_le", [P, MT, NE])
        tile_f = sb("tile_f", [P, MT])
        tile_code, tile_e = sb("tile_code", [P, MT // CODED]), sb("tile_e", [P, MT // CODED], I32)
        gate = sb("gate", [P, 2, NT])
        gate_t = sb("gate_t", [P, 2, NT])
        zero = sb("zero", [P, D])
        dve_step = sb("dve_step", [1, 1])
        xw = {k: sb(f"X1_{k}", [P, D]) for k in ("wq", "wk", "wv")}
        xb_ = {k: sb(f"X1_{k}", [P, 1]) for k in ("bq", "bk")}
        x_bv = sb("X1_bv", [P, D])
        xmask = sb("xmask", [P, QT, SC])
        x_kT = sb("x_kT", [P, NB * SC])
        x_v = sb("x_v", [SC, NB, D])
        x_lg = sb("x_lg", [P, QT, SC])
        x_neg, x_sum, x_rec = sb("x_neg", [P, QT]), sb("x_sum", [P, QT]), sb("x_rec", [P, QT])
        f_w1, f_w2 = sb("f_w1", [P, FF]), sb("f_w2", [P, FC, D])
        f_w1c = sb("f_w1c", [P, 3, FF])
        f_w2q = sb("f_w2q", [P, FC, D], BF16)
        f_taps = sb("f_taps", [P, 3, FF])
        f_cb = sb("f_cb", [P, FF], BF16)
        f_abs, f_mean, f_inv = sb("f_abs", [P, 2]), sb("f_mean", [P, 2]), sb("f_inv", [P, 2])
        f_row = sb("f_row", [P, 2])
        onesf = sb("onesf", [P, P])
        f_amax, f_scale, f_back = sb("f_amax", [P, QT]), sb("f_scale", [P, QT]), sb("f_back", [P, QT])
        f_xT = stk[:].rearrange("p u z h n -> p (u z h n)").bitcast(F32)[:, 0:NB * (S + 2)].rearrange("p (b n) -> p b n", b=NB)
        f_cur = sb("f_cur", [P, 2, P + 2])
        f_h, f_hm = probs[:, 0, 0:2], probs[:, 0, 2:4]
        f_hq, f_hT = parts[:, 0, 0:2], parts[:, 1, 0:2]
        f_hmax, f_hscale, f_hback = sb("f_hmax", [P, 2]), sb("f_hscale", [P, 2]), sb("f_hback", [P, 2])

        bank_max = [ps(f"bank_max{i}", [P, S]) for i in range(2)]
        bank_st = [ps(f"bank_st{i}", [P, 2, S]) for i in range(2)]
        bank_pv = ps("bank_pv", [P, S])
        bank_misc = ps("bank_misc", [P, S])
        misc_bf = bank_misc[:].bitcast(BF16)

        scr_xn = nc.dram_tensor("routed_tokens", [MT * P, D], F32).ap()
        scr_y = nc.dram_tensor("expert_outputs", [MT * P, D], F32).ap()
        scr = {a.name: nc.dram_tensor(f"stack_{a.name}", [2, NB, NH, HD, GR, S], BF16).ap() for a in atts}
        scr_kx = nc.dram_tensor("stack_kx", [NH, HD, GR, NB, SC], BF16).ap()

        s_x0, s_x = sem("s_x0"), sem("s_x")
        s_w, s_later, s_experts = sem("s_w"), sem("s_later"), sem("s_experts")
        s_ones, s_padded = sem("s_ones"), sem("s_padded")
        s_clear = sem("s_clear")
        s_fill, s_filled0, s_filled = sem("s_fill"), sem("s_filled0"), sem("s_filled")
        s_const = sem("s_const")
        s_stat, s_aggr, s_var, s_rstd = sem("s_stat"), sem("s_aggr"), sem("s_var"), sem("s_rstd")
        s_xn, s_xnT, s_xnT_sb = sem("s_xn"), sem("s_xnT"), sem("s_xnT_sb")
        s_xnT_used = sem("s_xnT_used")
        s_out = sem("s_out")
        s_zero, s_pin, s_p, s_b1p, s_xq = sem("s_zero"), sem("s_pin"), sem("s_p"), sem("s_b1p"), sem("s_xq")

        block = es.enter_context(nc.Block())

        NOTHING = (lambda: None, lambda: None)

        def x_tile(t, n=1):
            return xs[:, bass.ds(t, n), :]

        def take_wait(e):
            e.memset(dve_step[:], 0.0)

        def moments_dve(e, ln, b):
            g = 4 * ln + b
            if ln == 0:
                e.wait_ge(s_x0 if isinstance(b, int) and b == 0 else s_x, 16)
            else:
                e.wait_ge(x_new[ln - 1][0], x_new[ln - 1][1] + b + 1)
            take_wait(e)
            for j in range(QT):
                e.bn_stats(stats[:, j, :], x_tile(4 * b + j).rearrange("p o d -> p (o d)")).then_inc(s_stat, 1)
            e.wait_ge(s_stat, QT * (g + 1))
            take_wait(e)
            for j in range(QT):
                e.bn_aggr(mv[:, j, :], stats[:, j, :]).then_inc(s_aggr, 1)
            e.wait_ge(s_aggr, QT * (g + 1))
            e.tensor_scalar(var[:], mv[:, :, 1], EPS, None, ALU.add).then_inc(s_var, 1)

        def normed_dve(e, ln, b, kept=False):
            g = 4 * ln + b
            e.wait_ge(s_rstd, g + 1)
            e.wait_ge(s_xnT, FREE + g)
            if kept and not (isinstance(b, int) and b == 0):
                e.wait_ge(m["kept"], b)
            for j in range(QT):
                i = e.tensor_scalar(xn[:, j, :], x_tile(4 * b + j).rearrange("p o d -> p (o d)"),
                                    mv[:, j, 0:1], rstd[:, j:j + 1], ALU.subtract, ALU.mult)
            i.then_inc(s_xn, 1)

        def norm_dve(e, ln, b):
            moments_dve(e, ln, b)
            normed_dve(e, ln, b)

        def paced_dve(e, ln, first, second, kept=False, late=NOTHING):
            def normed(b):
                normed_dve(e, ln, b, kept)

            moments_dve(e, ln, 0)
            normed(0)
            moments_dve(e, ln, 1)
            with e.Fori(0, NB - 2) as b:
                first(b)
                normed(b + 1)
                moments_dve(e, ln, b + 2)
                second(b)
            first(NB - 2)
            normed(NB - 1)
            second(NB - 2)
            late[0]()
            first(NB - 1)
            second(NB - 1)
            late[1]()

        def norm_pool(e, ln, b):
            g = 4 * ln + b
            e.wait_ge(s_var, g + 1)
            e.tensor_tensor(rstd[:], var[:], mhalf[:], ALU.pow).then_inc(s_rstd, 1)

        def norm_pe(e, ln, b, bank):
            g = 4 * ln + b
            e.wait_ge(s_xn, g + 1)
            e.wait_ge(s_xnT_sb, FREE + g)
            for j in range(QT):
                i = e.transpose(bank[:, j * P:(j + 1) * P], xn[:, j, :], ident[:])
            i.then_inc(s_xnT, 1)

        def norm_act(e, ln, b, bank):
            g = 4 * ln + b
            e.wait_ge(s_xnT, FREE + g + 1)
            e.wait_ge(s_xnT_used, FREE + g)
            e.copy(xnT[:], bank[:]).then_inc(s_xnT_sb, 1)

        def between(e, norm, first, second, late=NOTHING):
            norm(0)
            with e.Fori(0, NB - 2) as b:
                first(b)
                norm(b + 1)
                second(b)
            first(NB - 2)
            norm(NB - 1)
            second(NB - 2)
            late[0]()
            first(NB - 1)
            second(NB - 1)
            late[1]()

        def ahead(e, norm, work, late=NOTHING):
            between(e, norm, lambda b: None, work, late)

        def behind(e, norm, work, late=NOTHING):
            between(e, norm, work, lambda b: None, late)

        def stage_pe(e, a, b):
            s, w, g = a.sem, wts[a.name], 4 * a.ln + b
            e.wait_ge(s_xnT_sb, FREE + g + 1)
            two = a is not a_cross
            if a.rope:
                e.wait_ge(s["cos_sin"], a.since["cos_sin"] + 2 * b)
            else:
                e.wait_ge(s["rest"], a.since["rest"] + (2 * b if two else b + 1))
            e.matmul(bank_max[0][:], w["wq"][:], xnT[:], start=True, stop=True).then_inc(s["q_proj"], 1)
            if a.rope:
                for z in range(2):
                    i = e.matmul(bank_st[z][:, 0], wsw[z][:], xnT[:], start=True, stop=True)
                i.then_inc(s["q_proj"], 1)
            if not two:
                e.drain().then_inc(s_xnT_used, 1)
                return
            e.matmul(bank_max[1][:], w["wk"][:], xnT[:], start=True, stop=True).then_inc(s["k_proj"], 1)
            e.wait_ge(s["v_done"], a.since["v_done"] + b)
            for j in range(QT):
                i = e.matmul(bank_pv[:, j * D:(j + 1) * D], xnT[:, j * P:(j + 1) * P], w["wv"][:], start=True, stop=True)
            i.then_inc(s["v_proj"], 1)
            e.drain().then_inc(s_xnT_used, 1)

        def stack_sp(e, a, z, n, part_count, of_parts, to):
            s = a.sem
            e.wait_ge(s["part3"], part_count)
            for first, rows, part, same in (K_RUNS if z else Q_RUNS):
                src = of_parts[:, part:part + (1 if same else rows), 0:n]
                if same and rows > 1:
                    src = src.to_broadcast([P, rows, n])
                e.dma_start(to[:, first:first + rows, :], src).then_inc(s["stacked_k" if z else "stacked_q"], 16)

        def heads(h):
            return h % 2, h // 2

        def load_unit(e, a, u, slot, b, free=None):
            s = a.sem
            if free is not None:
                e.wait_ge(s["scores"], a.since["scores"] + 2 * a.kt * free)
            hh = slice(slot * HG, (slot + 1) * HG)
            e.dma_start(stk[:, slot, 0], scr[a.name][0, bass.ds(b, 1), hh]
                        .rearrange("o (i j) d t n -> (o j d t) i n", j=2)).then_inc(s["slot"][slot], 16)
            for j in range(2):
                rows = slice(HR * j, HR * (j + 1))
                if a is a_cross:
                    e.dma_start(stk[rows, slot, 1 + j, :, 0:SC], scr_kx[slot * HG + j:(slot + 1) * HG:2, :, :, bass.ds(b, 1), :]
                                .rearrange("i d t o n -> (d t) i (o n)")).then_inc(s["slot"][slot], 16)
                else:
                    e.dma_start(stk[rows, slot, 1 + j], scr[a.name][1, bass.ds(b, 1), slot * HG + j:(slot + 1) * HG:2]
                                .rearrange("o i d t n -> (o d t) i n")).then_inc(s["slot"][slot], 16)

        def values_pool(e, a, u, slot, b):
            s = a.sem
            wait(e, s["pv"], a.since["pv"] + a.kt * (u - UNITS + 1))
            if a is a_cross:
                i = e.tensor_copy(vsl[0:SC, slot, 0, :, 0:HD + 1],
                                  v9[0:SC, bass.ds(b, 1), slot * HG:(slot + 1) * HG, :].rearrange("p o h d -> p (o h) d"))
            else:
                i = e.tensor_copy(vsl[:, slot, :, :, 0:HD + 1], v9[:, bass.ds(4 * b, QT), slot * HG:(slot + 1) * HG, :])
            i.then_inc(s["values"], 1)

        early_banks = [bank_st[i][:, 1] for i in range(2)]
        late_banks = [bank_max[i][:] for i in range(2)]

        def max_pe(e, a, u, slot, b, picks, banks=late_banks):
            s, n = a.sem, len(a.items)
            for m in picks:
                qt, h0, per, keys = a.items[m]
                if m == 0:
                    e.wait_ge(s["slot"][slot], a.since["slot"] + 16 * SLOT_DMAS * (b + 1))
                k = n * slot + m
                bank = banks[k % 2]
                wait(e, s["max_out"], a.since["max_out"] + n * u + m - 1)
                for i in range(per):
                    j, pp = heads(h0 + i)
                    o = bank[:, i * keys:(i + 1) * keys]
                    mm = e.matmul(o, stk[:, slot, 0, pp, qt * P:(qt + 1) * P], stk[:, slot, 1 + j, pp, 0:keys], start=True, stop=not a.causal)
                    if a.causal:
                        mm = e.matmul(o[:, qt * P:(qt + 1) * P], identb[:], mask_qk[:], start=False, stop=True)
                mm.then_inc(s["max_in"], 1)

        def max_dve(e, a, u, slot, picks, banks=late_banks):
            s, n = a.sem, len(a.items)
            for m in picks:
                qt, h0, per, keys = a.items[m]
                e.wait_ge(s["max_in"], a.since["max_in"] + n * u + m + 1)
                e.tensor_reduce(mx[:, slot % 2, qt, h0:h0 + per],
                                banks[(n * slot + m) % 2][:, 0:per * keys].rearrange("p (h k) -> p h k", h=per),
                                AX.X, ALU.max).then_inc(s["max_out"], 1)

        def negate_dve(e, a, u, slot):
            s, n = a.sem, len(a.items)
            e.wait_ge(s["max_out"], a.since["max_out"] + n * (u + 1))
            wait(e, s["turned"], a.since["turned"] + u - 1)
            src = mx[:, slot % 2].rearrange("p q (h j) -> p j h q", j=2)
            e.tensor_scalar(neg[:, slot % 2, :, 0], src, -1.0, None, ALU.mult).then_inc(s["neg_hi"], 1)
            e.wait_ge(s["neg_hi"], a.since["neg_hi"] + u + 1)
            for j in range(2):
                i = e.scalar_tensor_tensor(neg[:, slot % 2, j, 1], src[:, j], -1.0, neg[:, slot % 2, j, 0],
                                           ALU.mult, ALU.subtract)
            i.then_inc(s["neg_lo"], 1)

        def turn_pe(e, a, u, slot):
            s = a.sem
            e.wait_ge(s["neg_lo"], a.since["neg_lo"] + u + 1)
            e.transpose(misc_bf[0:8 * QT, 0:P], neg[:, slot % 2].rearrange("p j c h q -> p (j c h q)"),
                        identb[:]).then_inc(s["turned"], 1)

        def turn_dve(e, a, u, slot, b):
            s = a.sem
            e.wait_ge(s["turned"], a.since["turned"] + u + 1)
            wait(e, s["shifted"][(slot + 2) % UNITS], a.since["shifted"] + (16 * (b if slot < 2 else b + 1)))
            e.tensor_copy(negT[:, slot % 2, :], misc_bf[0:8 * QT, 0:P]).then_inc(s["rows"], 1)

        def shift_sp(e, a, u, slot):
            s = a.sem
            e.wait_ge(s["rows"], a.since["rows"] + u + 1)
            e.dma_start(stk[TERMS:P:P // (2 * SHIFT), slot, 0].rearrange("r h n -> r (h n)"),
                        negT[:, slot % 2, :]).then_inc(s["shifted"][slot], 16)

        def scores_pe(e, a, u, slot, b, kt, j):
            s = a.sem
            if kt == 0 and j == 0:
                e.wait_ge(s["shifted"][slot], a.since["shifted"] + 16 * (b + 1))
            q0 = a.first_query(kt)
            n = S - q0
            wait(e, s["probs"], a.since["probs"] + 2 * a.kt * u + 2 * kt + j - 1)
            for pp in range(2):
                o = bank_st[j][0:a.kp, pp, 0:n]
                mm = e.matmul(o, stk[:, slot, 1 + j, pp, kt * P:kt * P + a.kp], stk[:, slot, 0, pp, q0:S],
                              start=True, stop=not a.causal)
                if a.causal:
                    mm = e.matmul(o[:, 0:P], identb[:], mask_kq[:], start=False, stop=True)
            mm.then_inc(s["scores"], 1)

        def probs_of(a, slot, kt):
            return (kt if a.kt > 1 else slot) % 2

        def exp_act(e, a, u, slot, kt):
            s = a.sem
            n = S - a.first_query(kt)
            for j in range(2):
                e.wait_ge(s["scores"], a.since["scores"] + 2 * a.kt * u + 2 * kt + j + 1)
                if j == 0:
                    wait(e, s["pv"], a.since["pv"] + a.kt * u + kt - 1)
                e.activation(probs[0:a.kp, probs_of(a, slot, kt), j:HG:2, 0:n], bank_st[j][0:a.kp, :, 0:n], ACT.Exp,
                             scale=1 / math.sqrt(HD)).then_inc(s["probs"], 1)

        def pv_pe(e, a, u, slot, kt):
            s = a.sem
            if kt == 0:
                e.wait_ge(s["values"], a.since["values"] + u + 1)
                wait(e, s["pv_out"], a.since["pv_out"] + u)
            e.wait_ge(s["probs"], a.since["probs"] + 2 * a.kt * u + 2 * kt + 2)
            q0 = a.first_query(kt)
            half = probs_of(a, slot, kt)
            for h in range(HG):
                mm = e.matmul(bank_pv[VW * h:VW * (h + 1), q0:S], vsl[0:a.kp, slot, kt, h, :],
                              probs[0:a.kp, half, h, 0:S - q0], start=(kt == 0), stop=(kt == a.kt - 1),
                              skip_group_check=True)
            mm.then_inc(s["pv"], 1)

        def pv_out_act(e, a, u):
            s = a.sem
            e.wait_ge(s["pv"], a.since["pv"] + a.kt * (u + 1))
            wait(e, s["out_turned"], a.since["out_turned"] + u)
            e.copy(oT[:], bank_pv[:]).then_inc(s["pv_out"], 1)

        def finish_pe(e, a, u):
            s = a.sem
            e.wait_ge(s["pv_out"], a.since["pv_out"] + u + 1)
            wait(e, s["normed"], a.since["normed"] + u)
            for j in range(QT):
                i = e.transpose(bank_misc[:, j * P:(j + 1) * P], oT[:, j * P:(j + 1) * P], ident[:])
            i.then_inc(s["out_turned"], 1)

        def finish_dve(e, a, u, hg, b):
            s = a.sem
            e.wait_ge(s["out_turned"], a.since["out_turned"] + u + 1)
            src = bank_misc[:].rearrange("p (q h c) -> p q h c", q=QT, h=HG)
            e.reciprocal(rec[:], src[:, :, :, HD]).then_inc(s["reciprocal"], 1)
            e.wait_ge(s["reciprocal"], a.since["reciprocal"] + u + 1)
            if hg == 0:
                wait(e, s["merged"], a.since["merged"] + b)
            e.tensor_tensor(otok[:, :, hg * HG * HD:(hg + 1) * HG * HD].rearrange("p q (h c) -> p q h c", h=HG),
                            src[:, :, :, 0:HD], rec[:].unsqueeze(3).to_broadcast([P, QT, HG, HD]),
                            ALU.mult).then_inc(s["normed"], 1)

        def merge_pe(e, a, b):
            s = a.sem
            e.wait_ge(s["normed"], a.since["normed"] + UNITS * (b + 1))
            for j in range(QT):
                i = e.transpose(bank_misc[:, j * P:(j + 1) * P], otok[:, j, :], ident[:])
            i.then_inc(s["merged"], 1)

        def merge_act(e, a, b):
            s = a.sem
            e.wait_ge(s["merged"], a.since["merged"] + b + 1)
            wait(e, s["proj"], a.since["proj"] + b)
            e.copy(okT[:], bank_misc[:]).then_inc(s["merged_out"], 1)

        def proj_pe(e, a, b):
            s, w = a.sem, wts[a.name]
            e.wait_ge(s["merged_out"], a.since["merged_out"] + b + 1)
            for j in range(QT):
                o = bank_misc[:, j * D:(j + 1) * D]
                e.matmul(o, okT[:, j * P:(j + 1) * P], w["wo"][:], start=True, stop=False)
                i = e.matmul(o, ones_row[:], w["bo"][:], start=False, stop=True)
            i.then_inc(s["proj"], 1)

        def proj_dve(e, a, b):
            s = a.sem
            e.wait_ge(s["proj"], a.since["proj"] + b + 1)
            xb = x_tile(4 * b, QT)
            e.tensor_tensor(xb, xb, bank_misc[:].rearrange("p (q d) -> p q d", q=QT), ALU.add).then_inc(s["x_new"], 1)

        def step_pe(e, a, u, hg, b, ahead, first):
            s = a.sem
            for c in range(a.kt):
                items = list(a.share(c)) if ahead > 1 else []

                def maxima(picks):
                    max_pe(e, a, u + 2, (hg + 2) % UNITS, b + (hg + 2) // UNITS, picks)

                maxima(items[:1])
                scores_pe(e, a, u, hg, b, c, 0)
                maxima(items[1:2])
                if c == 0 and ahead > 0:
                    turn_pe(e, a, u + 1, (hg + 1) % UNITS)
                scores_pe(e, a, u, hg, b, c, 1)
                if c == min(1, a.kt - 1) and not first:
                    if ahead > 0:
                        e.wait_ge(s["rows"], a.since["rows"] + u + 2)
                    finish_pe(e, a, u - 1)
                maxima(items[2:])
                if c > 0:
                    pv_pe(e, a, u, hg, c - 1)
                if hg == 0 and not first:
                    if c == min(2, a.kt - 1):
                        merge_pe(e, a, b - 1)
                    if c == a.kt - 1:
                        proj_pe(e, a, b - 1)
            pv_pe(e, a, u, hg, a.kt - 1)

        def step_dve(e, a, u, hg, b, ahead, first):
            for c in range(a.kt):
                items = list(a.share(c)) if ahead > 1 else []
                max_dve(e, a, u + 2, (hg + 2) % UNITS, items[:2])
                if c == 0 and ahead > 0:
                    turn_dve(e, a, u + 1, (hg + 1) % UNITS, b + (hg + 1) // UNITS)
                if c == min(1, a.kt - 1) and not first:
                    finish_dve(e, a, u - 1, (hg - 1) % UNITS, b - 1 if hg == 0 else b)
                max_dve(e, a, u + 2, (hg + 2) % UNITS, items[2:])
                if hg == 0 and not first and c == a.kt - 1:
                    proj_dve(e, a, b - 1)
            if ahead > 1:
                negate_dve(e, a, u + 2, (hg + 2) % UNITS)

        def step_act(e, a, u, hg, b, ahead, first):
            for c in range(a.kt):
                if a.kt > 1:
                    exp_act(e, a, u, hg, c)
                if c == 0 and not first:
                    pv_out_act(e, a, u - 1)
                if a.kt == 1:
                    exp_act(e, a, u, hg, c)
                if hg == 0 and not first and c == min(2, a.kt - 1):
                    merge_act(e, a, b - 1)

        def steps(e, a, one):
            one(e, a, 0, 0, 0, 2, True)
            with e.Fori(0, NB - 1) as b:
                for hg in (1, 2, 3, 4):
                    one(e, a, UNITS * b + hg, hg % UNITS, b + hg // UNITS, 2, False)
            for u in range(UNITS * (NB - 1) + 1, UNITS * NB):
                one(e, a, u, u % UNITS, NB - 1, min(2, UNITS * NB - 1 - u), False)

        def attention_pe(e, a):
            e.wait_ge(a.sem["rest"], a.since["rest"] + a.totals()["rest"])
            e.wait_ge(a.sem["max_out"], a.since["max_out"] + 2 * len(a.items))
            e.wait_ge(a.sem["rows"], a.since["rows"] + 1)
            steps(e, a, step_pe)
            last = UNITS * NB - 1
            finish_pe(e, a, last)
            e.wait_ge(a.sem["normed"], a.since["normed"] + last + 1)
            merge_pe(e, a, NB - 1)
            proj_pe(e, a, NB - 1)

        def attention_dve(e, a):
            steps(e, a, step_dve)
            finish_dve(e, a, UNITS * NB - 1, UNITS - 1, NB - 1)
            proj_dve(e, a, NB - 1)

        def attention_act(e, a):
            steps(e, a, step_act)
            pv_out_act(e, a, UNITS * NB - 1)
            merge_act(e, a, NB - 1)

        def attention_pool(e, a):
            for u in range(UNITS):
                values_pool(e, a, u, u, 0)
            if a is a_self0:
                later_pool(e)
            with e.Fori(1, NB) as b:
                for hg in range(UNITS):
                    values_pool(e, a, UNITS * b + hg, hg, b)

        def attention_sp(e, a):
            s = a.sem
            shift_sp(e, a, 0, 0)
            shift_sp(e, a, 1, 1)
            e.wait_ge(s["stacked_q"], a.since["stacked_q"] + 16 * RUNS * NB)
            e.wait_ge(s["stacked_k"], a.since["stacked_k"] + 16 * RUNS * (1 if a is a_cross else NB))
            with e.Fori(1, NB) as b:
                for hg in range(UNITS):
                    u = UNITS * b + hg
                    load_unit(e, a, u, hg, b, free=u - 3)
                    shift_sp(e, a, u - 2, (hg + 2) % UNITS)
                    if a is a_self0 and "M0" in layers:
                        weights_sp(e, u - UNITS)
            for u in range(UNITS * NB - 2, UNITS * NB):
                shift_sp(e, a, u, u % UNITS)

        def roped(z):
            return probs[:, 1, z]

        def staging_pe(e, a):
            if a is a_cross:
                w = wts["X0"]
                s = a.sem
                e.matmul(bank_max[1][:, 0:NB * SC], w["wk"][:], ctxT[:], start=True, stop=True).then_inc(s["k_proj"], 1)
                for b in range(NB):
                    o = bank_pv[0:SC, b * D:(b + 1) * D]
                    i = e.matmul(o, ctxT[:, b * SC:(b + 1) * SC], w["wv"][:], start=True, stop=True)
                i.then_inc(s["v_proj"], 1)

            def maxima_0():
                max_pe(e, a, 0, 0, 0, range(len(a.items)), early_banks)

            def maxima_1():
                turn_pe(e, a, 0, 0)
                max_pe(e, a, 1, 1, 0, range(len(a.items)), early_banks)

            behind(e, lambda b: norm_pe(e, a.ln, b, bank_misc), lambda b: stage_pe(e, a, b), (maxima_0, maxima_1))

        def staging_act(e, a):
            w, s = wts[a.name], a.sem
            if a is a_cross:
                e.wait_ge(s["k_proj"], a.since["k_proj"] + 1)
                e.activation(parts[:, 1, 0, 0:NB * SC], bank_max[1][:, 0:NB * SC], ACT.Identity, bias=w["bk"][:])\
                    .then_inc(s["part1"], 1)
                e.wait_ge(s["rest"], a.since["rest"] + 1)
                e.copy(parts[:, 1, 1, 0:NB * SC], rest[:, 1, 0:NB * SC]).then_inc(s["part2"], 1)

            def first(b):
                if a is a_cross:
                    e.wait_ge(s["q_proj"], a.since["q_proj"] + b + 1)
                    e.wait_ge(s["stacked_q"], a.since["stacked_q"] + 16 * RUNS * b)
                    e.activation(parts[:, 0, 0, :], bank_max[0][:], ACT.Identity, bias=w["bq"][:]).then_inc(s["part1"], 1)
                else:
                    for z in range(2):
                        e.wait_ge(s["stacked_k" if z else "stacked_q"], a.since["stacked_k" if z else "stacked_q"] + 16 * RUNS * b)
                        if a.rope:
                            e.wait_ge(s["roped"], a.since["roped"] + 2 * b + z + 1)
                            e.copy(parts[:, z, 0, :], roped(z)).then_inc(s["part1"], 1)
                            continue
                        e.wait_ge(s["k_proj" if z else "q_proj"], a.since["k_proj" if z else "q_proj"] + b + 1)
                        e.activation(parts[:, z, 0, :], bank_max[z][:], ACT.Identity, bias=w["bk" if z else "bq"][:])\
                            .then_inc(s["part1"], 1)

            def second(b):
                for z in range(1 if a is a_cross else 2):
                    e.wait_ge(s["rest"], a.since["rest"] + (b + 2 if a is a_cross else 2 * b + z + 1))
                    e.copy(parts[:, z, 1, :], rest[:, z, :]).then_inc(s["part2"], 1)

            def norm(b):
                norm_act(e, a.ln, b, bank_misc)

            if a.rope:
                def both(b):
                    first(b)
                    second(b)

                ahead(e, norm, both)
            else:
                between(e, norm, first, second)

        def head_bias(bias):
            return bias.rearrange("p (h d) -> p h d", h=NH).unsqueeze(1)

        def staging_dve(e, a):
            w, s = wts[a.name], a.sem
            if a is a_cross:
                e.wait_ge(s["part1"], a.since["part1"] + 1)
                e.scalar_tensor_tensor(rest[:, 1, 0:NB * SC], bank_max[1][:, 0:NB * SC], w["bk"][:],
                                       parts[:, 1, 0, 0:NB * SC], ALU.add, ALU.subtract).then_inc(s["rest"], 1)
                e.wait_ge(s_padded, 1)
                e.wait_ge(s["v_proj"], a.since["v_proj"] + 1)
                e.tensor_tensor(v9[0:SC, 0:NB, :, 0:HD], bank_pv[0:SC].rearrange("p (b h d) -> p b h d", b=NB, h=NH),
                                head_bias(w["bv"][0:SC]).to_broadcast([SC, NB, NH, HD]), ALU.add).then_inc(s["v_done"], 1)

            def work(b):
                if a is a_self0:
                    e.wait_ge(s_w, 16 * len(loads))
                for z in range(2 if a.rope else 0):
                    e.wait_ge(s["k_proj" if z else "q_proj"], a.since["k_proj" if z else "q_proj"] + (b + 1 if z else 2 * b + 2))
                    e.wait_ge(s["roped"], a.since["roped"] + 2 * b)
                    e.scalar_tensor_tensor(probs[:, 0, z], bank_max[z][:], w["bk" if z else "bq"][:], cos_sin[:, 0],
                                           ALU.add, ALU.mult)
                    e.scalar_tensor_tensor(probs[:, 0, 2 + z], bank_st[z][:, 0], bsw[z][:], cos_sin[:, 1],
                                           ALU.add, ALU.mult).then_inc(s["cos_sin"], 1)
                for z in range(1 if a is a_cross else 2):
                    n0 = b + 1 if a is a_cross else 2 * b + z
                    e.wait_ge(s["part1"], a.since["part1"] + n0 + 1)
                    e.wait_ge(s["part3"], a.since["part3"] + (b + 1 if a is a_cross else 2 * b))
                    if a.rope:
                        e.tensor_tensor(rest[:, z, :], roped(z), parts[:, z, 0, :], ALU.subtract).then_inc(s["rest"], 1)
                        continue
                    e.scalar_tensor_tensor(rest[:, z, :], bank_max[z][:], w["bk" if z else "bq"][:], parts[:, z, 0, :],
                                           ALU.add, ALU.subtract).then_inc(s["rest"], 1)
                if a is not a_cross:
                    e.wait_ge(s_padded, 1)
                    e.wait_ge(s["v_proj"], a.since["v_proj"] + b + 1)
                    e.tensor_tensor(v9[:, bass.ds(4 * b, QT), :, 0:HD],
                                    bank_pv[:].rearrange("p (q h d) -> p q h d", q=QT, h=NH),
                                    head_bias(w["bv"][:]).to_broadcast([P, QT, NH, HD]), ALU.add).then_inc(s["v_done"], 1)


            def norm(b):
                combine_dve(e, a.ln - 1, b)
                norm_dve(e, a.ln, b)

            def maxima_0():
                max_dve(e, a, 0, 0, range(len(a.items)), early_banks)
                negate_dve(e, a, 0, 0)

            def maxima_1():
                turn_dve(e, a, 0, 0, 0)
                max_dve(e, a, 1, 1, range(len(a.items)), early_banks)
                negate_dve(e, a, 1, 1)

            if a is a_self1 and "M0" in layers:
                ahead(e, norm, work, (maxima_0, maxima_1))
            else:
                paced_dve(e, a.ln, lambda b: None, work, late=(maxima_0, maxima_1))

        def staging_pool(e, a):
            s = a.sem
            if a is a_self1 and "M0" in layers:
                e.memset(v9[:, :, :, HD:HD + 1], 1.0).then_inc(s_ones, 1)
                e.wait_ge(s_ones, 1)
            if a is a_cross:
                e.wait_ge(s["part2"], a.since["part2"] + 1)
                e.tensor_tensor(parts[:, 1, 2, 0:NB * SC], rest[:, 1, 0:NB * SC], parts[:, 1, 1, 0:NB * SC],
                                ALU.subtract).then_inc(s["part3"], 1)

            def work(b):
                for z in range(2 if a.rope else 0):
                    e.wait_ge(s["cos_sin"], a.since["cos_sin"] + 2 * b + z + 1)
                    e.wait_ge(s["rest"], a.since["rest"] + 2 * b)
                    e.tensor_tensor(roped(z), probs[:, 0, z], probs[:, 0, 2 + z], ALU.add).then_inc(s["roped"], 1)
                for z in range(1 if a is a_cross else 2):
                    e.wait_ge(s["part2"], a.since["part2"] + (b + 1 if a is a_cross else 2 * b + z) + 1)
                    e.wait_ge(s["stacked_k" if z else "stacked_q"], a.since["stacked_k" if z else "stacked_q"] + 16 * RUNS * b)
                    e.tensor_tensor(parts[:, z, 2, :], rest[:, z, :], parts[:, z, 1, :], ALU.subtract)\
                        .then_inc(s["part3"], 1)

            def norm(b):
                norm_pool(e, a.ln, b)
                if a is atts[0] and isinstance(b, int) and b == 0:
                    e.memset(v9[:], 1.0)
                    e.memset(vsl[:], 0.0).then_inc(s_padded, 1)

            if a is a_self1 and "M0" in layers:
                for b in range(NB + 1):
                    if b < NB:
                        fetch_pool(e, b)
                        norm(b)
                    if b:
                        work(b - 1)
            else:
                norm(0)
                norm(1)
                with e.Fori(0, NB - 2) as b:
                    norm(b + 2)
                    work(b)
                for b in (NB - 2, NB - 1):
                    work(b)
            e.wait_ge(s["v_done"], a.since["v_done"] + (1 if a is a_cross else NB))

        def staging_sp(e, a):
            s = a.sem
            if a is a_cross:
                stack_sp(e, a, 1, NB * SC, a.since["part3"] + 1, parts[:, 1], scr_kx.rearrange("h d t b n -> (h d) t (b n)"))

            def stacks(b):
                for z in range(1 if a is a_cross else 2):
                    stack_sp(e, a, z, S, a.since["part3"] + (b + 2 if a is a_cross else 2 * b + z + 1), parts[:, z],
                             scr[a.name][z, bass.ds(b, 1)].rearrange("o h d t n -> (o h d) t n"))

            for b in range(2):
                stacks(b)
            e.wait_ge(s_clear, 1)
            if a is a_self0:
                e.wait_ge(s_filled0, 16 * len(fills_of(a)))
            else:
                e.wait_ge(s_filled, 16 * sum(len(fills_of(o)) for o in atts if o is not a_self0))
            e.wait_ge(s["stacked_q"], a.since["stacked_q"] + 16 * RUNS)
            e.wait_ge(s["stacked_k"], a.since["stacked_k"] + 16 * RUNS)
            for u in range(UNITS):
                load_unit(e, a, u, u, 0)
            with e.Fori(2, NB) as b:
                stacks(b)

        m = {n: sem(f"M0_{n}") for n in """gate_proj logits top top_at top_f picked routed kept sum_in
            rank count floor cum base place tile_le tile_f tile_e
            diff expo plus recip gates zeroed scattered xT xT_out hidden silu act actT actT_out y_in y_out
            weighed landed""".split()}
        m |= {n: [sem(f"M0_{n}{i}") for i in range(2)] for n in ("tile_in", "stored")}
        m["got"] = [sem(f"M0_got{i}") for i in range(2)]

        def moe_dve(e, ln):

            def work(b):
                e.wait_ge(m["gate_proj"], b + 1)
                e.tensor_copy(lg[:], bank_max[0][:, 0:QT * NE].rearrange("p (q n) -> p q n", q=QT))\
                    .then_inc(m["logits"], 1)
                e.wait_ge(m["logits"], FREE + b + 1)
                take_wait(e)
                for j in range(QT):
                    e.max(top[:, j, :], lg[:, j, :]).then_inc(m["top"], 1)
                e.wait_ge(m["top"], QT * (b + 1))
                take_wait(e)
                for j in range(QT):
                    e.max_index(top_at[:, j, :], top[:, j, :], lg[:, j, :]).then_inc(m["top_at"], 1)
                e.tensor_copy(top_v[:, bass.ds(4 * b, QT), :], top[:, :, 0:2])
                e.wait_ge(m["top_at"], QT * (b + 1))
                e.tensor_copy(top_f[:], top_at[:, :, 0:2]).then_inc(m["top_f"], 1)
                e.wait_ge(m["top_f"], b + 1)
                for k in range(2):
                    e.tensor_tensor(picked[:, k, bass.ds(4 * b, QT), :],
                                    iota_e[:].unsqueeze(1).to_broadcast([P, QT, NE]),
                                    top_f[:, :, k].unsqueeze(2).to_broadcast([P, QT, NE]),
                                    ALU.is_equal).then_inc(m["picked"], 1)
                e.wait_ge(m["picked"], 2 * (b + 1))
                e.tensor_tensor(routed[:, bass.ds(4 * b, QT), :], picked[:, 0, bass.ds(4 * b, QT), :],
                                picked[:, 1, bass.ds(4 * b, QT), :], ALU.add).then_inc(m["routed"], 1)

            paced_dve(e, ln, lambda b: None, work, kept=True)
            e.wait_ge(m["routed"], NB)
            with nc.allow_low_precision("sums of up to 16 ones"):
                e.tensor_reduce(routed_sum[:], routed[:].rearrange("p t n -> p n t"), AX.X, ALU.add)\
                    .then_inc(m["sum_in"], 1)
            e.tensor_tensor(gate_t[:, 0], top_v[:, :, 1], top_v[:, :, 0], ALU.subtract).then_inc(m["diff"], 1)
            e.wait_ge(m["count"], 1)
            e.tensor_scalar(small["count"][:], bank_max[1][:, 0:NE], P - 1.0, 1.0 / P, ALU.add, ALU.mult)\
                .then_inc(m["floor"], 1)
            e.wait_ge(m["floor"], 1)
            e.tensor_scalar(small["tiles"][:], small["count"][:], -0.5 + 0.5 / P, ROUND, ALU.add, ALU.add)\
                .then_inc(m["floor"], 1)
            e.wait_ge(m["floor"], 2)
            e.tensor_scalar(small["count"][:], small["tiles"][:], -ROUND, None, ALU.add).then_inc(m["floor"], 1)
            e.wait_ge(m["floor"], 3)
            e.tensor_tensor_scan(small["cum"][:], onesf[:, 0:NE], small["count"][:], 0.0, ALU.mult, ALU.add)\
                .then_inc(m["cum"], 1)
            e.wait_ge(m["cum"], 1)
            e.tensor_tensor(small["base"][:], small["cum"][:], small["count"][:], ALU.subtract).then_inc(m["base"], 1)
            e.tensor_tensor(tile_le[:], small["cum"][:].unsqueeze(1).to_broadcast([P, MT, NE]),
                            iota_t[:].unsqueeze(2).to_broadcast([P, MT, NE]), ALU.is_le).then_inc(m["tile_le"], 1)
            e.wait_ge(m["rank"], 1)
            e.wait_ge(m["base"], 1)
            e.scalar_tensor_tensor(place[:], small["base"][:].unsqueeze(1).to_broadcast([P, NT, NE]),
                                   float(P), bank_max[0][:, 0:NT * NE].rearrange("p (t n) -> p t n", n=NE),
                                   ALU.mult, ALU.add).then_inc(m["place"], 1)
            e.wait_ge(m["place"], 1)
            for k in range(2):
                e.tensor_tensor(place_of[:, k], picked[:, k], place[:], ALU.mult).then_inc(m["place"], 1)
            e.wait_ge(m["place"], 3)
            e.tensor_reduce(place_f[:], place_of[:], AX.X, ALU.add).then_inc(m["place"], 1)
            e.wait_ge(m["place"], 4)
            e.tensor_copy(place_u[:], place_f[:]).then_inc(m["place"], 1)
            e.wait_ge(m["tile_le"], 1)
            e.tensor_reduce(tile_f[:], tile_le[:], AX.X, ALU.add).then_inc(m["tile_f"], 1)
            e.wait_ge(m["tile_f"], 1)
            e.tensor_scalar(tile_f[:], tile_f[:], NE - 1.0, None, ALU.min).then_inc(m["tile_e"], 1)
            e.wait_ge(m["tile_e"], 1)
            for n in range(1, CODED + 1):
                g = MT // CODED - (n == CODED)
                e.scalar_tensor_tensor(tile_code[:, 0:g], tile_f[:, n:MT:CODED], float(NE ** n),
                                       (tile_f[:, 0:MT:CODED] if n == 1 else tile_code[:])[:, 0:g], ALU.mult, ALU.add)\
                    .then_inc(m["tile_e"], 1)
                e.wait_ge(m["tile_e"], n + 1)
            e.tensor_copy(tile_e[:], tile_code[:]).then_inc(m["tile_e"], 1)
            e.wait_ge(m["expo"], 1)
            e.tensor_scalar(gate[:, 1], gate_t[:, 1], 1.0, None, ALU.add).then_inc(m["plus"], 1)
            e.wait_ge(m["plus"], 1)
            e.reciprocal(gate[:, 0], gate[:, 1]).then_inc(m["recip"], 1)
            e.wait_ge(m["recip"], 1)
            e.tensor_tensor(gate[:, 1], gate[:, 0], gate_t[:, 1], ALU.mult).then_inc(m["gates"], 1)

            if "F1" in layers:
                weights_dve(e)

            def turned(t, k):
                e.wait_ge(m["xT"], t + 1)
                e.tensor_copy(x_inT[:, k], bank_misc[:, 0:P]).then_inc(m["xT_out"], 1)

            def product(t, k):
                e.wait_ge(m["silu"], t + 1)
                e.tensor_tensor(act[:], hid[k][0], silu[:, k], ALU.mult).then_inc(m["act"], 1)
                e.wait_ge(m["actT"], t + 1)
                e.tensor_copy(actT[:], t_bank).then_inc(m["actT_out"], 1)

            for t in range(2):
                turned(t, t)
            with e.Fori(0, MT // 2 - 1) as i:
                for k in range(2):
                    product(2 * i + k, k)
                    turned(2 * i + k + 2, k)
            for k in range(2):
                product(MT - 2 + k, k)
            e.wait_ge(m["gates"], 1)
            if layers[-1] == "M0":
                with e.Fori(0, NB) as b:
                    combine_dve(e, ln, b)

        def combine_dve(e, ln, b):
            e.wait_ge(m["landed"], b + 1)
            for k in range(2):
                for j in range(QT):
                    xj = x_tile(4 * b + j).rearrange("p o d -> p (o d)")
                    if k:
                        e.wait_ge(m["weighed"], 2 * QT * b + j + 1)
                    e.scalar_tensor_tensor(xj, got[:, bass.ds(4 * b + j, 1), k].rearrange("p o d -> p (o d)"),
                                           gate[:, k, bass.ds(4 * b + j, 1)], xj, ALU.mult, ALU.add).then_inc(m["weighed"], 1)
            e.wait_ge(m["weighed"], 2 * QT * (b + 1))
            e.sem_inc(x_new[ln][0], 1)

        act = oT
        actT = okT
        silu = probs[:, 0, 0:2]
        y_sb = probs[:, 0, 2:4, 0:D]
        x_in = probs[:, 1, 0:2, 0:D]
        x_inT = probs[:, 1, 2:4, 0:P]
        got = probs[:].rearrange("p a h s -> p (a h s)").rearrange("p (t k d) -> p t k d", t=NT, k=2)
        hid = [(bank_max[0][:], bank_max[1][:]), (bank_st[1][:, 0], bank_st[1][:, 1])]
        y_bank = bank_st[0][:, 0]
        t_bank = bank_st[0][:, 1]

        def moe_pool(e, ln):
            with e.Fori(0, NB) as b:
                norm_pool(e, ln, b)
            e.wait_ge(m["kept"], NB)
            e.wait_ge(m["place"], 5)
            e.wait_ge(s_zero, 16)
            for t in range(NT):
                for k in range(2):
                    e.indirect_dma_start(scr_xn, bass.IndirectOffsetOnAxis(ap=place_u[:, k, t:t + 1], axis=0),
                                         xn_all[:, t, :], None).then_inc(m["scattered"], 16)
            for k in range(2):
                e.wait_ge(m["stored"][k], FREE + 16 * (MT // 2))
            if layers[-1] == "M0":
                for b in range(NB):
                    fetch_pool(e, b)

        def fetch_pool(e, b):
            for n in ([0, 1] if b == 0 else [b + 1] if b < NB - 1 else []):
                for t in range(QT * n, QT * (n + 1)):
                    for k in range(2):
                        e.indirect_dma_start(got[:, t, k], None, scr_y,
                                             bass.IndirectOffsetOnAxis(ap=place_u[:, k, t:t + 1], axis=0))\
                            .then_inc(m["got"][n % 2], 16)
            e.wait_ge(m["got"][b % 2], 16 * 2 * QT * (b // 2 + 1))
            e.sem_inc(m["landed"], 1)

        def moe_pe(e, ln):

            def work(b):
                e.wait_ge(s_xnT_sb, FREE + 4 * ln + b + 1)
                e.wait_ge(m["logits"], FREE + b)
                for j in range(QT):
                    o = bank_max[0][:, j * NE:(j + 1) * NE]
                    e.matmul(o, xnT[:, j * P:(j + 1) * P], gate_w[:], start=True, stop=False)
                    i = e.matmul(o, ones_row[:], gate_b[:], start=False, stop=True)
                i.then_inc(m["gate_proj"], 1)
                e.drain().then_inc(s_xnT_used, 1)

            behind(e, lambda b: norm_pe(e, ln, b, bank_misc), work)
            e.wait_ge(m["routed"], NB)
            r = routed[:].rearrange("p t n -> p (t n)")
            o = bank_max[0]
            e.matmul(o[:, 0:NT * NE], before[:], r, start=True, stop=False, skip_group_check=True)
            for k in range(1, NT):
                i = e.matmul(o[:, k * NE:NT * NE], onesb[:], r[:, 0:(NT - k) * NE], start=False, stop=(k == NT - 1),
                             skip_group_check=True)
            i.then_inc(m["rank"], 1)
            e.wait_ge(m["sum_in"], 1)
            e.matmul(bank_max[1][:, 0:NE], onesb[:], routed_sum[:], start=True, stop=True).then_inc(m["count"], 1)
            e.wait_ge(m["tile_e"], CODED + 2)
            e.wait_ge(m["place"], 1)
            if "F1" in layers:
                weights_pe(e)
            e.wait_ge(s_b1p, 16 * 3 * len(part_srcs))

            def experts(i):
                code = e.value_load(tile_e[0:1, bass.ds(i, 1)], min_val=0, max_val=NE ** (CODED + 1) - 1)
                return [(code >> (3 * n)) & (NE - 1) for n in range(CODED + 1)]

            def turn(k, loaded):
                e.wait_ge(m["tile_in"][k], loaded)
                e.transpose(bank_misc[:, 0:P], x_in[:, k], ident[:]).then_inc(m["xT"], 1)

            def hidden(t, k, ex, z):
                if z == 0:
                    e.wait_ge(m["xT_out"], t + 1)
                o = hid[k][z]
                e.matmul(o, x_inT[:, k], w1[:, bass.ds(ex, 1), z * FF:(z + 1) * FF].rearrange("p o n -> p (o n)"),
                         start=True, stop=False)
                mm = e.matmul(o, onesb[:], b1p[:, bass.ds(ex * (2 * FF) + z * FF, FF)], start=False, stop=True)
                if z == 1:
                    mm.then_inc(m["hidden"], 1)

            def turn_act(t):
                e.wait_ge(m["act"], t + 1)
                for c in range(FC):
                    mm = e.transpose(t_bank[:, c * P:(c + 1) * P], act[:, c * P:(c + 1) * P], ident[:])
                mm.then_inc(m["actT"], 1)

            def output(t, ex):
                e.wait_ge(m["actT_out"], t + 1)
                e.wait_ge(m["y_out"], FREE + t)
                for c in range(FC):
                    e.matmul(y_bank[:, 0:D], actT[:, c * P:(c + 1) * P],
                             w2[:, bass.ds(ex, 1), c, :].rearrange("p o n -> p (o n)"), start=(c == 0), stop=False)
                e.matmul(y_bank[:, 0:D], onesb[:], b2p[:, bass.ds(ex * D, D)], start=False, stop=True)\
                    .then_inc(m["y_in"], 1)

            e.wait_ge(s_experts, 16 * (W_PIECES if a_self0 in atts else 1))
            turn(0, 16)
            e.wait_ge(m["xT_out"], 1)
            turn(1, 16)
            first = experts(0)[0]
            for z in range(2):
                hidden(0, 0, first, z)

            def step(t, n, ex):
                k = n % 2
                more = not isinstance(t, int)
                if more or t + 1 < MT:
                    hidden(t + 1, 1 - k, ex[n + 1], 0)
                turn_act(t)
                if more or t + 2 < MT:
                    turn(k, 8 * (t - k) + 32)
                if more or t + 1 < MT:
                    hidden(t + 1, 1 - k, ex[n + 1], 1)
                output(t, ex[n])

            with e.Fori(0, MT // CODED - 1) as i:
                ex = experts(i)
                for n in range(CODED):
                    step(CODED * i + n, n, ex)
            ex = experts(MT // CODED - 1)
            for n in range(CODED):
                step(MT - CODED + n, n, ex)

        def moe_act(e, ln):
            with e.Fori(0, NB) as b:
                e.wait_ge(s_xn, 4 * ln + b + 1)
                e.copy(xn_all[:, bass.ds(4 * b, QT), :], xn[:]).then_inc(m["kept"], 1)
                norm_act(e, ln, b, bank_misc)
            e.wait_ge(m["diff"], 1)
            e.activation(gate_t[:, 1], gate_t[:, 0], ACT.Exp).then_inc(m["expo"], 1)

            def gate_part(t, k):
                e.wait_ge(m["hidden"], t + 1)
                e.activation(silu[:, k], hid[k][1], ACT.Silu).then_inc(m["silu"], 1)

            def keep(t, k, stored):
                e.wait_ge(m["y_in"], t + 1)
                e.wait_ge(m["stored"][k], FREE + stored)
                e.activation(y_sb[:, k], y_bank[:, 0:D], ACT.Copy).then_inc(m["y_out"], 1)
                e.wait_ge(m["y_out"], FREE + t + 1)
                e.dma_start(scr_y[bass.ds(t * P, P), :], y_sb[:, k]).then_inc(m["stored"][k], 16)

            gate_part(0, 0)
            with e.Fori(0, MT // 2 - 1) as i:
                for k in range(2):
                    gate_part(2 * i + k + 1, 1 - k)
                    keep(2 * i + k, k, 16 * i)
            gate_part(MT - 1, 1)
            for k in range(2):
                keep(MT - 2 + k, k, 16 * (MT // 2 - 1))

        def moe_sp(e):
            e.wait_ge(m["scattered"], 16 * 2 * NT)
            for k in range(2):
                e.dma_start(x_in[:, k], scr_xn[k * P:(k + 1) * P, :]).then_inc(m["tile_in"][k], 16)
            with e.Fori(0, MT // 2 - 1) as i:
                for k in range(2):
                    e.wait_ge(m["xT"], 2 * i + k + 1)
                    e.dma_start(x_in[:, k], scr_xn[bass.ds((2 * i + k + 2) * P, P), :]).then_inc(m["tile_in"][k], 16)

        c = {n: sem(f"X1_{n}") for n in "k_proj k_out v_proj v_out q_proj q_out logits masked neg probs probsT probsT_out out recip".split()}
        x_qT = okT
        x_p = probs[:, 0, 0:QT, 0:SC]
        x_pT = oT

        def cross_pe(e, ln):
            e.matmul(bank_max[1][:, 0:NB * SC], xw["wk"][:], ctxT[:], start=True, stop=True).then_inc(c["k_proj"], 1)
            for b in range(NB):
                o = bank_pv[0:SC, b * D:(b + 1) * D]
                i = e.matmul(o, ctxT[:, b * SC:(b + 1) * SC], xw["wv"][:], start=True, stop=True)
            i.then_inc(c["v_proj"], 1)
            e.wait_ge(c["k_out"], 1)
            e.wait_ge(c["v_out"], 1)

            def weights(b):
                e.wait_ge(s_xnT_sb, FREE + 4 * ln + b + 1)
                e.wait_ge(c["q_out"], FREE + b)
                e.matmul(bank_max[0][:], xw["wq"][:], xnT[:], start=True, stop=True).then_inc(c["q_proj"], 1)
                e.drain().then_inc(s_xnT_used, 1)
                e.wait_ge(c["q_out"], FREE + b + 1)
                e.wait_ge(c["masked"], FREE + b)
                for j in range(QT):
                    i = e.matmul(bank_max[1][:, j * SC:(j + 1) * SC], x_qT[:, j * P:(j + 1) * P],
                                 x_kT[:, bass.ds(b * SC, SC)], start=True, stop=True)
                i.then_inc(c["logits"], 1)
                e.wait_ge(c["probs"], FREE + QT * (b + 1))
                e.wait_ge(c["probsT_out"], FREE + b)
                for j in range(QT):
                    i = e.transpose(bank_st[0][0:SC, 0, j * P:(j + 1) * P], x_p[:, j], ident[:])
                i.then_inc(c["probsT"], 1)

            def output(b):
                e.wait_ge(c["probsT_out"], FREE + b + 1)
                e.wait_ge(x_new[ln][0], x_new[ln][1] + b)
                for j in range(QT):
                    i = e.matmul(bank_st[1][:, 0, j * P:(j + 1) * P], x_pT[0:SC, j * P:(j + 1) * P],
                                 x_v[:, bass.ds(b, 1), :].rearrange("p o n -> p (o n)"), start=True, stop=True)
                i.then_inc(c["out"], 1)

            between(e, lambda b: norm_pe(e, ln, b, bank_misc), weights, output)

        def cross_act(e, ln):
            e.wait_ge(c["k_proj"], 1)
            e.activation(x_kT[:], bank_max[1][:, 0:NB * SC], ACT.Identity, bias=xb_["bk"][:]).then_inc(c["k_out"], 1)

            def work(b):
                e.wait_ge(c["q_proj"], b + 1)
                e.wait_ge(c["logits"], FREE + b)
                e.activation(x_qT[:], bank_max[0][:], ACT.Identity, bias=xb_["bq"][:]).then_inc(c["q_out"], 1)
                e.wait_ge(c["neg"], b + 1)
                e.wait_ge(c["probsT"], FREE + b)
                e.wait_ge(c["recip"], FREE + b)
                for j in range(QT):
                    e.activation(x_p[:, j], x_lg[:, j], ACT.Exp, bias=x_neg[:, j:j + 1], accum_out=x_sum[:, j:j + 1])\
                        .then_inc(c["probs"], 1)
                e.wait_ge(c["probsT"], FREE + b + 1)
                e.wait_ge(c["out"], FREE + b)
                e.copy(x_pT[0:SC, :], bank_st[0][0:SC, 0]).then_inc(c["probsT_out"], 1)

            behind(e, lambda b: norm_act(e, ln, b, bank_misc), work)

        def cross_dve(e, ln):
            e.wait_ge(c["v_proj"], 1)
            e.tensor_tensor(x_v[:], bank_pv[0:SC].rearrange("p (b d) -> p b d", b=NB),
                            x_bv[0:SC].unsqueeze(1).to_broadcast([SC, NB, D]), ALU.add).then_inc(c["v_out"], 1)

            def scores(b):
                e.wait_ge(c["logits"], FREE + b + 1)
                e.wait_ge(c["probs"], FREE + QT * b)
                e.scalar_tensor_tensor(x_lg[:], bank_max[1][:, 0:QT * SC].rearrange("p (q k) -> p q k", q=QT),
                                       1 / math.sqrt(D), xmask[:], ALU.mult, ALU.add).then_inc(c["masked"], 1)
                e.wait_ge(c["masked"], FREE + b + 1)
                e.tensor_reduce(x_neg[:], x_lg[:], AX.X, ALU.max, negate=True).then_inc(c["neg"], 1)

            def output(b):
                e.wait_ge(c["probs"], FREE + QT * (b + 1))
                e.reciprocal(x_rec[:], x_sum[:]).then_inc(c["recip"], 1)
                e.wait_ge(c["recip"], FREE + b + 1)
                e.wait_ge(c["out"], FREE + b + 1)
                for j in range(QT):
                    xj = x_tile(4 * b + j).rearrange("p o d -> p (o d)")
                    i = e.scalar_tensor_tensor(xj, bank_st[1][:, 0, j * P:(j + 1) * P], x_rec[:, j:j + 1], xj,
                                               ALU.mult, ALU.add)
                i.then_inc(x_new[ln][0], 1)

            paced_dve(e, ln, scores, output)

        f = {n: sem(f"F1_{n}") for n in """abs total mean inv q1 q2 q3 taps amax aclip arec scale
            n1 n2 ends cur xT_out conv silu hmax hclip hrec hscale hm1 hm2 hq hT hT_out out""".split()}

        def weights_pe(e):
            e.wait_ge(f["abs"], 2)
            e.matmul(bank_misc[:, 0:2], onesf[:], f_abs[:], start=True, stop=True).then_inc(f["total"], 1)
            e.wait_ge(f["mean"], 1)

        def weights_dve(e):
            w = (f_w1[:], f_w2[:].rearrange("p c d -> p (c d)"))
            for k in range(2):
                e.tensor_reduce(f_abs[:, k:k + 1], w[k], AX.X, ALU.add, apply_absolute_value=True).then_inc(f["abs"], 1)
            e.wait_ge(f["total"], 1)
            e.tensor_scalar(f_mean[:], bank_misc[:, 0:2], 1.0 / (D * FF), 1e-5, ALU.mult, ALU.max).then_inc(f["mean"], 1)
            e.wait_ge(f["mean"], 1)
            e.reciprocal(f_inv[:], f_mean[:]).then_inc(f["inv"], 1)
            e.wait_ge(f["inv"], 1)
            for k in range(2):
                e.tensor_scalar(w[k], w[k], f_inv[:, k:k + 1], ROUND, ALU.mult, ALU.add).then_inc(f["q1"], 1)
            e.wait_ge(f["q1"], 2)
            for k in range(2):
                e.tensor_scalar(w[k], w[k], -ROUND, 1.0, ALU.add, ALU.min).then_inc(f["q2"], 1)
            e.wait_ge(f["q2"], 2)
            e.tensor_scalar(w[0], w[0], -1.0, f_mean[:, 0:1], ALU.max, ALU.mult).then_inc(f["q3"], 1)
            e.tensor_scalar(f_w2q[:].rearrange("p c d -> p (c d)"), w[1], -1.0, None, ALU.max).then_inc(f["q3"], 1)
            e.wait_ge(f["q3"], 2)
            for k in range(3):
                e.tensor_tensor(f_w1c[:, k], f_taps[:, k], w[0], ALU.mult).then_inc(f["taps"], 1)

        def ffn_dve(e, ln):
            if "M0" not in layers:
                weights_dve(e)

            def integers(b):
                e.wait_ge(s_xn, 4 * ln + b + 1)
                e.tensor_reduce(f_amax[:], xn[:], AX.X, ALU.max, apply_absolute_value=True).then_inc(f["amax"], 1)
                e.wait_ge(f["amax"], b + 1)
                e.tensor_scalar(f_amax[:], f_amax[:], 1e-5, None, ALU.max).then_inc(f["aclip"], 1)
                e.wait_ge(f["aclip"], b + 1)
                e.reciprocal(f_scale[:], f_amax[:]).then_inc(f["arec"], 1)
                e.tensor_scalar(f_back[:], f_amax[:], 1.0 / 127.0, None, ALU.mult)
                e.wait_ge(f["arec"], b + 1)
                e.tensor_scalar(f_scale[:], f_scale[:], 127.0, None, ALU.mult).then_inc(f["scale"], 1)
                e.wait_ge(f["scale"], b + 1)
                for j in range(QT):
                    i = e.tensor_scalar(xn[:, j], xn[:, j], f_scale[:, j:j + 1], ROUND, ALU.mult, ALU.add)
                i.then_inc(f["n1"], 1)
                e.wait_ge(f["n1"], b + 1)
                e.tensor_scalar(xn[:], xn[:], -ROUND, 127.0, ALU.add, ALU.min).then_inc(f["n2"], 1)
                e.wait_ge(f["n2"], b + 1)
                for j in range(QT):
                    i = e.tensor_scalar(xn[:, j], xn[:, j], -128.0, f_back[:, j:j + 1], ALU.max, ALU.mult)
                i.then_inc(s_xq, 1)

            moments_dve(e, ln, 0)
            with e.Fori(0, NB - 1) as b:
                normed_dve(e, ln, b)
                moments_dve(e, ln, b + 1)
                integers(b)
            normed_dve(e, ln, NB - 1)
            integers(NB - 1)
            for end in (0, S + 1):
                i = e.memset(f_xT[:, :, end:end + 1], 0.0)
            i.then_inc(f["ends"], 1)

            def quantize(t, j):
                k = j % 2
                e.wait_ge(f["silu"], FREE + t + 1)
                e.tensor_reduce(f_hmax[:, k:k + 1], f_h[:, k], AX.X, ALU.max, apply_absolute_value=True)\
                    .then_inc(f["hmax"], 1)
                e.wait_ge(f["hmax"], t + 1)
                e.tensor_scalar(f_hmax[:, k:k + 1], f_hmax[:, k:k + 1], 1e-5, None, ALU.max).then_inc(f["hclip"], 1)
                e.wait_ge(f["hclip"], t + 1)
                e.reciprocal(f_hscale[:, k:k + 1], f_hmax[:, k:k + 1]).then_inc(f["hrec"], 1)
                e.tensor_scalar(f_hback[:, k:k + 1], f_hmax[:, k:k + 1], 1.0 / 127.0, f_mean[:, 1:2],
                                ALU.mult, ALU.mult)
                e.wait_ge(f["hrec"], t + 1)
                e.tensor_scalar(f_hscale[:, k:k + 1], f_hscale[:, k:k + 1], 127.0, None, ALU.mult)\
                    .then_inc(f["hscale"], 1)
                e.wait_ge(f["hscale"], t + 1)
                e.tensor_scalar(f_hm[:, k], f_h[:, k], f_hscale[:, k:k + 1], ROUND, ALU.mult, ALU.add)\
                    .then_inc(f["hm1"], 1)
                e.wait_ge(f["hm1"], t + 1)
                e.tensor_scalar(f_hm[:, k], f_hm[:, k], ROUND + 127.0, ROUND - 128.0, ALU.min, ALU.max)\
                    .then_inc(f["hm2"], 1)

            def add(t, b, j):
                k = j % 2
                e.wait_ge(f["out"], t + 1)
                xj = x_tile(4 * b + j).rearrange("p o d -> p (o d)")
                e.scalar_tensor_tensor(xj, bank_st[1][:, k, 0:D], f_hback[:, k:k + 1], xj, ALU.mult, ALU.add)\
                    .then_inc(x_new[ln][0], 1)

            quantize(0, 0)

            def step(t, b, j):
                if in_range(t, 1):
                    quantize(t + 1, j + 1)
                add(t, b, j)

            tile_steps(e, step)

        def tile_steps(e, step):
            with e.Fori(0, NB - 1) as b:
                for j in range(QT):
                    step(QT * b + j, b, j)
            for j in range(QT):
                step(QT * (NB - 1) + j, NB - 1, j)

        def in_range(t, ahead):
            return not isinstance(t, int) or t + ahead < NT

        def ffn_pe(e, ln):
            if "M0" not in layers:
                weights_pe(e)
            e.wait_ge(f["taps"], 3)
            e.wait_ge(s_b1p, 16 * 3 * len(part_srcs))
            with e.Fori(0, NB) as b:
                e.wait_ge(s_xq, b + 1)
                e.wait_ge(f["xT_out"], FREE + b)
                for j in range(QT):
                    i = e.transpose(bank_misc[:, j * P:(j + 1) * P], xn[:, j, :], ident[:])
                i.then_inc(s_xnT, 1)

            def conv(t, j):
                e.wait_ge(f["cur"], t + 1)
                bank = bank_max[j % 2][:]
                for tap in range(3):
                    e.matmul(bank, f_cur[:, j % 2, tap:tap + P], f_w1c[:, tap], start=(tap == 0), stop=False)
                e.matmul(bank, onesb[:], f_cb[:], start=False, stop=True).then_inc(f["conv"], 1)

            def step(t, b, j):
                k = j % 2
                e.wait_ge(f["hq"], t + 1)
                for cc in range(FC):
                    i = e.transpose(f_tb[:, cc * P:(cc + 1) * P], f_hq[:, k, cc * P:(cc + 1) * P], identb[:])
                i.then_inc(f["hT"], 1)
                if in_range(t, 2):
                    conv(t + 2, j)
                e.wait_ge(f["hT_out"], t + 1)
                for cc in range(FC):
                    i = e.matmul(bank_st[1][:, k, 0:D], f_hT[:, k, cc * P:(cc + 1) * P], f_w2q[:, cc, :],
                                 start=(cc == 0), stop=(cc == FC - 1))
                i.then_inc(f["out"], 1)

            conv(0, 0)
            conv(1, 1)
            tile_steps(e, step)

        f_tb = bank_pv[:].bitcast(BF16)

        def ffn_act(e, ln):
            with e.Fori(0, NB) as b:
                e.wait_ge(s_xnT, FREE + 4 * ln + b + 1)
                e.copy(f_xT[:, bass.ds(b, 1), 1:S + 1].rearrange("p o n -> p (o n)"), bank_misc[:]).then_inc(f["xT_out"], 1)

            e.wait_ge(f["xT_out"], FREE + NB)
            e.wait_ge(f["ends"], 1)

            def current(b, j):
                b, j = b + j // QT, j % QT
                e.activation(f_cur[:, j % 2], f_xT[:, bass.ds(b, 1), j * P:j * P + P + 2].rearrange("p o n -> p (o n)"),
                             ACT.Copy).then_inc(f["cur"], 1)

            def silu(t, k):
                e.wait_ge(f["conv"], t + 1)
                e.activation(f_h[:, k], bank_max[k][:], ACT.Silu).then_inc(f["silu"], 1)

            def step(t, b, j):
                k = j % 2
                if in_range(t, 1):
                    silu(t + 1, 1 - k)
                if in_range(t, 3):
                    current(b, j + 3)
                e.wait_ge(f["hm2"], t + 1)
                e.activation(f_hq[:, k], f_hm[:, k], ACT.Copy, bias=-ROUND).then_inc(f["hq"], 1)
                e.wait_ge(f["hT"], t + 1)
                e.activation(f_hT[:, k], f_tb[:, 0:FF], ACT.Copy).then_inc(f["hT_out"], 1)

            current(0, 0)
            current(0, 1)
            silu(0, 0)
            current(0, 2)
            tile_steps(e, step)

        def norms_pool(e, ln):
            with e.Fori(0, NB) as b:
                norm_pool(e, ln, b)

        part_srcs = []
        if "M0" in layers:
            part_srcs += [(d["M0_b1"], b1p, NE * 2 * FF), (d["M0_b2"], b2p, NE * D)]
        if "F1" in layers:
            part_srcs += [(d["F1_cb"], f_cb, FF)]
        at = [0]
        for _, _, n in part_srcs:
            at.append(at[-1] + n // P)

        def parts_pool(e):
            if not part_srcs:
                return
            e.memset(b1p[:], 0.0)
            e.memset(b2p[:], 0.0)
            e.memset(f_cb[:], 0.0)
            e.wait_ge(s_pin, 16 * len(part_srcs))
            e.tensor_copy(bias_part[:, 0, 0:at[-1]], bias_in[:, 0:at[-1]]).then_inc(s_p, 1)
            e.wait_ge(s_p, 1)
            e.tensor_tensor(bias_in[:, 0:at[-1]], bias_in[:, 0:at[-1]], bias_part[:, 0, 0:at[-1]], ALU.subtract).then_inc(s_p, 1)
            e.wait_ge(s_p, 2)
            e.tensor_copy(bias_part[:, 1, 0:at[-1]], bias_in[:, 0:at[-1]]).then_inc(s_p, 1)
            e.wait_ge(s_p, 3)
            e.tensor_tensor(bias_in[:, 0:at[-1]], bias_in[:, 0:at[-1]], bias_part[:, 1, 0:at[-1]], ALU.subtract).then_inc(s_p, 1)
            e.wait_ge(s_p, 4)
            e.tensor_copy(bias_part[:, 2, 0:at[-1]], bias_in[:, 0:at[-1]]).then_inc(s_p, 1)

        def parts_in_dma(e):
            for (src, _, n), o in zip(part_srcs, at):
                e.dma_start(bias_in[:, o:o + n // P], src.rearrange("o (p c) -> (o p) c", p=P)).then_inc(s_pin, 16)

        def parts_out_sp(e):
            if not part_srcs:
                return
            e.wait_ge(s_p, 5)
            for (_, dst, n), o in zip(part_srcs, at):
                for i in range(3):
                    e.dma_start(dst[i:i + 1, :], bias_part[:, i, o:o + n // P]).then_inc(s_b1p, 16)

        def on_all(row):
            return row.to_broadcast([P, D])

        loads, later = [], []
        for a in atts:
            (loads if a is a_self0 else later).extend(
                [(wts[a.name][k][:], on_all(d[f"{a.name}_{k}"]) if k == "bv" else d[f"{a.name}_{k}"]) for k in wts[a.name]])
        if "A0" in layers:
            for i, k in enumerate("qk"):
                loads += [(wsw[i][:], d[f"A0_w{k}_swapped"]), (bsw[i][:], d[f"A0_b{k}_swapped"])]
            loads += [(cos_sin[:], d["cos_sin"])]
        if "X0" in layers or "X1" in layers:
            later += [(ctxT[:], d["ctxT"])]
        if "M0" in layers:
            later += [(gate_w[:], d["M0_gate_w"]), (gate_b[:], d["M0_gate_b"])]
        if "X1" in layers:
            later += [(xw[k][:], d[f"X1_{k}"]) for k in xw] + [(xb_[k][:], d[f"X1_{k}"]) for k in xb_]
            later += [(x_bv[:], on_all(d["X1_bv"])), (xmask[:], d["xmask"].rearrange("(q p) k -> p q k", p=P))]
        if "F1" in layers:
            later += [(f_w1[:], d["F1_w1"]), (f_w2[:], d["F1_w2"].rearrange("(c p) n -> p c n", p=P))]
            later += [(f_taps[:, k], d["F1_taps"][k:k + 1, :].to_broadcast([P, FF])) for k in range(3)]

        def program(e, kind, table):
            for n in layers:
                if n == "A0":
                    if kind == "pe":
                        e.wait_ge(s_w, 16 * len(loads))
                elif n == layers[0] or layers[layers.index(n) - 1] == "A0":
                    e.wait_ge(s_later, 16 * len(later))
                for fn in table[n]:
                    fn(e, next((a for a in atts if a.name == n), ln_of[n]))

        def fills_of(a):
            l = [(scr[a.name][z, :, :, :, t].rearrange("b h d n -> (h d) b n"),
                  fill[:, z].unsqueeze(1).to_broadcast([P, NB, S])) for t in range(TERMS, GR) for z in range(1 if a is a_cross else 2)]
            if a is a_cross:
                l.append((scr_kx[:, :, TERMS:GR].rearrange("h d t b n -> (h d) t (b n)"),
                          fill[:, 1, 0:NB * SC].unsqueeze(1).to_broadcast([P, GR - TERMS, NB * SC])))
            return l

        def fill_dma(e, a):
            for dst, src in fills_of(a):
                e.dma_start(dst, src).then_inc(s_filled0 if a is a_self0 else s_filled, 16)

        def weights_sp(e, n, pieces=1):
            e.dma_start(w12[:, bass.ds(n, pieces)], d["M0_w"][bass.ds(n, pieces)].rearrange("a p n -> p a n"))\
                .then_inc(s_experts, 16)

        def later_pool(e):
            for a in atts:
                if a is not a_self0:
                    fill_dma(e, a)
            for dst, src in later:
                e.dma_start(dst, src).then_inc(s_later, 16)
            parts_in_dma(e)
            if "M0" in layers:
                e.wait_ge(m["zeroed"], 1)
                e.dma_start(scr_xn.rearrange("(t p) d -> p t d", p=P), zero[:].unsqueeze(1).to_broadcast([P, MT, D]))\
                    .then_inc(s_zero, 16)

        @block.sync
        def _(e):
            tokens = d["x"].rearrange("(t p) d -> p t d", p=P)
            e.dma_start(xs[:, 0:QT], tokens[:, 0:QT]).then_inc(s_x0, 16)
            e.dma_start(xs[:, QT:NT], tokens[:, QT:NT]).then_inc(s_x, 16)
            for dst, src in loads:
                e.dma_start(dst, src).then_inc(s_w, 16)
            e.wait_ge(s_fill, 1)
            if a_self0 in atts:
                fill_dma(e, a_self0)
            if layers[0] != "A0":
                if "M0" in layers:
                    weights_sp(e, 0, W_PIECES)
                parts_out_sp(e)
            program(e, "sp", {"A0": [staging_sp, attention_sp, lambda e, a: parts_out_sp(e)], "X0": [staging_sp, attention_sp],
                              "M0": [lambda e, ln: moe_sp(e)], "A1": [staging_sp, attention_sp], "X1": [], "F1": []})
            e.wait_ge(x_new[-1][0], x_new[-1][1] + (NT if layers[-1] == "F1" else NB))
            e.dma_start(out.rearrange("(t p) d -> p t d", p=P), xs[:]).then_inc(s_out, 16)
            e.wait_ge(s_out, 16)

        @block.gpsimd
        def _(e):
            starts_at_one = [att_sem[n] for n in ATT_FREE] + [s_xnT, s_xnT_sb, s_xnT_used, m["logits"], m["y_out"]]
            starts_at_one += m["stored"] + [x for (x, _), n in zip(x_new, layers) if n not in of_att]
            starts_at_one += [c[n] for n in "q_out masked probsT_out logits probsT recip out probs".split()]
            starts_at_one += [f["xT_out"], f["silu"]]
            for free in starts_at_one:
                e.sem_inc(free, FREE)
            e.memset(mhalf[:], -0.5)
            e.memset(ones_row[:], 1.0)
            e.memset(onesb[:], 1.0)
            e.memset(onesf[:], 1.0)
            for z in range(2):
                i = e.memset(fill[:, z], float(z))
            i.then_inc(s_fill, 1)
            e.memset(zero[:], 0.0).then_inc(m["zeroed"], 1)
            e.iota(iota_e[:], pattern=[[1, NE]], base=0, channel_multiplier=0, allow_small_or_imprecise_dtypes=True)
            e.iota(iota_t[:], pattern=[[1, MT]], base=0, channel_multiplier=0, allow_small_or_imprecise_dtypes=True)
            e.memset(ident[:], 1.0).then_inc(s_const, 1)
            e.wait_ge(s_const, 1)
            e.affine_select(out=ident[:], in_=ident[:], compare_op=ALU.is_equal, fill=0.0, base=0,
                            pattern=[[-1, P]], channel_multiplier=1)
            e.affine_select(out=before[:], in_=onesb[:], compare_op=ALU.is_gt, fill=0.0, base=0,
                            pattern=[[1, P]], channel_multiplier=-1)
            e.memset(mask_qk[:], 0.0)
            e.memset(mask_kq[:], 0.0).then_inc(s_const, 1)
            e.wait_ge(s_const, 2)
            e.affine_select(out=mask_qk[:], in_=mask_qk[:], compare_op=ALU.is_ge, fill=MASKED, base=0,
                            pattern=[[-1, P]], channel_multiplier=1)
            e.affine_select(out=mask_kq[:], in_=mask_kq[:], compare_op=ALU.is_ge, fill=MASKED, base=0,
                            pattern=[[1, P]], channel_multiplier=-1)
            e.tensor_copy(identb[:], ident[:]).then_inc(s_const, 1)
            if layers[0] != "A0":
                later_pool(e)
                parts_pool(e)
            program(e, "pool", {"A0": [staging_pool, attention_pool, lambda e, a: parts_pool(e)], "X0": [staging_pool, attention_pool],
                                "M0": [moe_pool], "A1": [staging_pool, attention_pool],
                                "X1": [norms_pool], "F1": [norms_pool]})

        @block.tensor
        def _(e):
            e.wait_ge(s_const, 3)
            program(e, "pe", {"A0": [staging_pe, attention_pe], "X0": [staging_pe, attention_pe], "M0": [moe_pe],
                              "A1": [staging_pe, attention_pe], "X1": [cross_pe], "F1": [ffn_pe]})

        @block.vector
        def _(e):
            e.memset(stk[:], 0.0).then_inc(s_clear, 1)
            e.wait_ge(s_const, 3)
            program(e, "dve", {"A0": [staging_dve, attention_dve], "X0": [staging_dve, attention_dve],
                               "M0": [moe_dve], "A1": [staging_dve, attention_dve], "X1": [cross_dve],
                               "F1": [ffn_dve]})

        @block.scalar
        def _(e):
            program(e, "act", {"A0": [staging_act, attention_act], "X0": [staging_act, attention_act],
                               "M0": [moe_act], "A1": [staging_act, attention_act], "X1": [cross_act],
                               "F1": [ffn_act]})


def lay_out(i):
    t = lambda v: np.ascontiguousarray(np.asarray(v).T)
    col = lambda v: np.asarray(v).reshape(P, 1)
    row = lambda v: np.asarray(v).reshape(1, -1)
    o = {"x": np.asarray(i["x"]).reshape(NT * P, D), "ctxT": t(np.asarray(i["ctx_1024"]).reshape(NB * SC, D)),
         "xmask": np.asarray(i["mask_1xSxS2_ff0"])[0]}
    for name, src in (("A0", "L0_attn_"), ("A1", "L1_attn_")):
        o |= {f"{name}_w{k}": t(i[f"{src}w{k}"]) for k in "qkvo"}
        o |= {f"{name}_b{k}": (col if k in "qk" else row)(i[f"{src}b{k}"]) for k in "qkvo"}
    o |= {f"X0_w{k}": np.asarray(i[f"L0_xattn_W{k}"]) for k in "qkvo"}
    o |= {f"X0_b{k}": (col if k in "qk" else row)(i[f"L0_xattn_b{k}"]) for k in "qkvo"}
    pair = np.arange(D) ^ 1
    for k in "qk":
        o[f"A0_w{k}_swapped"] = np.ascontiguousarray(o[f"A0_w{k}"][:, pair])
        o[f"A0_b{k}_swapped"] = np.ascontiguousarray(o[f"A0_b{k}"][pair])
    f32 = np.float32
    rate = np.exp((f32(2.0) * np.arange(HD // 2, dtype=f32) / f32(HD) * f32(math.log(10000.0))).astype(f32))
    theta = (np.arange(S, dtype=f32)[None, :] / rate[:, None]).astype(f32).astype(np.float64)
    which = (np.arange(D) % HD) // 2
    sign = np.where(np.arange(D) % 2 == 0, -1.0, 1.0)[:, None]
    o["cos_sin"] = np.stack([np.cos(theta)[which], sign * np.sin(theta)[which]], axis=1).astype(f32)
    o |= {"M0_gate_w": i["L0_ffn_gate_w"], "M0_gate_b": row(i["L0_ffn_gate_b"]), "M0_b1": row(i["L0_ffn_b1"]), "M0_b2": row(i["L0_ffn_b2"])}
    w2 = np.asarray(i["L0_ffn_w2"]).reshape(NE // 2, 2, FC, P, D).transpose(0, 3, 1, 2, 4).reshape(NE // 2, P, 2 * FF)
    o["M0_w"] = np.concatenate([np.asarray(i["L0_ffn_w1"]), w2])
    o |= {f"X1_w{k}": i[f"L1_xattn_kernel_{k}"] for k in "qkv"}
    o |= {f"X1_b{k}": (col if k in "qk" else row)(i[f"L1_xattn_bias_{k}"]) for k in "qkv"}
    o |= {"F1_w1": t(i["L1_ffn_w1"]), "F1_taps": np.ascontiguousarray(np.asarray(i["L1_ffn_conv_w"])[:, 0, :].T),
          "F1_cb": row(i["L1_ffn_conv_b"]), "F1_w2": t(i["L1_ffn_w2"])}
    return {k: np.ascontiguousarray(v) for k, v in o.items()}


def kernel(**inputs):
    import concourse.bacc as bacc
    from concourse.bass_utils import run_bass_kernel_spmd

    nc = bacc.Bacc("TRN2", target_bir_lowering=False, num_devices=1)
    arrays = {f"in_{k}": v for k, v in lay_out(inputs).items()}
    d = {k[3:]: nc.dram_tensor(k, v.shape, mybir.dt.from_np(v.dtype), kind="ExternalInput").ap() for k, v in arrays.items()}
    out = nc.dram_tensor("out", (NT * P, D), F32, kind="ExternalOutput").ap()
    build(nc, d, out)
    r = run_bass_kernel_spmd(nc, [arrays], core_ids=[0])
    return r.results[0]["out"].reshape(NB, S, D)
```
